# Optimizing a Trainium2 kernel written in Bass

```python
import numpy as np
import jax
import jax.numpy as jnp

def _softmax(x, axis=-1):
    return jax.nn.softmax(x, axis=axis)

def _gelu(x):
    return jax.nn.gelu(x, approximate=True)

def _silu(x):
    return jax.nn.silu(x)

def _sigmoid(x):
    return jax.nn.sigmoid(x)

def _layernorm(x, axis=-1, eps=1e-05):
    m = jnp.mean(x, axis=axis, keepdims=True)
    v = jnp.var(x, axis=axis, keepdims=True)
    return (x - m) / jnp.sqrt(v + eps)

def _scatter_add(tgt, idx, src, axis=0):
    return tgt.at[idx].add(src)

def _segment_sum(src, seg, n):
    return jax.ops.segment_sum(src, seg, n)
kernel_name = 'mk_seq_postln_d2_jaxref_r2_80e941'

def setup_inputs(seed: int=0):
    np.random.seed(seed)
    _w = jnp.asarray

    def _L0_attn_setup():
        import jax, jax.numpy as jnp
        import numpy as np
        B, S, DM, H, DH = (2, 1024, 512, 16, 64)
        HID = H * DH

        def _xavier(key, shape):
            fan_out, fan_in = shape
            lim = float(np.sqrt(6.0 / (fan_in + fan_out)))
            return jax.random.uniform(key, shape, jnp.float32, -lim, lim)

        def _gla_scan(q, k, v, g):
            qt = jnp.moveaxis(q, 1, 0)
            kt = jnp.moveaxis(k, 1, 0)
            vt = jnp.moveaxis(v, 1, 0)
            gt = jnp.moveaxis(g, 1, 0)

            def step(s, inp):
                qi, ki, vi, gi = inp
                s = jnp.exp(gi)[:, :, None, None] * s + ki[..., :, None] * vi[..., None, :]
                o = jnp.einsum('bhk,bhkv->bhv', qi, s)
                return (s, o)
            s0 = jnp.zeros(q.shape[0:1] + q.shape[2:] + q.shape[-1:], q.dtype)
            _, o = jax.lax.scan(step, s0, (qt, kt, vt, gt))
            return jnp.moveaxis(o, 0, 1)
        key = jax.random.key(seed)
        ks = jax.random.split(key, 8)
        return {'x': jax.random.normal(ks[0], (B, S, DM), jnp.float32), 'Wq': _xavier(ks[1], (HID, DM)), 'Wk': _xavier(ks[2], (HID, DM)), 'Wv': _xavier(ks[3], (HID, DM)), 'Wo': _xavier(ks[4], (DM, HID)), 'Wg': _xavier(ks[5], (HID, DM)), 'Wog': _xavier(ks[6], (HID, DM)), 'Wd': _xavier(ks[7], (H, DM)), 'bd': jnp.full((H,), -2.0, jnp.float32), 'norm_w': jnp.ones((HID,), jnp.float32)}
    _L0_attn_in = _L0_attn_setup()

    def _L0_ffn_setup():
        import jax, jax.numpy as jnp
        import numpy as np
        LN_EPS = 0.001
        EPS = 1e-05
        QB = 128.0

        def ste_round(x):
            return x + jax.lax.stop_gradient(jnp.round(x) - x)
        key = jax.random.key(seed)
        k1, k2 = jax.random.split(key)
        x = jax.random.normal(k1, (4, 4096, 512), dtype=jnp.float32)
        weight = jax.random.normal(k2, (512, 512), dtype=jnp.float32) * 0.02
        ln_gamma = jnp.ones((512,), dtype=jnp.float32)
        ln_beta = jnp.zeros((512,), dtype=jnp.float32)
        return {'x': x, 'weight': weight, 'ln_gamma': ln_gamma, 'ln_beta': ln_beta}
    _L0_ffn_in = _L0_ffn_setup()

    def _L1_attn_setup():
        import jax, jax.numpy as jnp
        import numpy as np
        _A = np.array([[1, 1, 1, 0, 1, 1, 1, 0, 0, 0, 1, 1], [1, 1, 0, 1, 1, 1, 0, 0, 0, 1, 1, 0], [1, 0, 1, 1, 1, 0, 0, 0, 1, 1, 0, 1], [0, 1, 1, 1, 0, 0, 0, 1, 1, 0, 1, 1], [0, 0, 0, 0, 1, 1, 1, 1, 1, 1, 1, 1], [1, 1, 1, 1, 0, 0, 0, 0, 0, 0, 0, 0], [0, 0, 0, 0, 1, 1, 1, 1, 0, 0, 0, 0], [1, 1, 0, 0, 1, 1, 0, 0, 1, 1, 0, 0], [1, 0, 1, 0, 1, 0, 1, 0, 1, 0, 1, 0], [0, 1, 0, 1, 0, 1, 0, 1, 0, 1, 0, 1], [1, 0, 0, 1, 1, 0, 0, 1, 1, 0, 0, 1], [0, 1, 1, 0, 0, 1, 1, 0, 0, 1, 1, 0]], dtype=np.float32)
        _H = jnp.asarray(np.concatenate([_A.T, np.eye(12, dtype=np.float32)], axis=1))

        def _fractal_dimension(x):
            s = x.reshape(-1)
            sn = (s - s.min()) / (s.max() - s.min() + 1e-10)
            counts = []
            for sc in (2, 4, 8, 16, 32):
                blk = sn[:sc * sc]
                counts.append(jnp.maximum(jnp.sum(blk > blk.mean()).astype(jnp.float32), 1.0))
            lx = jnp.log(jnp.array([2.0, 4.0, 8.0, 16.0, 32.0], dtype=jnp.float32))
            ly = jnp.log(jnp.stack(counts))
            n = jnp.float32(5.0)
            num = n * jnp.sum(lx * ly) - jnp.sum(lx) * jnp.sum(ly)
            den = n * jnp.sum(lx * lx) - jnp.sum(lx) ** 2
            return jnp.clip(-num / den, 1.0, 2.0)

        def _wave_filter(D, d):
            k = jnp.fft.fftfreq(d).astype(jnp.float32)
            ka = jnp.abs(k) + 1e-08
            omega = 1.0 + 0.2 * D
            a = 1.0 + 0.5 * D
            b = 0.1 * D
            real = jnp.sin(omega * D + a * ka)
            phase = omega * D - ka + b * ka ** 2
            return real * jnp.exp(1j * phase)

        def _golay_correct(bits):
            syn = (bits @ _H.T > 0.5).astype(jnp.float32)
            w = syn.sum(-1)
            _, idx = jax.lax.top_k(syn, 3)
            take = (jnp.arange(3)[None, :] < jnp.minimum(w, 3.0)[:, None]).astype(jnp.float32)
            pattern = (jax.nn.one_hot(idx, 24, dtype=jnp.float32) * take[..., None]).sum(axis=1)
            do_fix = ((w > 0) & (w <= 3))[:, None]
            return jnp.where(do_fix, jnp.mod(bits + pattern, 2.0), bits)
        key = jax.random.key(seed)
        k1, k2, k3 = jax.random.split(key, 3)
        B, S, E = (8, 1024, 512)
        x = jax.random.normal(k1, (B, S, E), dtype=jnp.float32)
        W_el = jax.random.normal(k2, (E, 24), dtype=jnp.float32) * 0.02
        b_el = jnp.zeros((24,), dtype=jnp.float32)
        W_le = jax.random.normal(k3, (24, E), dtype=jnp.float32) * 0.02
        b_le = jnp.zeros((E,), dtype=jnp.float32)
        return {'x': x, 'W_el': W_el, 'b_el': b_el, 'W_le': W_le, 'b_le': b_le}
    _L1_attn_in = _L1_attn_setup()

    def _L1_ffn_setup():
        import jax, jax.numpy as jnp
        import numpy as np
        LN_EPS = 0.001
        EPS = 1e-05
        QB = 128.0

        def ste_round(x):
            return x + jax.lax.stop_gradient(jnp.round(x) - x)
        key = jax.random.key(seed)
        k1, k2 = jax.random.split(key)
        x = jax.random.normal(k1, (4, 4096, 512), dtype=jnp.float32)
        weight = jax.random.normal(k2, (512, 512), dtype=jnp.float32) * 0.02
        ln_gamma = jnp.ones((512,), dtype=jnp.float32)
        ln_beta = jnp.zeros((512,), dtype=jnp.float32)
        return {'x': x, 'weight': weight, 'ln_gamma': ln_gamma, 'ln_beta': ln_beta}
    _L1_ffn_in = _L1_ffn_setup()
    _d = {'L0_attn_x': _L0_attn_in['x'], 'L0_attn_Wq': _L0_attn_in['Wq'], 'L0_attn_Wk': _L0_attn_in['Wk'], 'L0_attn_Wv': _L0_attn_in['Wv'], 'L0_attn_Wo': _L0_attn_in['Wo'], 'L0_attn_Wg': _L0_attn_in['Wg'], 'L0_attn_Wog': _L0_attn_in['Wog'], 'L0_attn_Wd': _L0_attn_in['Wd'], 'L0_attn_bd': _L0_attn_in['bd'], 'L0_attn_norm_w': _L0_attn_in['norm_w'], 'L0_ffn_weight': _L0_ffn_in['weight'], 'L0_ffn_ln_gamma': _L0_ffn_in['ln_gamma'], 'L0_ffn_ln_beta': _L0_ffn_in['ln_beta'], 'L1_attn_W_el': _L1_attn_in['W_el'], 'L1_attn_b_el': _L1_attn_in['b_el'], 'L1_attn_W_le': _L1_attn_in['W_le'], 'L1_attn_b_le': _L1_attn_in['b_le'], 'L1_ffn_weight': _L1_ffn_in['weight'], 'L1_ffn_ln_gamma': _L1_ffn_in['ln_gamma'], 'L1_ffn_ln_beta': _L1_ffn_in['ln_beta']}
    _x0 = _d['L0_attn_x']
    _d['L0_attn_x'] = jax.random.normal(jax.random.fold_in(jax.random.key(seed), 1), (4, 2048, 512), dtype=_x0.dtype)
    del _x0
    return _d

def reference(L0_attn_x, L0_attn_Wq, L0_attn_Wk, L0_attn_Wv, L0_attn_Wo, L0_attn_Wg, L0_attn_Wog, L0_attn_Wd, L0_attn_bd, L0_attn_norm_w, L0_ffn_weight, L0_ffn_ln_gamma, L0_ffn_ln_beta, L1_attn_W_el, L1_attn_b_el, L1_attn_W_le, L1_attn_b_le, L1_ffn_weight, L1_ffn_ln_gamma, L1_ffn_ln_beta):

    def _L0_attn_ref(x, Wq, Wk, Wv, Wo, Wg, Wog, Wd, bd, norm_w):
        import jax, jax.numpy as jnp
        import numpy as np
        B, S, DM, H, DH = (2, 1024, 512, 16, 64)
        HID = H * DH

        def _xavier(key, shape):
            fan_out, fan_in = shape
            lim = float(np.sqrt(6.0 / (fan_in + fan_out)))
            return jax.random.uniform(key, shape, jnp.float32, -lim, lim)

        def _gla_scan(q, k, v, g):
            qt = jnp.moveaxis(q, 1, 0)
            kt = jnp.moveaxis(k, 1, 0)
            vt = jnp.moveaxis(v, 1, 0)
            gt = jnp.moveaxis(g, 1, 0)

            def step(s, inp):
                qi, ki, vi, gi = inp
                s = jnp.exp(gi)[:, :, None, None] * s + ki[..., :, None] * vi[..., None, :]
                o = jnp.einsum('bhk,bhkv->bhv', qi, s)
                return (s, o)
            s0 = jnp.zeros(q.shape[0:1] + q.shape[2:] + q.shape[-1:], q.dtype)
            _, o = jax.lax.scan(step, s0, (qt, kt, vt, gt))
            return jnp.moveaxis(o, 0, 1)
        b, s, _ = x.shape
        q = (x @ Wq.T).reshape(b, s, H, DH)
        k = (x @ Wk.T).reshape(b, s, H, DH)
        v = (x @ Wv.T).reshape(b, s, H, DH)
        log_decay = -jax.nn.softplus(x @ Wd.T + bd)
        gate = jax.nn.sigmoid((x @ Wg.T).reshape(b, s, H, DH))
        k_gated = k * gate
        out = _gla_scan(q, k_gated, v, log_decay)
        out = out.reshape(b, s, HID)
        eps = jnp.finfo(out.dtype).eps
        out = out * jax.lax.rsqrt(jnp.mean(out * out, -1, keepdims=True) + eps) * norm_w
        out = out * jax.nn.sigmoid(x @ Wog.T)
        return out @ Wo.T

    def _L0_ffn_ref(x, weight, ln_gamma, ln_beta):
        import jax, jax.numpy as jnp
        import numpy as np
        LN_EPS = 0.001
        EPS = 1e-05
        QB = 128.0

        def ste_round(x):
            return x + jax.lax.stop_gradient(jnp.round(x) - x)
        mu = jnp.mean(x, axis=-1, keepdims=True)
        var = jnp.var(x, axis=-1, keepdims=True)
        xn = (x - mu) * jax.lax.rsqrt(var + LN_EPS) * ln_gamma + ln_beta
        beta = jnp.mean(jnp.abs(weight))
        w_q = jnp.clip(ste_round(weight / (beta + EPS)), -1.0, 1.0)
        gamma = jnp.max(jnp.abs(xn))
        xq = jnp.clip(xn * QB / gamma, -QB + EPS, QB - EPS)
        y = jnp.einsum('bsd,du->bsu', xq, w_q)
        return y * (gamma * beta / QB)

    def _L1_attn_ref(x, W_el, b_el, W_le, b_le):
        import jax, jax.numpy as jnp
        import numpy as np
        _A = np.array([[1, 1, 1, 0, 1, 1, 1, 0, 0, 0, 1, 1], [1, 1, 0, 1, 1, 1, 0, 0, 0, 1, 1, 0], [1, 0, 1, 1, 1, 0, 0, 0, 1, 1, 0, 1], [0, 1, 1, 1, 0, 0, 0, 1, 1, 0, 1, 1], [0, 0, 0, 0, 1, 1, 1, 1, 1, 1, 1, 1], [1, 1, 1, 1, 0, 0, 0, 0, 0, 0, 0, 0], [0, 0, 0, 0, 1, 1, 1, 1, 0, 0, 0, 0], [1, 1, 0, 0, 1, 1, 0, 0, 1, 1, 0, 0], [1, 0, 1, 0, 1, 0, 1, 0, 1, 0, 1, 0], [0, 1, 0, 1, 0, 1, 0, 1, 0, 1, 0, 1], [1, 0, 0, 1, 1, 0, 0, 1, 1, 0, 0, 1], [0, 1, 1, 0, 0, 1, 1, 0, 0, 1, 1, 0]], dtype=np.float32)
        _H = jnp.asarray(np.concatenate([_A.T, np.eye(12, dtype=np.float32)], axis=1))

        def _fractal_dimension(x):
            s = x.reshape(-1)
            sn = (s - s.min()) / (s.max() - s.min() + 1e-10)
            counts = []
            for sc in (2, 4, 8, 16, 32):
                blk = sn[:sc * sc]
                counts.append(jnp.maximum(jnp.sum(blk > blk.mean()).astype(jnp.float32), 1.0))
            lx = jnp.log(jnp.array([2.0, 4.0, 8.0, 16.0, 32.0], dtype=jnp.float32))
            ly = jnp.log(jnp.stack(counts))
            n = jnp.float32(5.0)
            num = n * jnp.sum(lx * ly) - jnp.sum(lx) * jnp.sum(ly)
            den = n * jnp.sum(lx * lx) - jnp.sum(lx) ** 2
            return jnp.clip(-num / den, 1.0, 2.0)

        def _wave_filter(D, d):
            k = jnp.fft.fftfreq(d).astype(jnp.float32)
            ka = jnp.abs(k) + 1e-08
            omega = 1.0 + 0.2 * D
            a = 1.0 + 0.5 * D
            b = 0.1 * D
            real = jnp.sin(omega * D + a * ka)
            phase = omega * D - ka + b * ka ** 2
            return real * jnp.exp(1j * phase)

        def _golay_correct(bits):
            syn = (bits @ _H.T > 0.5).astype(jnp.float32)
            w = syn.sum(-1)
            _, idx = jax.lax.top_k(syn, 3)
            take = (jnp.arange(3)[None, :] < jnp.minimum(w, 3.0)[:, None]).astype(jnp.float32)
            pattern = (jax.nn.one_hot(idx, 24, dtype=jnp.float32) * take[..., None]).sum(axis=1)
            do_fix = ((w > 0) & (w <= 3))[:, None]
            return jnp.where(do_fix, jnp.mod(bits + pattern, 2.0), bits)
        B, S, E = x.shape
        D = _fractal_dimension(x)
        filt = _wave_filter(D, E)
        x1 = jnp.fft.ifft(jnp.fft.fft(x, axis=-1) * filt, axis=-1).real.astype(x.dtype)
        lat = x1 @ W_el + b_el
        bits = (jax.nn.sigmoid(lat) > 0.5).astype(jnp.float32).reshape(B * S, 24)
        corrected = _golay_correct(bits).reshape(B, S, 24)
        return x1 + corrected @ W_le + b_le

    def _L1_ffn_ref(x, weight, ln_gamma, ln_beta):
        import jax, jax.numpy as jnp
        import numpy as np
        LN_EPS = 0.001
        EPS = 1e-05
        QB = 128.0

        def ste_round(x):
            return x + jax.lax.stop_gradient(jnp.round(x) - x)
        mu = jnp.mean(x, axis=-1, keepdims=True)
        var = jnp.var(x, axis=-1, keepdims=True)
        xn = (x - mu) * jax.lax.rsqrt(var + LN_EPS) * ln_gamma + ln_beta
        beta = jnp.mean(jnp.abs(weight))
        w_q = jnp.clip(ste_round(weight / (beta + EPS)), -1.0, 1.0)
        gamma = jnp.max(jnp.abs(xn))
        xq = jnp.clip(xn * QB / gamma, -QB + EPS, QB - EPS)
        y = jnp.einsum('bsd,du->bsu', xq, w_q)
        return y * (gamma * beta / QB)
    x = L0_attn_x
    x = _layernorm(x + _L0_attn_ref(x, L0_attn_Wq, L0_attn_Wk, L0_attn_Wv, L0_attn_Wo, L0_attn_Wg, L0_attn_Wog, L0_attn_Wd, L0_attn_bd, L0_attn_norm_w), axis=-1)
    x = _layernorm(x + _L0_ffn_ref(x, L0_ffn_weight, L0_ffn_ln_gamma, L0_ffn_ln_beta), axis=-1)
    x = _layernorm(x + _L1_attn_ref(x, L1_attn_W_el, L1_attn_b_el, L1_attn_W_le, L1_attn_b_le), axis=-1)
    x = _layernorm(x + _L1_ffn_ref(x, L1_ffn_weight, L1_ffn_ln_gamma, L1_ffn_ln_beta), axis=-1)
    return x

_drawn_inputs = setup_inputs


def setup_inputs(seed=0):
    import zlib

    import numpy as np

    out = dict(_drawn_inputs(seed))
    spreads = {'L0_attn_bd': (-2.0, 0.2),
     'L0_attn_norm_w': (1.0, 0.2),
     'L0_ffn_ln_gamma': (1.0, 0.2),
     'L0_ffn_ln_beta': (0.0, 0.304),
     'L1_attn_b_el': (0.0, 0.426),
     'L1_attn_b_le': (0.0, 0.1),
     'L1_ffn_ln_gamma': (1.0, 0.2),
     'L1_ffn_ln_beta': (0.0, 0.306)}
    factors = {}
    for name, (base, spread) in spreads.items():
        noise = np.random.default_rng([zlib.crc32(name.encode()), seed]).standard_normal(out[name].shape)
        drawn = base * np.exp(spread * noise) if base else spread * noise
        out[name] = jnp.asarray(drawn.astype(out[name].dtype))
    for name, factor in factors.items():
        out[name] = (out[name] * factor).astype(out[name].dtype)
    return out
```

```python
import numpy as np
import concourse.bass as bass
from concourse import mybir
from contextlib import ExitStack

FP32 = mybir.dt.float32
FP32R = mybir.dt.float32r
ALU = mybir.AluOpType
ACT = mybir.ActivationFunctionType
AX = mybir.AxisListType
REDUCE = bass.bass_isa.ReduceOp

P = 128
BATCH, SEQ, DM = 4, 2048, 512
TOKENS = BATCH * SEQ
HEADS, DH = 16, 64
HID = HEADS * DH
HALVES = 2
HALF = HID // HALVES
HH = HEADS // HALVES
PAIRS = HALF // P
KT = DM // P
ST = 512
CH = P
CHUNKS = ST // CH
ROUNDS = TOKENS // ST
ROUNDS_PER_BATCH = SEQ // ST
TILES = TOKENS // P
LN_EPS = 1e-5
FFN_LN_EPS = 1e-3
RMS_EPS = float(np.finfo(np.float32).eps)
QB, Q_EPS = 128.0, 1e-5
MASKED = -1e30


class Count:

    def __init__(self, sem, per_round, step=1):
        self.sem, self.per_round, self.step = sem, per_round, step

    def credit(self, engine):
        engine.sem_inc(self.sem, self.step * self.per_round)

    def now(self, r, j):
        return (r + 1) * (self.step * self.per_round) + self.step * j

    def before(self, r, j):
        return r * (self.step * self.per_round) + self.step * j


def split_fp32r(hi):
    return hi.bitcast(FP32)


def attention_half(nc, half, xT, wT, woT, wdT, bd, norm_w, g_dram, y_dram, ssq, late):
    hid0 = half * HALF
    with ExitStack() as ctx:
        def sb(name, shape, dt=FP32):
            return ctx.enter_context(nc.sbuf_tensor(f"{name}_{half}", shape, dt))

        def sem(name):
            return nc.alloc_semaphore(f"{name}_{half}")

        def counted(name, per_round, step=1):
            return Count(sem(name), per_round, step)

        W = {}
        for name in ("v", "g", "k", "q", "og"):
            W[name] = (sb(f"w_{name}_hi", [P, KT, HALF], FP32R), sb(f"w_{name}_lo", [P, KT, HALF], FP32R))
        wo_hi, wo_lo = sb("wo_hi", [P, PAIRS, DM], FP32R), sb("wo_lo", [P, PAIRS, DM], FP32R)
        if half == 0:
            wd_raw = sb("wd_raw", [P, KT, HEADS])
            wd_hi, wd_lo = sb("wd_hi", [P, KT, P], FP32R), sb("wd_lo", [P, KT, P], FP32R)
            bd_sb = sb("bd", [HEADS, 1])
        norm_sb = sb("norm", [P, PAIRS])
        x_raw = sb("x_raw", [P, KT, ST])
        x_hi, x_lo = sb("x_hi", [P, KT, ST], FP32R), sb("x_lo", [P, KT, ST], FP32R)
        qT, kT = sb("qT", [P, 2, ST]), sb("kT", [P, 2, ST])
        gate = sb("gate", [P, ST])
        osig = sb("osig", [P, 2, ST])
        q_dec = sb("q_dec", [P, ST])
        k_dec = sb("k_dec", [P, CHUNKS, 2, DH])
        G = sb("G", [P, 2, 2, CHUNKS, CH])
        E = sb("E", [P, 2, CHUNKS, CH])
        A = sb("A", [P, 2, CHUNKS, CH])
        v = sb("v", [P, CHUNKS, HALF])
        o_hi, o_lo = sb("o_hi", [P, PAIRS, ST], FP32R), sb("o_lo", [P, PAIRS, ST], FP32R)
        o_gated = sb("o_gated", [P, ST])
        sq = sb("sq", [P, ST])
        sq_sum = sb("sq_sum", [P, ST])
        S_in = sb("S_in", [P, PAIRS, P])
        S = sb("S", [P, 2, CHUNKS, P])
        gT = sb("gT", [HEADS, ST])
        gs = sb("gs", [P, CHUNKS, HH])
        mask = sb("mask", [P, CH])
        ident = sb("ident", [P, P])
        ones = sb("ones", [P, CH])
        z_l = A[0:HEADS, 0, :, :].rearrange("p c t -> p (c t)")
        z_m = A[0:HEADS, 1, :, :].rearrange("p c t -> p (c t)")

        pj = [ctx.enter_context(nc.psum_tensor(f"pj{b}_{half}", [P, 512], FP32)) for b in range(4)]
        sc = [ctx.enter_context(nc.psum_tensor(f"sc{b}_{half}", [P, CHUNKS, CH], FP32)) for b in range(2)]
        kk = ctx.enter_context(nc.psum_tensor(f"kk_{half}", [P, CHUNKS, P], FP32))
        ot = ctx.enter_context(nc.psum_tensor(f"ot_{half}", [P, ST], FP32))

        const_made = sem("const_made")
        small_loaded = sem("small_loaded")
        w_loaded = [sem("w_loaded0"), sem("w_loaded1")]
        pad_made, wd_hi_made, wd_lo_made = sem("pad_made"), sem("wd_hi_made"), sem("wd_lo_made")
        w_hi_made, w_lo_made = sem("w_hi_made"), sem("w_lo_made")
        z_done, v_done = counted("z_done", 1), counted("v_done", CHUNKS)
        g_done, k_done = counted("g_done", PAIRS), counted("k_done", PAIRS)
        q_done, og_done = counted("q_done", PAIRS), counted("og_done", PAIRS)
        gst_done, kt_done = counted("gst_done", 1), counted("kt_done", PAIRS)
        sc_done, kv_done = counted("sc_done", 2 * PAIRS), counted("kv_done", PAIRS)
        o_done, y_done = counted("o_done", PAIRS), counted("y_done", CHUNKS)
        ssq_done = counted("ssq_done", 1)
        xh_ready, zabs_ready = counted("xh_ready", 1), counted("zabs_ready", 1)
        zexp_ready, zlog_ready = counted("zexp_ready", 1), counted("zlog_ready", 1)
        v_ready, gate_ready = counted("v_ready", CHUNKS), counted("gate_ready", PAIRS)
        q_ready, osig_ready = counted("q_ready", PAIRS), counted("osig_ready", PAIRS)
        e_ready, d_ready = counted("e_ready", PAIRS), counted("d_ready", PAIRS)
        sq_ready, oh_ready = counted("sq_ready", PAIRS), counted("oh_ready", PAIRS)
        xl_ready, zmax_ready = counted("xl_ready", 1), counted("zmax_ready", 1)
        glog_ready, gT_ready = counted("glog_ready", 1), counted("gT_ready", 1)
        k_ready, gs_ready = counted("k_ready", PAIRS), counted("gs_ready", 1)
        kdec_ready, a_ready = counted("kdec_ready", PAIRS), counted("a_ready", 2 * PAIRS)
        s_step, s_ready = counted("s_step", 2 * PAIRS * CHUNKS), counted("s_ready", PAIRS)
        og_ready, ol_ready = counted("og_ready", PAIRS), counted("ol_ready", PAIRS)
        carried, ssq_read = counted("carried", PAIRS), counted("ssq_read", 1)
        zeroed = sem("zeroed")
        y_free = counted("y_free", CHUNKS)
        dsub_ready, dmask_ready = counted("dsub_ready", PAIRS), counted("dmask_ready", PAIRS)
        qd_ready, sqsum_ready = counted("qd_ready", PAIRS), counted("sqsum_ready", PAIRS)
        x_loaded = counted("x_loaded", 1, 16)
        gT_stored, gT_loaded = counted("gT_stored", 1, 16), counted("gT_loaded", 1, 16)
        G_loaded = [counted(f"G_loaded{s}", PAIRS // 2, 16) for s in range(2)]
        y_stored = [counted(f"y_stored{s}", CHUNKS // 2, 16) for s in range(2)]

        if half == 0:
            y_out = sb("y_out", [P, 2, DM])
        else:
            x_tok = sb("x_tok", [P, CHUNKS, DM])
            y_first = [sq, o_gated]
            stats, mv = sb("stats", [P, CHUNKS, 6]), sb("mv", [P, CHUNKS, 2])
            rms = sb("rms", [P, CHUNKS])
            var1, rstd, var2 = (sb(n, [P, CHUNKS]) for n in ("var1", "rstd", "var2"))
            g_bc, b_bc = sb("g_bc", [P, DM]), sb("b_bc", [P, DM])
            top_now = sb("top_now", [P, CHUNKS])
            minus_half = sb("minus_half", [P, CHUNKS])
            xt_loaded = [counted(f"xt_loaded{c}", 1, 16) for c in range(CHUNKS)]
            yf_loaded = [counted(f"yf_loaded{s}", CHUNKS // 2, 16) for s in range(2)]
            x1_stored = counted("x1_stored", CHUNKS, 16)
            rms_ready, t2_ready = counted("rms_ready", 2), counted("t2_ready", CHUNKS)
            st_ready, mv_ready = counted("st_ready", CHUNKS), counted("mv_ready", CHUNKS)
            var_ready = counted("var_ready", 5)
            x1_ready = counted("x1_ready", CHUNKS)
            xn_step = counted("xn_step", 3 * CHUNKS + 1)
            sq_rstd = counted("sq_rstd", 1)
            loaded_gb = sem("loaded_gb")

        stage = [v[:, :, :], x_raw[:, :, :]]

        block = ctx.enter_context(nc.Block())

        @block.sync
        def _(sp):
            for c in (x_loaded, gT_stored, gT_loaded, *G_loaded, *y_stored):
                c.credit(sp)
            if half == 0:
                sp.dma_start(wd_raw[:, :, :], wdT.rearrange("(k p) h -> p k h", p=P)).then_inc(small_loaded, 16)
                sp.dma_start(bd_sb[:, :], bd.rearrange("(h a) -> h a", a=1)).then_inc(small_loaded, 16)
            sp.dma_start(norm_sb[:, :], norm_w[:, half * PAIRS:(half + 1) * PAIRS]).then_inc(small_loaded, 16)
            if half == 1:
                for c in (*xt_loaded, *yf_loaded, x1_stored):
                    c.credit(sp)
                sp.dma_start(g_bc[:, :], late["ln_gamma"].rearrange("(a n) -> a n", a=1).broadcast_to((P, DM))).then_inc(loaded_gb, 16)
                sp.dma_start(b_bc[:, :], late["ln_beta"].rearrange("(a n) -> a n", a=1).broadcast_to((P, DM))).then_inc(loaded_gb, 16)
            for i, name in enumerate(("v", "g", "k", "q", "og")):
                if i >= 2:
                    sp.wait_ge(w_lo_made, i - 1)
                sp.dma_start(stage[i % 2], wT[name][:, hid0:hid0 + HALF].rearrange("(k p) n -> p k n", p=P)).then_inc(w_loaded[i % 2], 16)
            sp.wait_ge(w_lo_made, 4)
            sp.dma_start(stage[1], woT[hid0:hid0 + HALF, :].rearrange("(b p) n -> p b n", p=P)).then_inc(w_loaded[1], 16)
            sp.wait_ge(w_lo_made, 8)
            sp.dma_start(x_raw[:, :, :], xT[:, 0:ST].rearrange("(k p) t -> p k t", p=P)).then_inc(x_loaded.sem, 16)
            with sp.Fori(0, ROUNDS) as n:
                start = sp.snap(((n + 1) % ROUNDS) * ST)
                sp.wait_ge(xl_ready.sem, xl_ready.now(n, 1))
                sp.dma_start(x_raw[:, :, :], xT[:, bass.ds(start, ST)].rearrange("(k p) t -> p k t", p=P)).then_inc(x_loaded.sem, 16)
                if half == 0:
                    sp.wait_ge(gT_ready.sem, gT_ready.now(n, 1))
                    sp.dma_start(g_dram[:, bass.ds(n * ST, ST)], gT[:, :]).then_inc(gT_stored.sem, 16)
                    sp.wait_ge(gT_stored.sem, gT_stored.now(n, 1))
                else:
                    sp.wait_ge(gst_done.sem, gst_done.before(n, 1))
                    sp.dma_start(gT[0:HH, :], g_dram[HH:HEADS, bass.ds(n * ST, ST)]).then_inc(gT_loaded.sem, 16)
                for p in range(PAIRS):
                    start = sp.snap(n * ST)
                    sp.wait_ge(kdec_ready.sem, kdec_ready.before(n, p + 3) if p < 2 else kdec_ready.now(n, p - 1))
                    sp.nop(nofuse=True)
                    sp.wait_ge(a_ready.sem, a_ready.before(n, 2 * (p + 3)) if p < 2 else a_ready.now(n, 2 * (p - 1)))
                    src = g_dram[half * HH + 2 * p:half * HH + 2 * p + 2, bass.ds(start, ST)].unsqueeze(0).broadcast_to((P, 2, ST))
                    sp.dma_start(G[:, p % 2, :, :, :].rearrange("p h c t -> p h (c t)"), src).then_inc(G_loaded[p % 2].sem, 16)
                if half == 0:
                    for c in range(CHUNKS):
                        sp.wait_ge(y_free.sem, y_free.now(n, c + 1))
                        sp.dma_start(y_dram[bass.ds(n * ST + c * P, P), :], y_out[:, c % 2, :]).then_inc(y_stored[c % 2].sem, 16)
                else:
                    for c in range(CHUNKS):
                        sp.wait_ge(x1_stored.sem, x1_stored.before(n, CHUNKS))
                        sp.wait_ge(xn_step.sem, xn_step.before(n, 3 * CHUNKS + 1))
                        sp.dma_start(x_tok[:, c, :], late["x"][bass.ds(n * ST + c * P, P), :]).then_inc(xt_loaded[c].sem, 16)
                    for c in range(CHUNKS):
                        if c == 0:
                            sp.wait_ge(sqsum_ready.sem, sqsum_ready.now(n, PAIRS))
                        elif c == 1:
                            sp.wait_ge(ol_ready.sem, ol_ready.now(n, PAIRS))
                        else:
                            sp.wait_ge(t2_ready.sem, t2_ready.now(n, c - 1))
                        sp.dma_start(y_first[c % 2][:, :], y_dram[bass.ds(n * ST + c * P, P), :]).then_inc(yf_loaded[c % 2].sem, 16)
                    for c in range(CHUNKS):
                        sp.wait_ge(x1_ready.sem, x1_ready.now(n, c + 1))
                        sp.dma_start(late["x1"][bass.ds(n * ST + c * P, P), :], x_tok[:, c, :]).then_inc(x1_stored.sem, 16)
            for c, per in ([(y, CHUNKS // 2) for y in y_stored] if half == 0 else [(x1_stored, CHUNKS)]):
                sp.wait_ge(c.sem, c.now(ROUNDS - 1, per))
            sp.wait_ge(x_loaded.sem, x_loaded.now(ROUNDS, 1))

        @block.gpsimd
        def _(pool):
            for c in (dsub_ready, dmask_ready, qd_ready, sqsum_ready):
                c.credit(pool)
            pool.memset(mask[:, :], 0.0).then_inc(const_made, 1)
            pool.memset(ident[:, :], 0.0).then_inc(const_made, 1)
            pool.memset(ones[:, :], 1.0).then_inc(const_made, 1)
            pool.wait_ge(const_made, 3)
            pool.affine_select(out=mask[:, :], in_=mask[:, :], compare_op=ALU.is_ge, fill=MASKED, base=0,
                               pattern=[[1, CH]], channel_multiplier=-1).then_inc(const_made, 1)
            pool.affine_select(out=ident[:, :], in_=ident[:, :], compare_op=ALU.not_equal, fill=1.0, base=0,
                               pattern=[[-1, P]], channel_multiplier=1).then_inc(const_made, 1)
            if half == 1:
                var_ready.credit(pool)
                pool.memset(minus_half[:, :], -0.5).then_inc(const_made, 1)
            pool.wait_ge(const_made, 5 + (half == 1))

            def decay(n, p):
                Gp = G[:, p % 2, :, :, :]
                pool.wait_ge(e_ready.sem, e_ready.now(n, p + 1))
                if p == 0:
                    pool.wait_ge(gs_ready.sem, gs_ready.now(n, 1))
                pool.tensor_tensor(Gp, Gp, gs[:, :, 2 * p:2 * p + 2].rearrange("p c h -> p h c").unsqueeze(3).broadcast_to((P, 2, CHUNKS, CH)),
                                   ALU.subtract).then_inc(dsub_ready.sem, 1)
                pool.wait_ge(dsub_ready.sem, dsub_ready.now(n, p + 1))
                G8 = Gp.rearrange("p h c t -> p (h c) t")
                pool.tensor_tensor(G8, G8, mask[:, :].unsqueeze(1).broadcast_to((P, 2 * CHUNKS, CH)), ALU.add).then_inc(dmask_ready.sem, 1)

            def query_decay(n, p):
                pool.wait_ge(q_ready.sem, q_ready.now(n, p + 1))
                pool.wait_ge(o_done.sem, o_done.now(n, p) if p else o_done.before(n, PAIRS))
                pool.tensor_tensor(q_dec[:, :], qT[:, p % 2, :], E[:, p % 2, :, :].rearrange("p c t -> p (c t)"),
                                   ALU.mult).then_inc(qd_ready.sem, 1)

            def squares(n, p):
                pool.wait_ge(sq_ready.sem, sq_ready.now(n, p + 1))
                if p == 0:
                    pool.wait_ge(ssq_done.sem, ssq_done.before(n, 1))
                    pool.nop(nofuse=True)
                    pool.tensor_scalar(sq_sum[:, :], sq[:, :], 1.0, 0.0, ALU.mult, ALU.add).then_inc(sqsum_ready.sem, 1)
                else:
                    pool.wait_ge(sqsum_ready.sem, sqsum_ready.now(n, p))
                    pool.tensor_tensor(sq_sum[:, :], sq_sum[:, :], sq[:, :], ALU.add).then_inc(sqsum_ready.sem, 1)

            with pool.Fori(0, ROUNDS) as n:
                decay(n, 0)
                query_decay(n, 0)
                decay(n, 1)
                query_decay(n, 1)
                squares(n, 0)
                decay(n, 2)
                query_decay(n, 2)
                squares(n, 1)
                decay(n, 3)
                query_decay(n, 3)
                squares(n, 2)
                squares(n, 3)
                if half == 1:
                    pool.wait_ge(rms_ready.sem, rms_ready.now(n, 1))
                    pool.tensor_tensor(rms[:, :], rms[:, :], minus_half[:, :], ALU.pow).then_inc(var_ready.sem, 1)
                    pool.wait_ge(mv_ready.sem, mv_ready.now(n, CHUNKS))
                    pool.nop(nofuse=True)
                    pool.tensor_scalar(var1[:, :], mv[:, :, 1], 1.0, LN_EPS, ALU.mult, ALU.add).then_inc(var_ready.sem, 1)
                    pool.wait_ge(var_ready.sem, var_ready.now(n, 2))
                    pool.tensor_tensor(rstd[:, :], var1[:, :], minus_half[:, :], ALU.pow).then_inc(var_ready.sem, 1)
                    pool.wait_ge(rms_ready.sem, rms_ready.now(n, 2))
                    pool.nop(nofuse=True)
                    pool.tensor_scalar(var2[:, :], var2[:, :], 1.0, FFN_LN_EPS, ALU.mult, ALU.add).then_inc(var_ready.sem, 1)
                    pool.wait_ge(var_ready.sem, var_ready.now(n, 4))
                    pool.tensor_tensor(late["rho"][:, bass.ds(n * CHUNKS, CHUNKS)], var2[:, :], minus_half[:, :], ALU.pow).then_inc(var_ready.sem, 1)

        @block.scalar
        def _(act):
            for c in (xh_ready, zabs_ready, zexp_ready, zlog_ready, v_ready, gate_ready, q_ready, osig_ready,
                      e_ready, d_ready, sq_ready, oh_ready):
                c.credit(act)
            if half == 0:
                y_free.credit(act)
            if half == 0:
                act.wait_ge(small_loaded, 48)
                act.wait_ge(pad_made, 2)
                act.activation(wd_hi[:, :, 0:HEADS], wd_raw[:, :, :], ACT.Copy).then_inc(wd_hi_made, 1)
            for i, name in enumerate(("v", "g", "k", "q", "og")):
                act.wait_ge(w_loaded[i % 2], 16 * (i // 2 + 1))
                act.activation(W[name][0][:, :, :], stage[i % 2], ACT.Copy).then_inc(w_hi_made, 1)
            act.wait_ge(w_lo_made, 7)
            act.activation(wo_hi[:, :, :], stage[1], ACT.Copy).then_inc(w_hi_made, 1)

            def split_x(n_of_x):
                act.wait_ge(x_loaded.sem, x_loaded.now(n_of_x, 1))
                act.activation(x_hi[:, :, :], x_raw[:, :, :], ACT.Copy).then_inc(xh_ready.sem, 1)

            split_x(0)

            def log_decay(n):
                act.wait_ge(zmax_ready.sem, zmax_ready.now(n, 1))
                act.activation(z_l, ot[0:HEADS, :], ACT.Abs, bias=bd_sb[:, :]).then_inc(zabs_ready.sem, 1)
                act.wait_ge(zabs_ready.sem, zabs_ready.now(n, 1))
                act.activation(z_l, z_l, ACT.Exp, scale=-1.0).then_inc(zexp_ready.sem, 1)
                act.wait_ge(zexp_ready.sem, zexp_ready.now(n, 1))
                act.activation(z_l, z_l, ACT.Ln, bias=1.0).then_inc(zlog_ready.sem, 1)

            def values(n):
                for c in range(CHUNKS):
                    act.wait_ge(v_done.sem, v_done.now(n, c + 1))
                    act.activation(v[:, c, :], pj[c][:, :], ACT.Copy).then_inc(v_ready.sem, 1)

            def gate_tanh(n, p):
                act.wait_ge(g_done.sem, g_done.now(n, p + 1))
                act.wait_ge(k_ready.sem, k_ready.now(n, p) if p else k_ready.before(n, PAIRS))
                act.activation(gate[:, :], pj[0][:, :], ACT.Tanh, scale=0.5).then_inc(gate_ready.sem, 1)

            def queries(n, p):
                act.wait_ge(q_done.sem, q_done.now(n, p + 1))
                act.wait_ge(sc_done.sem, sc_done.now(n, 2 * (p - 1)) if p >= 2 else sc_done.before(n, 2 * (p + 3)))
                act.wait_ge(qd_ready.sem, qd_ready.now(n, p - 1) if p >= 2 else qd_ready.before(n, p + 3))
                act.activation(qT[:, p % 2, :], pj[2][:, :], ACT.Copy, scale=0.5).then_inc(q_ready.sem, 1)

            def out_gate(n, p):
                act.wait_ge(og_done.sem, og_done.now(n, p + 1))
                act.wait_ge(og_ready.sem, og_ready.now(n, p - 1) if p >= 2 else og_ready.before(n, p + 3))
                act.activation(osig[:, p % 2, :], pj[3][:, :], ACT.Tanh, scale=0.5).then_inc(osig_ready.sem, 1)

            def chunk_decay(n, p):
                act.wait_ge(G_loaded[p % 2].sem, G_loaded[p % 2].now(n, p // 2 + 1))
                act.wait_ge(qd_ready.sem, qd_ready.now(n, p - 1) if p >= 2 else qd_ready.before(n, p + 3))
                act.wait_ge(s_ready.sem, s_ready.now(n, p - 1) if p >= 2 else s_ready.before(n, p + 3))
                act.activation(E[0:DH, p % 2, :, :], G[0:DH, p % 2, 0, :, :], ACT.Exp)
                act.activation(E[DH:P, p % 2, :, :], G[DH:P, p % 2, 1, :, :], ACT.Exp).then_inc(e_ready.sem, 1)

            def token_decay(n, p):
                act.wait_ge(dmask_ready.sem, dmask_ready.now(n, p + 1))
                act.activation(G[:, p % 2, :, :, :], G[:, p % 2, :, :, :], ACT.Exp).then_inc(d_ready.sem, 1)

            def square(n, p):
                act.wait_ge(o_done.sem, o_done.now(n, p + 1))
                if half == 1 and p == 0:
                    act.wait_ge(xn_step.sem, xn_step.before(n, 3 * CHUNKS + 1))
                act.wait_ge(sqsum_ready.sem, sqsum_ready.now(n, p) if p else sqsum_ready.before(n, PAIRS))
                act.activation(sq[:, :], ot[:, :], ACT.Square).then_inc(sq_ready.sem, 1)

            def out_hi(n, p):
                act.wait_ge(og_ready.sem, og_ready.now(n, p + 1))
                act.wait_ge(y_done.sem, y_done.before(n, CHUNKS))
                act.activation(o_hi[:, p, :], o_gated[:, :], ACT.Copy).then_inc(oh_ready.sem, 1)

            with act.Fori(0, ROUNDS) as n:
                if half == 0:
                    log_decay(n)
                values(n)
                gate_tanh(n, 0); queries(n, 0); out_gate(n, 0)
                chunk_decay(n, 0)
                gate_tanh(n, 1); queries(n, 1); out_gate(n, 1)
                chunk_decay(n, 1)
                token_decay(n, 0)
                gate_tanh(n, 2); queries(n, 2)
                token_decay(n, 1)
                square(n, 0); out_hi(n, 0)
                out_gate(n, 2)
                chunk_decay(n, 2)
                gate_tanh(n, 3); queries(n, 3)
                square(n, 1); out_hi(n, 1)
                chunk_decay(n, 3)
                token_decay(n, 2)
                out_gate(n, 3)
                split_x(n + 1)
                token_decay(n, 3)
                square(n, 2); out_hi(n, 2)
                square(n, 3); out_hi(n, 3)
                if half == 0:
                    for c in range(CHUNKS):
                        act.wait_ge(y_done.sem, y_done.now(n, c + 1))
                        s = y_stored[c % 2]
                        act.wait_ge(s.sem, s.now(n, 1) if c >= 2 else s.before(n, 2))
                        act.activation(y_out[:, c % 2, :], pj[c][:, :], ACT.Copy).then_inc(y_free.sem, 1)

        @block.vector
        def _(dve):
            for c in (xl_ready, zmax_ready, glog_ready, gT_ready, k_ready, gs_ready, kdec_ready, a_ready, s_step,
                      s_ready, og_ready, ol_ready, carried, ssq_read):
                c.credit(dve)
            if half == 1:
                for c in (y_free, rms_ready, t2_ready, st_ready, mv_ready, x1_ready, xn_step, sq_rstd):
                    c.credit(dve)
            if half == 0:
                dve.memset(wd_hi[:, :, :].bitcast(FP32), 0.0).then_inc(pad_made, 1)
                dve.memset(wd_lo[:, :, :].bitcast(FP32), 0.0).then_inc(pad_made, 1)
            dve.memset(S[:, :, :, :], 0.0)
            dve.memset(S_in[:, :, :], 0.0)
            if half == 0:
                dve.wait_ge(wd_hi_made, 1)
                dve.tensor_tensor(wd_lo[:, :, 0:HEADS], wd_raw[:, :, :], split_fp32r(wd_hi[:, :, 0:HEADS]), ALU.subtract).then_inc(wd_lo_made, 1)
            for i, name in enumerate(("v", "g", "k", "q", "og")):
                dve.wait_ge(w_hi_made, i + 1)
                dve.tensor_tensor(W[name][1][:, :, :], stage[i % 2], split_fp32r(W[name][0][:, :, :]), ALU.subtract).then_inc(w_lo_made, 1)
            if half == 1:
                dve.memset(late["top"][:, :], 0.0)
            dve.wait_ge(small_loaded, 48 if half == 0 else 16)
            dve.wait_ge(w_loaded[1], 16 * 3)
            dve.tensor_tensor(stage[1], stage[1], norm_sb[:, :].unsqueeze(2).broadcast_to((P, PAIRS, DM)), ALU.mult).then_inc(w_lo_made, 2)
            dve.wait_ge(w_hi_made, 6)
            dve.tensor_tensor(wo_lo[:, :, :], stage[1], split_fp32r(wo_hi[:, :, :]), ALU.subtract).then_inc(w_lo_made, 1)

            def split_x(n_of_x):
                dve.wait_ge(xh_ready.sem, xh_ready.now(n_of_x, 1))
                dve.tensor_tensor(x_lo[:, :, :], x_raw[:, :, :], split_fp32r(x_hi[:, :, :]), ALU.subtract).then_inc(xl_ready.sem, 1)

            split_x(0)

            def log_decay(n):
                dve.wait_ge(z_done.sem, z_done.now(n, 1))
                dve.tensor_scalar(z_m, ot[0:HEADS, :], bd_sb[:, :], 0.0, ALU.add, ALU.max).then_inc(zmax_ready.sem, 1)
                dve.wait_ge(zlog_ready.sem, zlog_ready.now(n, 1))
                dve.wait_ge(zmax_ready.sem, zmax_ready.now(n, 1))
                dve.scalar_tensor_tensor(z_m, z_m, -1.0, z_l, ALU.mult, ALU.subtract).then_inc(glog_ready.sem, 1)
                dve.wait_ge(glog_ready.sem, glog_ready.now(n, 1))
                dve.wait_ge(gT_stored.sem, gT_stored.before(n, 1))
                for c in range(CHUNKS):
                    scan = dve.tensor_tensor_scan(gT[:, c * CH:(c + 1) * CH], ones[0:HEADS, :], z_m[:, c * CH:(c + 1) * CH], 0.0,
                                                  ALU.mult, ALU.add)
                scan.then_inc(gT_ready.sem, 1)

            def keys(n, p):
                dve.wait_ge(k_done.sem, k_done.now(n, p + 1))
                dve.wait_ge(gate_ready.sem, gate_ready.now(n, p + 1))
                dve.wait_ge(sc_done.sem, sc_done.now(n, 2 * (p - 1)) if p >= 2 else sc_done.before(n, 2 * (p + 3)))
                dve.scalar_tensor_tensor(kT[:, p % 2, :], gate[:, :], 1.0, pj[1][:, :], ALU.add, ALU.mult).then_inc(k_ready.sem, 1)

            def token_logs(n):
                dve.wait_ge(gst_done.sem, gst_done.now(n, 1))
                dve.wait_ge(dsub_ready.sem, dsub_ready.before(n, PAIRS))
                dve.tensor_copy(gs[:, :, :].rearrange("p c h -> p (c h)"), ot[:, 0:CHUNKS * HH]).then_inc(gs_ready.sem, 1)

            def key_decay(n, p):
                dve.wait_ge(kt_done.sem, kt_done.now(n, p + 1))
                dve.wait_ge(d_ready.sem, d_ready.now(n, p + 1))
                dve.wait_ge(kv_done.sem, kv_done.now(n, p) if p else kv_done.before(n, PAIRS))
                to_end = G[:, p % 2, :, :, CH - 1].rearrange("p h c -> p c h").unsqueeze(3).broadcast_to((P, CHUNKS, 2, DH))
                dve.tensor_tensor(k_dec[:, :, :, :], kk[:, :, :].rearrange("p c (h d) -> p c h d", h=2), to_end,
                                  ALU.mult).then_inc(kdec_ready.sem, 1)

            def scores(n, p):
                for j in range(2):
                    dve.wait_ge(sc_done.sem, sc_done.now(n, 2 * p + j + 1))
                    if j == 0:
                        dve.wait_ge(o_done.sem, o_done.now(n, p) if p else o_done.before(n, PAIRS))
                    dve.tensor_tensor(A[:, j, :, :], sc[j][:, :, :], G[:, p % 2, j, :, :], ALU.mult).then_inc(a_ready.sem, 1)

            def states(n, p, batch):
                dve.wait_ge(kv_done.sem, kv_done.now(n, p + 1))
                dve.wait_ge(zeroed, batch + 1)
                dve.wait_ge(carried.sem, carried.before(n, p + 1))
                dve.wait_ge(carried.sem, carried.now(n, p - 1) if p >= 2 else carried.before(n, p + 3))
                for c in range(CHUNKS):
                    if c:
                        dve.wait_ge(s_step.sem, s_step.now(n, 2 * (p * CHUNKS + c)))
                    for h in range(2):
                        rows = slice(h * DH, (h + 1) * DH)
                        before = S_in[rows, p, h * DH:(h + 1) * DH] if c == 0 else S[rows, p % 2, c - 1, h * DH:(h + 1) * DH]
                        step = dve.scalar_tensor_tensor(S[rows, p % 2, c, h * DH:(h + 1) * DH], before, E[rows, p % 2, c, CH - 1:CH],
                                                        kk[rows, c, h * DH:(h + 1) * DH], ALU.mult, ALU.add)
                        step.then_inc(s_step.sem, 1)
                dve.wait_ge(s_step.sem, s_step.now(n, 2 * (p + 1) * CHUNKS))
                dve.sem_inc(s_ready.sem, 1)

            def out_gated(n, p):
                dve.wait_ge(sq_ready.sem, sq_ready.now(n, p + 1))
                dve.wait_ge(osig_ready.sem, osig_ready.now(n, p + 1))
                dve.wait_ge(ol_ready.sem, ol_ready.now(n, p) if p else ol_ready.before(n, PAIRS))
                dve.scalar_tensor_tensor(o_gated[:, :], osig[:, p % 2, :], 1.0, ot[:, :], ALU.add, ALU.mult).then_inc(og_ready.sem, 1)
                dve.tensor_copy(S_in[:, p, :], S[:, p % 2, CHUNKS - 1, :]).then_inc(carried.sem, 1)

            def out_lo(n, p):
                dve.wait_ge(oh_ready.sem, oh_ready.now(n, p + 1))
                dve.tensor_tensor(o_lo[:, p, :], o_gated[:, :], split_fp32r(o_hi[:, p, :]), ALU.subtract).then_inc(ol_ready.sem, 1)

            def finish(n):
                dve.tensor_tensor(rms[:, :], ssq[:, bass.ds(n * CHUNKS, CHUNKS)], kk[:, 0, 0:CHUNKS], ALU.add).then_inc(ssq_read.sem, 1)
                dve.wait_ge(ssq_read.sem, ssq_read.now(n, 1))
                dve.tensor_scalar(rms[:, :], rms[:, :], 4.0 / HID, 4.0 * RMS_EPS, ALU.mult, ALU.add).then_inc(rms_ready.sem, 1)
                for c in range(CHUNKS):
                    dve.wait_ge(y_done.sem, y_done.now(n, c + 1))
                    dve.wait_ge(yf_loaded[c % 2].sem, yf_loaded[c % 2].now(n, c // 2 + 1))
                    dve.tensor_tensor(y_first[c % 2][:, :], pj[c][:, :], y_first[c % 2][:, :], ALU.add).then_inc(y_free.sem, 1)
                    dve.wait_ge(y_free.sem, y_free.now(n, c + 1))
                    dve.wait_ge(var_ready.sem, var_ready.now(n, 1))
                    dve.wait_ge(xt_loaded[c].sem, xt_loaded[c].now(n, 1))
                    dve.scalar_tensor_tensor(x_tok[:, c, :], y_first[c % 2][:, :], rms[:, c:c + 1], x_tok[:, c, :], ALU.mult, ALU.add).then_inc(t2_ready.sem, 1)
                    dve.wait_ge(t2_ready.sem, t2_ready.now(n, c + 1))
                    dve.nop(nofuse=True)
                    dve.bn_stats(stats[:, c, :], x_tok[:, c, :]).then_inc(st_ready.sem, 1)
                    dve.wait_ge(st_ready.sem, st_ready.now(n, c + 1))
                    dve.nop(nofuse=True)
                    dve.bn_aggr(mv[:, c, :], stats[:, c, :]).then_inc(mv_ready.sem, 1)
                dve.wait_ge(var_ready.sem, var_ready.now(n, 3))
                for c in range(CHUNKS):
                    dve.tensor_scalar(x_tok[:, c, :], x_tok[:, c, :], mv[:, c, 0:1], rstd[:, c:c + 1], ALU.subtract, ALU.mult).then_inc(x1_ready.sem, 1)
                dve.tensor_tensor(var2[:, :], mv[:, :, 1], rstd[:, :], ALU.mult).then_inc(sq_rstd.sem, 1)
                dve.wait_ge(sq_rstd.sem, sq_rstd.now(n, 1))
                dve.tensor_tensor(var2[:, :], var2[:, :], rstd[:, :], ALU.mult).then_inc(rms_ready.sem, 1)
                dve.wait_ge(loaded_gb, 32)
                dve.wait_ge(var_ready.sem, var_ready.now(n, 5))
                for c in range(CHUNKS):
                    xn = y_first[c % 2][:, :]
                    if c >= 2:
                        dve.wait_ge(xn_step.sem, xn_step.now(n, 3 * (c - 1)))
                    dve.wait_ge(x1_ready.sem, x1_ready.now(n, c + 1))
                    dve.scalar_tensor_tensor(xn, x_tok[:, c, :], late["rho"][:, bass.ds(n * CHUNKS + c, 1)], g_bc[:, :], ALU.mult, ALU.mult).then_inc(xn_step.sem, 1)
                    dve.wait_ge(xn_step.sem, xn_step.now(n, 3 * c + 1))
                    dve.tensor_tensor(xn, xn, b_bc[:, :], ALU.add).then_inc(xn_step.sem, 1)
                    dve.wait_ge(xn_step.sem, xn_step.now(n, 3 * c + 2))
                    dve.tensor_reduce(top_now[:, c:c + 1], xn, AX.X, ALU.max, apply_absolute_value=True).then_inc(xn_step.sem, 1)
                dve.wait_ge(xn_step.sem, xn_step.now(n, 3 * CHUNKS))
                dve.tensor_tensor(late["top"][:, :], late["top"][:, :], top_now[:, :], ALU.max).then_inc(xn_step.sem, 1)

            with dve.Fori(0, BATCH) as batch:
                dve.wait_ge(carried.sem, carried.before(batch * ROUNDS_PER_BATCH, PAIRS))
                dve.memset(S_in[:, :, :], 0.0).then_inc(zeroed, 1)
                with dve.Fori(0, ROUNDS_PER_BATCH) as r:
                    n = batch * ROUNDS_PER_BATCH + r
                    if half == 0:
                        log_decay(n)
                    keys(n, 0)
                    token_logs(n)
                    keys(n, 1)
                    key_decay(n, 0); scores(n, 0)
                    keys(n, 2)
                    states(n, 0, batch)
                    out_gated(n, 0); out_lo(n, 0)
                    key_decay(n, 1); scores(n, 1)
                    keys(n, 3)
                    states(n, 1, batch)
                    out_gated(n, 1); out_lo(n, 1)
                    key_decay(n, 2); scores(n, 2)
                    split_x(n + 1)
                    states(n, 2, batch)
                    out_gated(n, 2); out_lo(n, 2)
                    key_decay(n, 3); scores(n, 3)
                    states(n, 3, batch)
                    out_gated(n, 3); out_lo(n, 3)
                    dve.wait_ge(ssq_done.sem, ssq_done.now(n, 1))
                    if half == 0:
                        dve.tensor_copy(ssq[:, bass.ds(n * CHUNKS, CHUNKS)], kk[:, 0, 0:CHUNKS]).then_inc(ssq_read.sem, 1)
                    else:
                        finish(n)


        @block.tensor
        def _(pe):
            for c in (z_done, v_done, g_done, k_done, q_done, og_done, gst_done, kt_done, sc_done, kv_done, o_done,
                      y_done, ssq_done):
                c.credit(pe)
            pe.wait_ge(const_made, 5)

            def projection(out, w, cols):
                hi, lo = w
                for t, (a, b) in enumerate(((hi, x_hi), (lo, x_hi), (hi, x_lo))):
                    for k in range(KT):
                        last = pe.matmul(out, a[:, k, cols], b[:, k, :], start=(t + k == 0), stop=(t == 2 and k == KT - 1))
                return last

            def decay_logits(n):
                pe.wait_ge(wd_lo_made, 1)
                pe.wait_ge(sq_ready.sem, sq_ready.before(n, PAIRS))
                pe.wait_ge(og_ready.sem, og_ready.before(n, PAIRS))
                for t, (a, b) in enumerate(((wd_hi, x_hi), (wd_lo, x_hi), (wd_hi, x_lo))):
                    for k in range(KT):
                        last = pe.matmul(ot[:, :], a[:, k, :], b[:, k, :],
                                         start=(t + k == 0), stop=(t == 2 and k == KT - 1))
                last.then_inc(z_done.sem, 1)

            def values(n):
                pe.wait_ge(w_lo_made, 1)
                for c in range(CHUNKS):
                    pe.wait_ge(y_free.sem, y_free.before(n, c + 1))
                    for t, (a, b) in enumerate(((x_hi, 0), (x_hi, 1), (x_lo, 0))):
                        for k in range(KT):
                            last = pe.matmul(pj[c][:, :], a[:, k, c * P:(c + 1) * P], W["v"][b][:, k, :],
                                             start=(t + k == 0), stop=(t == 2 and k == KT - 1))
                    last.then_inc(v_done.sem, 1)

            bank_of = {"g": 0, "k": 1, "q": 2, "og": 3}
            done_of = {"g": g_done, "k": k_done, "q": q_done, "og": og_done}
            read_of = {"g": gate_ready, "k": k_ready, "q": q_ready, "og": osig_ready}

            def project(n, name, p):
                b = bank_of[name]
                pe.wait_ge(w_lo_made, ("v", "g", "k", "q", "og").index(name) + 1)
                if p == 0:
                    pe.wait_ge(v_ready.sem, v_ready.now(n, b + 1))
                else:
                    pe.wait_ge(read_of[name].sem, read_of[name].now(n, p))
                projection(pj[b][:, :], W[name], slice(p * P, (p + 1) * P)).then_inc(done_of[name].sem, 1)

            def token_logs(n):
                if half == 0:
                    pe.wait_ge(gT_ready.sem, gT_ready.now(n, 1))
                    pe.wait_ge(zabs_ready.sem, zabs_ready.now(n, 1))
                else:
                    pe.wait_ge(gT_loaded.sem, gT_loaded.now(n, 1))
                    pe.wait_ge(sq_ready.sem, sq_ready.before(n, PAIRS))
                    pe.wait_ge(og_ready.sem, og_ready.before(n, PAIRS))
                pe.nop(nofuse=True)
                for c in range(CHUNKS):
                    last = pe.transpose(ot[:, c * HH:(c + 1) * HH], gT[0:HH, c * CH:(c + 1) * CH], ident[0:HH, 0:HH])
                last.then_inc(gst_done.sem, 1)

            def scores(n, p):
                pe.wait_ge(k_ready.sem, k_ready.now(n, p + 1))
                pe.wait_ge(s_ready.sem, s_ready.now(n, p) if p else s_ready.before(n, PAIRS))
                if p == 0:
                    pe.wait_ge(ssq_read.sem, ssq_read.before(n, 1))
                for c in range(CHUNKS):
                    last = pe.transpose(kk[:, c, :], kT[:, p % 2, c * CH:(c + 1) * CH], ident[:, :])
                last.then_inc(kt_done.sem, 1)
                pe.wait_ge(q_ready.sem, q_ready.now(n, p + 1))
                pe.wait_ge(a_ready.sem, a_ready.now(n, 2 * p) if p else a_ready.before(n, 2 * PAIRS))
                for c in range(CHUNKS):
                    cols = slice(c * CH, (c + 1) * CH)
                    for h in range(2):
                        rows = slice(h * DH, (h + 1) * DH)
                        last = pe.matmul(sc[h][:, c, :], kT[rows, p % 2, cols], qT[rows, p % 2, cols], start=True, stop=True)
                        if c == CHUNKS - 1:
                            last.then_inc(sc_done.sem, 1)

            def outputs(n, p):
                pe.wait_ge(kdec_ready.sem, kdec_ready.now(n, p + 1))
                pe.wait_ge(v_ready.sem, v_ready.now(n, CHUNKS))
                for c in range(CHUNKS):
                    last = pe.matmul(kk[:, c, :], k_dec[:, c, :, :].rearrange("p h d -> p (h d)"), v[:, c, p * P:(p + 1) * P],
                                     start=True, stop=True)
                last.then_inc(kv_done.sem, 1)
                if p == 0:
                    pe.wait_ge(gs_ready.sem, gs_ready.now(n, 1))
                else:
                    pe.wait_ge(sq_ready.sem, sq_ready.now(n, p))
                    pe.wait_ge(og_ready.sem, og_ready.now(n, p))
                pe.wait_ge(a_ready.sem, a_ready.now(n, 2 * p + 2))
                for c in range(CHUNKS):
                    for h in range(2):
                        cols = slice(p * P + h * DH, p * P + (h + 1) * DH)
                        pe.matmul(ot[h * DH:(h + 1) * DH, c * CH:(c + 1) * CH], v[:, c, cols], A[:, h, c, :],
                                  start=(c == 0), stop=False, skip_group_check=True)
                pe.wait_ge(s_ready.sem, s_ready.now(n, p + 1))
                pe.wait_ge(qd_ready.sem, qd_ready.now(n, p + 1))
                for c in range(CHUNKS):
                    state = S_in[:, p, :] if c == 0 else S[:, p % 2, c - 1, :]
                    last = pe.matmul(ot[:, c * CH:(c + 1) * CH], state, q_dec[:, c * CH:(c + 1) * CH], start=False,
                                     stop=(c == CHUNKS - 1), skip_group_check=True)
                last.then_inc(o_done.sem, 1)

            def project_out(n, p):
                pe.wait_ge(w_lo_made, 8)
                pe.wait_ge(oh_ready.sem, oh_ready.now(n, p + 1))
                pe.wait_ge(ol_ready.sem, ol_ready.now(n, p + 1))
                if p == 0:
                    for name in ("g", "k", "q", "og"):
                        pe.wait_ge(read_of[name].sem, read_of[name].now(n, PAIRS))
                for c in range(CHUNKS):
                    cols = slice(c * P, (c + 1) * P)
                    for t, (a, b) in enumerate(((o_hi, wo_hi), (o_hi, wo_lo), (o_lo, wo_hi))):
                        last = pe.matmul(pj[c][:, :], a[:, p, cols], b[:, p, :], start=(p == 0 and t == 0),
                                         stop=(p == PAIRS - 1 and t == 2))
                    if p == PAIRS - 1:
                        last.then_inc(y_done.sem, 1)

            def sum_squares(n):
                pe.wait_ge(sqsum_ready.sem, sqsum_ready.now(n, PAIRS))
                pe.wait_ge(s_ready.sem, s_ready.now(n, PAIRS))
                for c in range(CHUNKS):
                    last = pe.matmul(kk[:, 0, c:c + 1], sq_sum[:, c * P:(c + 1) * P], ones[:, 0:1], start=(c == 0), stop=True,
                                     skip_group_check=True)
                last.then_inc(ssq_done.sem, 1)

            with pe.Fori(0, ROUNDS) as n:
                pe.wait_ge(xl_ready.sem, xl_ready.now(n, 1))
                if half == 0:
                    decay_logits(n)
                values(n)
                for name in ("g", "k", "q", "og"):
                    project(n, name, 0)
                token_logs(n)
                for name in ("g", "k", "q", "og"):
                    project(n, name, 1)
                scores(n, 0)
                for name in ("g", "k", "q", "og"):
                    project(n, name, 2)
                outputs(n, 0)
                scores(n, 1)
                for name in ("g", "k", "q"):
                    project(n, name, 3)
                outputs(n, 1)
                scores(n, 2)
                project(n, "og", 3)
                project_out(n, 0)
                outputs(n, 2)
                scores(n, 3)
                project_out(n, 1)
                outputs(n, 3)
                project_out(n, 2)
                sum_squares(n)
                project_out(n, 3)


def quantised_product(nc, part, X, rho, top, x1, w, g_col, b_col, extremes, out):
    with ExitStack() as ctx:
        def sb(name, shape, dt=FP32):
            return ctx.enter_context(nc.sbuf_tensor(f"{name}_{part}", shape, dt))

        def sem(name):
            return nc.alloc_semaphore(f"{name}_{part}")

        def counted(name, per_round, step=1):
            return Count(sem(name), per_round, step)

        wq = sb("wq", [P, KT, DM], FP32R)
        xq = sb("xq", [P, KT, ST])
        w_raw = xq
        hi, lo = sb("hi", [P, 2, KT, ST], FP32R), sb("lo", [P, 2, KT, ST], FP32R)
        xs = sb("xs", [P, CHUNKS, DM])
        ident, minus_half = sb("ident", [P, P]), sb("minus_half", [P, CHUNKS])
        gcol, bcol = sb("gcol", [P, KT]), sb("bcol", [P, KT])
        beta, gamma = sb("beta", [P, 1]), sb("gamma", [P, 1])
        part_sum, part_top = sb("part_sum", [P, 1]), sb("part_top", [P, 1])
        b_eps, b_inv, g_inv, scale = (sb(x, [P, 1]) for x in ("b_eps", "b_inv", "g_inv", "scale"))
        low = sb("low", [P, DM])
        stats, mv = sb("stats", [P, CHUNKS, 6]), sb("mv", [P, CHUNKS, 2])
        var1, rstd = sb("var1", [P, CHUNKS]), sb("rstd", [P, CHUNKS])
        ends_now = sb("ends_now", [P, 2])

        tb = [ctx.enter_context(nc.psum_tensor(f"tb{k}_{part}", [P, ST], FP32)) for k in range(KT)]
        yb = [ctx.enter_context(nc.psum_tensor(f"yb{c}_{part}", [P, DM], FP32)) for c in range(CHUNKS)]

        const_made, loaded, w_loaded = sem("const_made"), sem("loaded"), sem("w_loaded")
        sums_made, reduced, setup = sem("sums_made"), sem("reduced"), sem("setup")
        x_loaded = [sem(f"x_loaded{s}") for s in range(2)]
        xs_ready, t_done = counted("xs_ready", CHUNKS), counted("t_done", KT)
        xn_ready, clipped = counted("xn_ready", KT), counted("clipped", KT)
        hi_ready, lo_ready = counted("hi_ready", KT), counted("lo_ready", KT)
        y_done, sum_ready = counted("y_done", CHUNKS), counted("sum_ready", CHUNKS)
        st_ready, mv_ready = counted("st_ready", CHUNKS), counted("mv_ready", CHUNKS)
        var_ready, x_ready = counted("var_ready", 2), counted("x_ready", CHUNKS)
        ends_ready = counted("ends_ready", 3)
        stored = counted("stored", 1, 16)

        block = ctx.enter_context(nc.Block())

        def tiles(n):
            return X[:, bass.ds(n * CHUNKS, CHUNKS), :]

        @block.sync
        def _(sp):
            stored.credit(sp)
            sp.dma_start(w_raw[:, :, :], w.rearrange("(k p) n -> p k n", p=P)).then_inc(w_loaded, 16)
            sp.dma_start(gcol[:, :], g_col).then_inc(loaded, 16)
            sp.dma_start(bcol[:, :], b_col).then_inc(loaded, 16)
            if x1 is not None:
                for n in range(ROUNDS):
                    if n >= 2:
                        sp.wait_ge(x_loaded[n % 2], 16 * (n // 2))
                    sp.dma_start(X[:, n * CHUNKS:(n + 1) * CHUNKS, :],
                                 x1[n * ST:(n + 1) * ST, :].rearrange("(c p) f -> p c f", p=P)).then_inc(x_loaded[n % 2], 16)
                sp.wait_ge(x_loaded[0], 16 * (ROUNDS // 2))
                sp.sem_inc(x_loaded[0], 16)
            if out is not None:
                with sp.Fori(0, ROUNDS) as n:
                    sp.wait_ge(x_ready.sem, x_ready.now(n, CHUNKS))
                    sp.dma_start(out[bass.ds(n * ST, ST), :].rearrange("(c p) f -> p c f", p=P), tiles(n)).then_inc(stored.sem, 16)
                sp.wait_ge(stored.sem, stored.now(ROUNDS - 1, 1))

        @block.gpsimd
        def _(pool):
            clipped.credit(pool)
            var_ready.credit(pool)
            pool.memset(ident[:, :], 0.0).then_inc(const_made, 1)
            pool.memset(minus_half[:, :], -0.5).then_inc(const_made, 1)
            pool.wait_ge(const_made, 2)
            pool.affine_select(out=ident[:, :], in_=ident[:, :], compare_op=ALU.not_equal, fill=1.0, base=0,
                               pattern=[[-1, P]], channel_multiplier=1).then_inc(const_made, 1)
            pool.wait_ge(sums_made, 1)
            pool.partition_all_reduce(gamma[:, :], part_top[:, :], P, REDUCE.max).then_inc(reduced, 1)
            pool.wait_ge(sums_made, 2)
            pool.partition_all_reduce(beta[:, :], part_sum[:, :], P, REDUCE.add).then_inc(reduced, 1)

            def clip(n):
                for k in range(KT):
                    pool.wait_ge(xn_ready.sem, xn_ready.now(n, k + 1))
                    pool.nop(nofuse=True)
                    pool.tensor_scalar(xq[:, k, :], xq[:, k, :], QB - Q_EPS, -QB + Q_EPS, ALU.min, ALU.max).then_inc(clipped.sem, 1)

            clip(0)
            with pool.Fori(0, ROUNDS) as n:
                clip(n + 1)
                pool.wait_ge(mv_ready.sem, mv_ready.now(n, CHUNKS))
                pool.nop(nofuse=True)
                pool.tensor_scalar(var1[:, :], mv[:, :, 1], 1.0, LN_EPS, ALU.mult, ALU.add).then_inc(var_ready.sem, 1)
                pool.wait_ge(var_ready.sem, var_ready.now(n, 1))
                pool.tensor_tensor(rstd[:, :], var1[:, :], minus_half[:, :], ALU.pow).then_inc(var_ready.sem, 1)

        @block.scalar
        def _(act):
            for c in (xs_ready, xn_ready, hi_ready):
                c.credit(act)

            def scale_tokens(n, last):
                tile = act.snap(((n + 1) % ROUNDS) * CHUNKS) if last else 0
                for c in range(CHUNKS):
                    act.wait_ge(t_done.sem, t_done.now(n, KT) if last else t_done.before(0, KT))
                    act.activation(xs[:, c, :], X[:, bass.ds(tile + c, 1), :].rearrange("p a f -> p (a f)") if last else X[:, c, :],
                                   ACT.Copy, scale=rho[:, bass.ds(tile + c, 1)] if last else rho[:, c:c + 1]).then_inc(xs_ready.sem, 1)

            def normalised(n, slot):
                for k in range(KT):
                    act.wait_ge(t_done.sem, t_done.now(n, k + 1))
                    act.wait_ge(lo_ready.sem, lo_ready.before(n, k + 1))
                    act.activation(xq[:, k, :], tb[k][:, :], ACT.Identity, scale=gcol[:, k:k + 1], bias=bcol[:, k:k + 1]).then_inc(xn_ready.sem, 1)
                for k in range(KT):
                    act.wait_ge(clipped.sem, clipped.now(n, k + 1))
                    act.activation(hi[:, slot, k, :], xq[:, k, :], ACT.Copy).then_inc(hi_ready.sem, 1)

            if x1 is not None:
                act.wait_ge(x_loaded[0], 16)
            scale_tokens(0, False)
            act.wait_ge(setup, 7 + 3 * KT)
            normalised(0, 0)
            with act.Fori(0, ROUNDS // 2) as i:
                for s in range(2):
                    n = i * 2 + s
                    if x1 is not None:
                        act.wait_ge(x_loaded[1 - s], (i + 1 + s) * 16)
                    scale_tokens(n, True)
                    act.wait_ge(y_done.sem, y_done.before(n, CHUNKS))
                    normalised(n + 1, 1 - s)

        @block.vector
        def _(dve):
            for c in (lo_ready, sum_ready, st_ready, mv_ready, x_ready, ends_ready):
                c.credit(dve)
            dve.tensor_reduce(part_top[:, :], top[:, :], AX.X, ALU.max).then_inc(sums_made, 1)
            dve.wait_ge(w_loaded, 16)
            dve.tensor_reduce(part_sum[:, :], w_raw[:, :, :].rearrange("p k n -> p (k n)"), AX.X, ALU.add,
                              apply_absolute_value=True).then_inc(sums_made, 1)
            dve.wait_ge(reduced, 2)
            done = 0

            def chained(step):
                nonlocal done
                done += 1
                step.then_inc(setup, 1)
                dve.wait_ge(setup, done)

            chained(dve.tensor_scalar(beta[:, :], beta[:, :], 1.0 / (DM * DM), None, ALU.mult))
            chained(dve.tensor_scalar(b_eps[:, :], beta[:, :], Q_EPS, None, ALU.add))
            chained(dve.reciprocal(b_inv[:, :], b_eps[:, :]))
            chained(dve.reciprocal(g_inv[:, :], gamma[:, :]))
            dve.wait_ge(loaded, 32)
            chained(dve.tensor_scalar(gcol[:, :], gcol[:, :], g_inv[:, :], QB, ALU.mult, ALU.mult))
            chained(dve.tensor_scalar(bcol[:, :], bcol[:, :], g_inv[:, :], QB, ALU.mult, ALU.mult))
            chained(dve.scalar_tensor_tensor(scale[:, :], gamma[:, :], 1.0 / QB, beta[:, :], ALU.mult, ALU.mult))
            for k in range(KT):
                chained(dve.tensor_scalar(w_raw[:, k, :], w_raw[:, k, :], b_inv[:, :], None, ALU.mult))
                chained(dve.tensor_scalar(low[:, :], w_raw[:, k, :], -0.5, None, ALU.is_lt))
                chained(dve.scalar_tensor_tensor(wq[:, k, :], w_raw[:, k, :], 0.5, low[:, :], ALU.is_gt, ALU.subtract))
            if extremes is not None:
                chained(dve.memset(extremes[:, :], -3.0e38))

            def low_parts(n, slot):
                for k in range(KT):
                    dve.wait_ge(hi_ready.sem, hi_ready.now(n, k + 1))
                    dve.tensor_tensor(lo[:, slot, k, :], xq[:, k, :], split_fp32r(hi[:, slot, k, :]), ALU.subtract).then_inc(lo_ready.sem, 1)

            low_parts(0, 0)
            with dve.Fori(0, ROUNDS // 2) as i:
                for s in range(2):
                    n = i * 2 + s
                    low_parts(n + 1, 1 - s)
                    for c in range(CHUNKS):
                        x = X[:, bass.ds(n * CHUNKS + c, 1), :].rearrange("p a f -> p (a f)")
                        dve.wait_ge(y_done.sem, y_done.now(n, c + 1))
                        dve.scalar_tensor_tensor(x, yb[c][:, :], scale[:, :], x, ALU.mult, ALU.add).then_inc(sum_ready.sem, 1)
                        dve.wait_ge(sum_ready.sem, sum_ready.now(n, c + 1))
                        dve.nop(nofuse=True)
                        dve.bn_stats(stats[:, c, :], x).then_inc(st_ready.sem, 1)
                        dve.wait_ge(st_ready.sem, st_ready.now(n, c + 1))
                        dve.nop(nofuse=True)
                        dve.bn_aggr(mv[:, c, :], stats[:, c, :]).then_inc(mv_ready.sem, 1)
                    dve.wait_ge(var_ready.sem, var_ready.now(n, 2))
                    for c in range(CHUNKS):
                        x = X[:, bass.ds(n * CHUNKS + c, 1), :].rearrange("p a f -> p (a f)")
                        dve.tensor_scalar(x, x, mv[:, c, 0:1], rstd[:, c:c + 1], ALU.subtract, ALU.mult).then_inc(x_ready.sem, 1)
                    if extremes is not None:
                        dve.wait_ge(x_ready.sem, x_ready.now(n, CHUNKS))
                        dve.nop(nofuse=True)
                        dve.tensor_reduce(ends_now[:, 0:1], tiles(n), AX.XY, ALU.max).then_inc(ends_ready.sem, 1)
                        dve.tensor_reduce(ends_now[:, 1:2], tiles(n), AX.XY, ALU.min, negate=True).then_inc(ends_ready.sem, 1)
                        dve.wait_ge(ends_ready.sem, ends_ready.now(n, 2))
                        dve.tensor_tensor(extremes[:, :], extremes[:, :], ends_now[:, :], ALU.max).then_inc(ends_ready.sem, 1)

        @block.tensor
        def _(pe):
            t_done.credit(pe)
            y_done.credit(pe)
            pe.wait_ge(const_made, 3)

            def transposes(n):
                pe.wait_ge(xs_ready.sem, xs_ready.now(n, CHUNKS))
                for k in range(KT):
                    pe.wait_ge(xn_ready.sem, xn_ready.before(n, k + 1))
                    for c in range(CHUNKS):
                        last = pe.transpose(tb[k][:, c * P:(c + 1) * P], xs[:, c, k * P:(k + 1) * P], ident[:, :])
                    last.then_inc(t_done.sem, 1)

            transposes(0)
            pe.wait_ge(setup, 7 + 3 * KT)
            with pe.Fori(0, ROUNDS // 2) as i:
                for s in range(2):
                    n = i * 2 + s
                    transposes(n + 1)
                    for c in range(CHUNKS):
                        pe.wait_ge(sum_ready.sem, sum_ready.before(n, c + 1))
                        for k in range(KT):
                            if c == 0:
                                pe.wait_ge(lo_ready.sem, lo_ready.now(n, k + 1))
                            for part_of in (hi, lo):
                                last = pe.matmul(yb[c][:, :], part_of[:, s, k, c * P:(c + 1) * P], wq[:, k, :],
                                                 start=(k == 0 and part_of is hi), stop=(k == KT - 1 and part_of is lo))
                        last.then_inc(y_done.sem, 1)


LATENT, CHECKS = 24, 12
SCALES = (2, 4, 8, 16, 32)
LOG_SCALES = [float(x) for x in np.log(np.array(SCALES, np.float32))]
SUM_LX = float(np.sum(np.array(LOG_SCALES, np.float32)))
DEN = float(np.float32(5.0 * np.sum(np.array(LOG_SCALES) ** 2) - np.sum(LOG_SCALES) ** 2))


def wave_filter(nc, X, extremes, basis, freq, w_el, C, M):
    with ExitStack() as ctx:
        def sb(name, shape, dt=FP32):
            return ctx.enter_context(nc.sbuf_tensor(f"{name}_filter", shape, dt))

        def sem(name):
            return nc.alloc_semaphore(f"{name}_filter")

        n_seq = SCALES[-1] ** 2
        seq, above = sb("seq", [1, n_seq]), sb("above", [1, n_seq])
        ends, span, inv = sb("ends", [P, 2]), sb("span", [P, 1]), sb("inv", [P, 1])
        total, mean, count = (sb(x, [1, len(SCALES)]) for x in ("total", "mean", "count"))
        logs, num, lx = sb("logs", [1, len(SCALES)]), sb("num", [1, 4]), sb("lx", [1, len(SCALES)])
        D = sb("D", [P, 1])
        dim1 = sb("dim1", [1, 1])
        omega, a_par, b_par, omega_d = (sb(x, [P, 1]) for x in ("omega", "a_par", "b_par", "omega_d"))
        ka, arg, phase, f = (sb(x, [P, KT]) for x in ("ka", "arg", "phase", "f"))
        B, Bf, Cf = sb("B", [P, KT, DM]), sb("Bf", [P, KT, DM]), sb("Cf", [P, KT, DM])
        wel = sb("wel", [P, KT, LATENT])
        Mf = sb("Mf", [P, KT, LATENT])
        cb = [ctx.enter_context(nc.psum_tensor(f"cb{m}_filter", [P, DM], FP32)) for m in range(KT)]
        mb = ctx.enter_context(nc.psum_tensor("mb_filter", [P, KT, LATENT], FP32))
        loaded, reduced, step, logged, spread, sined = (sem(x) for x in ("loaded", "reduced", "step", "logged", "spread", "sined"))
        c_done, c_read, m_done, hi_made = sem("c_done"), sem("c_read"), sem("m_done"), sem("hi_made")
        n_step = {}
        block = ctx.enter_context(nc.Block())

        @block.sync
        def _(sp):
            for token in range(n_seq // DM):
                sp.dma_start(seq[0:1, token * DM:(token + 1) * DM], X[token:token + 1, 0, :]).then_inc(loaded, 16)
            sp.dma_start(ka[:, :], freq).then_inc(loaded, 16)
            sp.dma_start(B[:, :, :], basis.rearrange("(k p) n -> p k n", p=P)).then_inc(loaded, 16)
            sp.dma_start(wel[:, :, :], w_el.rearrange("(k p) n -> p k n", p=P)).then_inc(loaded, 16)

        @block.vector
        def _(dve):
            done = 0

            def chained(ins, name=None):
                nonlocal done
                done += 1
                ins.then_inc(step, 1)
                dve.wait_ge(step, done)
                if name:
                    n_step[name] = done

            for j, value in enumerate(LOG_SCALES):
                chained(dve.memset(lx[:, j:j + 1], value))
            for part in M:
                chained(dve.memset(part[:, :, :].bitcast(FP32), 0.0))
            dve.wait_ge(loaded, 80)
            dve.wait_ge(reduced, 1)
            chained(dve.tensor_tensor(span[:, :], ends[:, 0:1], ends[:, 1:2], ALU.add))
            chained(dve.tensor_scalar(span[:, :], span[:, :], 1e-10, None, ALU.add))
            chained(dve.reciprocal(inv[:, :], span[:, :]))
            chained(dve.tensor_scalar(seq[:, :], seq[:, :], ends[0:1, 1:2], inv[0:1, :], ALU.add, ALU.mult))
            for j, size in enumerate(SCALES):
                m = size * size
                chained(dve.tensor_reduce(total[:, j:j + 1], seq[:, 0:m], AX.X, ALU.add))
                chained(dve.tensor_scalar(mean[:, j:j + 1], total[:, j:j + 1], 1.0 / m, None, ALU.mult))
                chained(dve.tensor_scalar(above[:, 0:m], seq[:, 0:m], mean[:, j:j + 1], None, ALU.is_gt))
                chained(dve.tensor_reduce(count[:, j:j + 1], above[:, 0:m], AX.X, ALU.add))
            chained(dve.tensor_scalar(count[:, :], count[:, :], 1.0, None, ALU.max), "counts")
            dve.wait_ge(logged, 1)
            chained(dve.tensor_tensor(lx[:, :], lx[:, :], logs[:, :], ALU.mult))
            chained(dve.tensor_reduce(num[:, 0:1], lx[:, :], AX.X, ALU.add))
            chained(dve.tensor_reduce(num[:, 1:2], logs[:, :], AX.X, ALU.add))
            chained(dve.tensor_scalar(num[:, 2:3], num[:, 0:1], -float(len(SCALES)) / DEN, None, ALU.mult))
            chained(dve.scalar_tensor_tensor(num[:, 3:4], num[:, 1:2], SUM_LX / DEN, num[:, 2:3], ALU.mult, ALU.add))
            chained(dve.tensor_scalar(dim1[:, :], num[:, 3:4], 1.0, 2.0, ALU.max, ALU.min), "dimension")
            dve.wait_ge(spread, 1)
            chained(dve.tensor_scalar(omega[:, :], D[:, :], 0.2, 1.0, ALU.mult, ALU.add))
            chained(dve.tensor_scalar(a_par[:, :], D[:, :], 0.5, 1.0, ALU.mult, ALU.add))
            chained(dve.tensor_scalar(b_par[:, :], D[:, :], 0.1, None, ALU.mult))
            chained(dve.tensor_tensor(omega_d[:, :], omega[:, :], D[:, :], ALU.mult))
            chained(dve.tensor_scalar(arg[:, :], ka[:, :], a_par[:, :], omega_d[:, :], ALU.mult, ALU.add))
            chained(dve.tensor_scalar(arg[:, :], arg[:, :], -1.0, float(np.pi), ALU.mult, ALU.add))
            chained(dve.tensor_tensor(phase[:, :], ka[:, :], ka[:, :], ALU.mult))
            chained(dve.scalar_tensor_tensor(phase[:, :], phase[:, :], b_par[:, :], ka[:, :], ALU.mult, ALU.subtract))
            chained(dve.tensor_scalar(phase[:, :], phase[:, :], omega_d[:, :], None, ALU.add))
            chained(dve.tensor_scalar(phase[:, :], phase[:, :], -1.0, float(np.pi / 2), ALU.mult, ALU.add), "angles")
            dve.wait_ge(sined, 2)
            chained(dve.tensor_tensor(f[:, :], arg[:, :], phase[:, :], ALU.mult))
            chained(dve.tensor_tensor(Bf[:, :, :], B[:, :, :], f[:, :].unsqueeze(2).broadcast_to((P, KT, DM)), ALU.mult), "scaled")
            for m in range(KT):
                dve.wait_ge(c_done, m + 1)
                dve.tensor_copy(Cf[:, m, :], cb[m][:, :]).then_inc(c_read, 1)
            dve.wait_ge(m_done, 1)
            dve.tensor_copy(Mf[:, :, :], mb[:, :, :]).then_inc(c_read, 1)
            dve.wait_ge(hi_made, 2)
            dve.tensor_tensor(C[1][:, :, :], Cf[:, :, :], split_fp32r(C[0][:, :, :]), ALU.subtract)
            dve.tensor_tensor(M[1][:, :, 0:LATENT], Mf[:, :, :], split_fp32r(M[0][:, :, 0:LATENT]), ALU.subtract)

        @block.gpsimd
        def _(pool):
            pool.partition_all_reduce(ends[:, :], extremes[:, :], P, REDUCE.max).then_inc(reduced, 1)
            pool.wait_ge(step, n_step["dimension"])
            pool.partition_broadcast(D[:, :], dim1[:, :]).then_inc(spread, 1)

        @block.scalar
        def _(act):
            act.wait_ge(step, n_step["counts"])
            act.activation(logs[:, :], count[:, :], ACT.Ln).then_inc(logged, 1)
            act.wait_ge(step, n_step["angles"])
            act.activation(arg[:, :], arg[:, :], ACT.Sin).then_inc(sined, 1)
            act.activation(phase[:, :], phase[:, :], ACT.Sin).then_inc(sined, 1)
            act.wait_ge(c_read, KT)
            act.activation(C[0][:, :, :], Cf[:, :, :], ACT.Copy).then_inc(hi_made, 1)
            act.wait_ge(c_read, KT + 1)
            act.activation(M[0][:, :, 0:LATENT], Mf[:, :, :], ACT.Copy).then_inc(hi_made, 1)

        @block.tensor
        def _(pe):
            pe.wait_ge(step, n_step["scaled"])
            for m in range(KT):
                for k in range(KT):
                    last = pe.matmul(cb[m][:, :], Bf[:, k, m * P:(m + 1) * P], B[:, k, :], start=(k == 0), stop=(k == KT - 1))
                last.then_inc(c_done, 1)
            pe.wait_ge(c_read, KT)
            for m in range(KT):
                for k in range(KT):
                    last = pe.matmul(mb[:, m, :], Cf[:, k, m * P:(m + 1) * P], wel[:, k, :], start=(k == 0), stop=(k == KT - 1),
                                     skip_group_check=True)
            last.then_inc(m_done, 1)


def mix(nc, X, rho, top, C, M, checks, b_el, w_le, b_le, gamma_w, beta_w):
    with ExitStack() as ctx:
        def sb(name, shape, dt=FP32):
            return ctx.enter_context(nc.sbuf_tensor(f"{name}_mix", shape, dt))

        def sem(name):
            return nc.alloc_semaphore(f"{name}_mix")

        def counted(name, per_round, step=1):
            return Count(sem(name), per_round, step)

        L = LATENT
        BF16 = mybir.dt.bfloat16
        hi, lo = sb("hi", [P, 2, KT, ST], FP32R), sb("lo", [P, 2, KT, ST], FP32R)
        ident, minus_half = sb("ident", [P, P]), sb("minus_half", [P, CHUNKS])
        xs = sb("xs", [P, CHUNKS, DM])
        le_hi, le_lo = sb("le_hi", [L + 1, DM], FP32R), sb("le_lo", [L + 1, DM], FP32R)
        code = sb("code", [L + 1, ST], FP32R)
        bits, syn, fix = (sb(x, [L, ST], BF16) for x in ("bits", "syn", "fix"))
        parity_f, first_f = sb("parity_f", [L, L]), sb("first_f", [L, L])
        parity, first = sb("parity", [L, L], BF16), sb("first", [L, L], BF16)
        bel = sb("bel", [L, 1])
        g_bc, b_bc = sb("g_bc", [P, DM]), sb("b_bc", [P, DM])
        xn = sb("xn", [P, 2, DM])
        le = xn[0:L + 1, 0, :]
        stats, mv = sb("stats", [P, CHUNKS, 6]), sb("mv", [P, CHUNKS, 2])
        var1, rstd, var2 = (sb(x, [P, CHUNKS]) for x in ("var1", "rstd", "var2"))
        top_now = sb("top_now", [P, CHUNKS])

        tb = [ctx.enter_context(nc.psum_tensor(f"tb{k}_mix", [P, ST], FP32)) for k in range(2)]
        yb = [ctx.enter_context(nc.psum_tensor(f"yb{c}_mix", [P, DM], FP32)) for c in range(CHUNKS)]
        lat = ctx.enter_context(nc.psum_tensor("lat_mix", [P, ST], FP32))
        chk = ctx.enter_context(nc.psum_tensor("chk_mix", [L, ST], FP32))

        const_made, loaded, prepared = sem("const_made"), sem("loaded"), sem("prepared")
        t_done, xs_loaded = counted("t_done", KT), counted("xs_loaded", 1, 16)
        hi_ready, lo_ready = counted("hi_ready", KT), counted("lo_ready", KT)
        lat_done, syn_done, weight_done = counted("lat_done", 1), counted("syn_done", 1), counted("weight_done", 1)
        bits_ready, syn_ready = counted("bits_ready", 1), counted("syn_ready", 1)
        fix_ready, code_ready = counted("fix_ready", 1), counted("code_ready", 1)
        y_done, sum_ready = counted("y_done", CHUNKS), counted("sum_ready", CHUNKS)
        st_ready, mv_ready = counted("st_ready", CHUNKS), counted("mv_ready", CHUNKS)
        var_ready, x_ready = counted("var_ready", 4), counted("x_ready", CHUNKS)
        sq_ready = counted("sq_ready", 2)
        xn_ready, xb_ready = counted("xn_ready", CHUNKS), counted("xb_ready", CHUNKS)
        top_ready = counted("top_ready", CHUNKS + 1)
        block = ctx.enter_context(nc.Block())

        def tile(t):
            return X[:, bass.ds(t, 1), :].rearrange("p a f -> p (a f)")

        @block.sync
        def _(sp):
            xs_loaded.credit(sp)
            sp.dma_start(xs[:, :, :], X[:, 0:CHUNKS, :]).then_inc(xs_loaded.sem, 16)
            sp.dma_start(xn[0:L, 0, :], w_le).then_inc(loaded, 16)
            sp.dma_start(xn[L:L + 1, 0, :], b_le.rearrange("(a n) -> a n", a=1)).then_inc(loaded, 16)
            sp.dma_start(parity_f[:, :], checks[0]).then_inc(loaded, 16)
            sp.dma_start(first_f[:, :], checks[1]).then_inc(loaded, 16)
            sp.dma_start(bel[:, :], b_el.rearrange("(h a) -> h a", a=1)).then_inc(loaded, 16)
            sp.dma_start(g_bc[:, :], gamma_w.rearrange("(a n) -> a n", a=1).broadcast_to((P, DM))).then_inc(loaded, 16)
            sp.dma_start(b_bc[:, :], beta_w.rearrange("(a n) -> a n", a=1).broadcast_to((P, DM))).then_inc(loaded, 16)
            with sp.Fori(0, ROUNDS) as n:
                tile_next = sp.snap(((n + 1) % ROUNDS) * CHUNKS)
                sp.wait_ge(t_done.sem, t_done.now(n, KT))
                sp.dma_start(xs[:, :, :], X[:, bass.ds(tile_next, CHUNKS), :]).then_inc(xs_loaded.sem, 16)
            sp.wait_ge(xs_loaded.sem, xs_loaded.now(ROUNDS, 1))

        @block.gpsimd
        def _(pool):
            var_ready.credit(pool)
            xb_ready.credit(pool)
            pool.memset(ident[:, :], 0.0).then_inc(const_made, 1)
            pool.memset(minus_half[:, :], -0.5).then_inc(const_made, 1)
            pool.wait_ge(const_made, 2)
            pool.affine_select(out=ident[:, :], in_=ident[:, :], compare_op=ALU.not_equal, fill=1.0, base=0,
                               pattern=[[-1, P]], channel_multiplier=1).then_inc(const_made, 1)
            pool.wait_ge(const_made, 3)
            with pool.Fori(0, ROUNDS) as n:
                pool.wait_ge(mv_ready.sem, mv_ready.now(n, CHUNKS))
                pool.nop(nofuse=True)
                pool.tensor_scalar(var1[:, :], mv[:, :, 1], 1.0, LN_EPS, ALU.mult, ALU.add).then_inc(var_ready.sem, 1)
                pool.wait_ge(var_ready.sem, var_ready.now(n, 1))
                pool.tensor_tensor(rstd[:, :], var1[:, :], minus_half[:, :], ALU.pow).then_inc(var_ready.sem, 1)
                pool.wait_ge(sq_ready.sem, sq_ready.now(n, 2))
                pool.nop(nofuse=True)
                pool.tensor_scalar(var2[:, :], var2[:, :], 1.0, FFN_LN_EPS, ALU.mult, ALU.add).then_inc(var_ready.sem, 1)
                pool.wait_ge(var_ready.sem, var_ready.now(n, 3))
                pool.tensor_tensor(rho[:, bass.ds(n * CHUNKS, CHUNKS)], var2[:, :], minus_half[:, :], ALU.pow).then_inc(var_ready.sem, 1)
                for c in range(CHUNKS):
                    pool.wait_ge(xn_ready.sem, xn_ready.now(n, c + 1))
                    pool.tensor_tensor(xn[:, c % 2, :], xn[:, c % 2, :], b_bc[:, :], ALU.add).then_inc(xb_ready.sem, 1)

        @block.scalar
        def _(act):
            hi_ready.credit(act)
            act.wait_ge(loaded, 112)
            act.activation(le_hi[:, :], le, ACT.Copy).then_inc(prepared, 1)

            def high_parts(n, slot):
                for k in range(KT):
                    act.wait_ge(t_done.sem, t_done.now(n, k + 1))
                    act.activation(hi[:, slot, k, :], tb[k % 2][:, :], ACT.Copy).then_inc(hi_ready.sem, 1)

            high_parts(0, 0)
            with act.Fori(0, ROUNDS // 2) as i:
                for s in range(2):
                    n = i * 2 + s
                    act.wait_ge(y_done.sem, y_done.before(n, CHUNKS))
                    high_parts(n + 1, 1 - s)

        @block.vector
        def _(dve):
            for c in (lo_ready, bits_ready, syn_ready, fix_ready, code_ready, sum_ready, st_ready, mv_ready, x_ready, sq_ready,
                      xn_ready, top_ready):
                c.credit(dve)
            dve.memset(top[:, :], 0.0)
            dve.memset(code[:, :].bitcast(FP32), 1.0)
            dve.wait_ge(loaded, 112)
            dve.tensor_copy(parity[:, :], parity_f[:, :])
            dve.tensor_copy(first[:, :], first_f[:, :]).then_inc(prepared, 1)
            dve.wait_ge(prepared, 2)
            dve.tensor_tensor(le_lo[:, :], le, split_fp32r(le_hi[:, :]), ALU.subtract).then_inc(prepared, 1)

            def low_parts(n, slot):
                for k in range(KT):
                    dve.wait_ge(hi_ready.sem, hi_ready.now(n, k + 1))
                    dve.tensor_tensor(lo[:, slot, k, :], tb[k % 2][:, :], split_fp32r(hi[:, slot, k, :]), ALU.subtract).then_inc(lo_ready.sem, 1)

            low_parts(0, 0)
            with dve.Fori(0, ROUNDS // 2) as i:
                for s in range(2):
                    n = i * 2 + s
                    dve.wait_ge(lat_done.sem, lat_done.now(n, 1))
                    dve.tensor_scalar(bits[:, :], lat[0:L, :], bel[:, :], 0.0, ALU.add, ALU.is_gt).then_inc(bits_ready.sem, 1)
                    dve.wait_ge(syn_done.sem, syn_done.now(n, 1))
                    dve.tensor_scalar(syn[:, :], chk[:, :], 0.5, None, ALU.is_gt).then_inc(syn_ready.sem, 1)
                    dve.wait_ge(weight_done.sem, weight_done.now(n, 1))
                    dve.wait_ge(syn_ready.sem, syn_ready.now(n, 1))
                    dve.scalar_tensor_tensor(fix[:, :], chk[:, :], 3.5, syn[:, :], ALU.is_lt, ALU.mult).then_inc(fix_ready.sem, 1)
                    dve.wait_ge(fix_ready.sem, fix_ready.now(n, 1))
                    dve.wait_ge(y_done.sem, y_done.before(n, CHUNKS))
                    dve.tensor_tensor(code[0:L, :], bits[:, :], fix[:, :], ALU.not_equal).then_inc(code_ready.sem, 1)
                    low_parts(n + 1, 1 - s)
                    for c in range(CHUNKS):
                        x = tile(n * CHUNKS + c)
                        dve.wait_ge(y_done.sem, y_done.now(n, c + 1))
                        dve.tensor_tensor(x, yb[c][:, :], x, ALU.add).then_inc(sum_ready.sem, 1)
                        dve.wait_ge(sum_ready.sem, sum_ready.now(n, c + 1))
                        dve.nop(nofuse=True)
                        dve.bn_stats(stats[:, c, :], x).then_inc(st_ready.sem, 1)
                        dve.wait_ge(st_ready.sem, st_ready.now(n, c + 1))
                        dve.nop(nofuse=True)
                        dve.bn_aggr(mv[:, c, :], stats[:, c, :]).then_inc(mv_ready.sem, 1)
                    dve.wait_ge(var_ready.sem, var_ready.now(n, 2))
                    dve.tensor_tensor(var2[:, :], mv[:, :, 1], rstd[:, :], ALU.mult).then_inc(sq_ready.sem, 1)
                    dve.wait_ge(sq_ready.sem, sq_ready.now(n, 1))
                    dve.tensor_tensor(var2[:, :], var2[:, :], rstd[:, :], ALU.mult).then_inc(sq_ready.sem, 1)
                    for c in range(CHUNKS):
                        x = tile(n * CHUNKS + c)
                        dve.tensor_scalar(x, x, mv[:, c, 0:1], rstd[:, c:c + 1], ALU.subtract, ALU.mult).then_inc(x_ready.sem, 1)
                    dve.wait_ge(var_ready.sem, var_ready.now(n, 4))

                    def top_of(c):
                        dve.wait_ge(xb_ready.sem, xb_ready.now(n, c + 1))
                        dve.tensor_reduce(top_now[:, c:c + 1], xn[:, c % 2, :], AX.X, ALU.max, apply_absolute_value=True).then_inc(top_ready.sem, 1)

                    for c in range(CHUNKS):
                        if c >= 2:
                            top_of(c - 2)
                            dve.wait_ge(top_ready.sem, top_ready.now(n, c - 1))
                        dve.wait_ge(x_ready.sem, x_ready.now(n, c + 1))
                        dve.scalar_tensor_tensor(xn[:, c % 2, :], tile(n * CHUNKS + c), rho[:, bass.ds(n * CHUNKS + c, 1)], g_bc[:, :],
                                                 ALU.mult, ALU.mult).then_inc(xn_ready.sem, 1)
                    top_of(2)
                    top_of(3)
                    dve.wait_ge(top_ready.sem, top_ready.now(n, CHUNKS))
                    dve.tensor_tensor(top[:, :], top[:, :], top_now[:, :], ALU.max).then_inc(top_ready.sem, 1)

        @block.tensor
        def _(pe):
            for c in (t_done, lat_done, syn_done, weight_done, y_done):
                c.credit(pe)
            pe.wait_ge(const_made, 3)

            def transposes(n):
                pe.wait_ge(xs_loaded.sem, xs_loaded.now(n, 1))
                for k in range(KT):
                    pe.wait_ge(lo_ready.sem, lo_ready.now(n, k - 1) if k >= 2 else lo_ready.before(n, k + 3))
                    pe.nop(nofuse=True)
                    for c in range(CHUNKS):
                        last = pe.transpose(tb[k % 2][:, c * P:(c + 1) * P], xs[:, c, k * P:(k + 1) * P], ident[:, :])
                    last.then_inc(t_done.sem, 1)

            transposes(0)
            pe.wait_ge(prepared, 3)
            with pe.Fori(0, ROUNDS // 2) as i:
                for s in range(2):
                    n = i * 2 + s
                    pe.wait_ge(lo_ready.sem, lo_ready.now(n, KT))
                    pe.wait_ge(bits_ready.sem, bits_ready.before(n, 1))
                    for t, (a, b) in enumerate(((M[0], hi), (M[1], hi), (M[0], lo))):
                        for k in range(KT):
                            last = pe.matmul(lat[:, :], a[:, k, :], b[:, s, k, :], start=(t + k == 0), stop=(t == 2 and k == KT - 1))
                    last.then_inc(lat_done.sem, 1)

                    def filtered(c):
                        pe.wait_ge(sum_ready.sem, sum_ready.before(n, c + 1))
                        for t, (a, b) in enumerate(((hi, C[0]), (hi, C[1]), (lo, C[0]))):
                            for k in range(KT):
                                pe.matmul(yb[c][:, :], a[:, s, k, c * P:(c + 1) * P], b[:, k, :], start=(t + k == 0), stop=False)

                    def coded(c):
                        for part in (le_hi, le_lo):
                            last = pe.matmul(yb[c][:, :], code[:, c * P:(c + 1) * P], part[:, :], start=False, stop=(part is le_lo))
                        last.then_inc(y_done.sem, 1)

                    filtered(0)
                    pe.wait_ge(bits_ready.sem, bits_ready.now(n, 1))
                    pe.wait_ge(fix_ready.sem, fix_ready.before(n, 1))
                    pe.nop(nofuse=True)
                    pe.matmul(chk[:, :], parity[:, :], bits[:, :], start=True, stop=True).then_inc(syn_done.sem, 1)
                    filtered(1)
                    pe.wait_ge(syn_ready.sem, syn_ready.now(n, 1))
                    pe.nop(nofuse=True)
                    pe.matmul(chk[:, :], first[:, :], syn[:, :], start=True, stop=True).then_inc(weight_done.sem, 1)
                    filtered(2)
                    filtered(3)
                    pe.wait_ge(code_ready.sem, code_ready.now(n, 1))
                    pe.nop(nofuse=True)
                    for c in range(CHUNKS):
                        coded(c)
                    transposes(n + 1)


def program(nc, x, x_t, wv_t, wg_t, wk_t, wq_t, wog_t, wo_t, wd_t, bd, norm_w, ln_gamma0, ln_beta0, gcol0, bcol0, w0,
            basis, freq, w_el, b_el, parity, first, w_le, b_le, ln_gamma1, ln_beta1, gcol1, bcol1, w1, out):
    g_dram = nc.dram_tensor("log_decay_dram", [HEADS, TOKENS], FP32, kind="Internal").ap()
    y_dram = nc.dram_tensor("y_first_dram", [TOKENS, DM], FP32, kind="Internal").ap()
    x1_dram = nc.dram_tensor("x1_dram", [TOKENS, DM], FP32, kind="Internal").ap()
    wT = {"v": wv_t, "g": wg_t, "k": wk_t, "q": wq_t, "og": wog_t}
    with nc.sbuf_tensor("rho", [P, TILES], FP32) as rho, nc.sbuf_tensor("top", [P, CHUNKS], FP32) as top:
        with nc.sbuf_tensor("ssq", [P, TILES], FP32) as ssq:
            late = {"x": x, "x1": x1_dram, "ln_gamma": ln_gamma0, "ln_beta": ln_beta0, "rho": rho, "top": top}
            for half in range(HALVES):
                with nc.cleanup_on_exit():
                    attention_half(nc, half, x_t, wT, wo_t, wd_t, bd, norm_w, g_dram, y_dram, ssq, late)
        with nc.sbuf_tensor("X", [P, TILES, DM], FP32) as X, nc.sbuf_tensor("extremes", [P, 2], FP32) as extremes:
            with nc.cleanup_on_exit():
                quantised_product(nc, "first", X, rho, top, x1_dram, w0, gcol0, bcol0, extremes, None)
            with ExitStack() as ctx:
                C = [ctx.enter_context(nc.sbuf_tensor(f"C_{part}", [P, KT, DM], FP32R)) for part in ("hi", "lo")]
                M = [ctx.enter_context(nc.sbuf_tensor(f"M_{part}", [P, KT, P], FP32R)) for part in ("hi", "lo")]
                with nc.cleanup_on_exit():
                    wave_filter(nc, X, extremes, basis, freq, w_el, C, M)
                with nc.cleanup_on_exit():
                    mix(nc, X, rho, top, C, M, (parity, first), b_el, w_le, b_le, ln_gamma1, ln_beta1)
            with nc.cleanup_on_exit():
                quantised_product(nc, "second", X, rho, top, None, w1, gcol1, bcol1, None, out)


def kernel(**inputs):
    import concourse.bacc as bacc
    from concourse.bass_utils import run_bass_kernel_spmd

    def laid(a):
        return np.ascontiguousarray(a)

    def columns(v):
        return laid(np.asarray(v).reshape(-1, P).T)

    x = np.asarray(inputs["L0_attn_x"]).reshape(TOKENS, DM)
    point, wave = np.arange(DM), np.arange(DM // 2 + 1)
    angle = 2 * np.pi * ((wave[:, None] * point[None, :]) % DM) / DM
    cosines, sines = np.cos(angle) * np.sqrt(2 / DM), np.sin(angle[1:-1]) * np.sqrt(2 / DM)
    cosines[[0, -1]] /= np.sqrt(2)
    basis = np.concatenate([cosines, sines]).astype(np.float32)
    freq = np.concatenate([wave, wave[1:-1]]).astype(np.float32) / np.float32(DM) + np.float32(1e-8)
    rows = ("111011100011", "110111000110", "101110001101", "011100011011", "000011111111", "111100000000",
            "000011110000", "110011001100", "101010101010", "010101010101", "100110011001", "011001100110")
    parity = np.zeros((LATENT, LATENT), np.float32)
    parity[:CHECKS, :CHECKS] = [[int(b) for b in row] for row in rows]
    parity[CHECKS:, :CHECKS] = np.eye(CHECKS)
    first = np.zeros((LATENT, LATENT), np.float32)
    first[:CHECKS, :] = 1.0

    given = {
        "x": x, "x_t": laid(x.T),
        **{f"w{n}_t": laid(np.asarray(inputs[f"L0_attn_W{n}"]).T) for n in ("v", "g", "k", "q", "og", "o", "d")},
        "bd": inputs["L0_attn_bd"], "norm_w": columns(inputs["L0_attn_norm_w"]),
        "ln_gamma0": inputs["L0_ffn_ln_gamma"], "ln_beta0": inputs["L0_ffn_ln_beta"],
        "gcol0": columns(inputs["L0_ffn_ln_gamma"]), "bcol0": columns(inputs["L0_ffn_ln_beta"]), "w0": inputs["L0_ffn_weight"],
        "basis": basis, "freq": columns(freq), "w_el": inputs["L1_attn_W_el"], "b_el": inputs["L1_attn_b_el"],
        "parity": parity, "first": first, "w_le": inputs["L1_attn_W_le"], "b_le": inputs["L1_attn_b_le"],
        "ln_gamma1": inputs["L1_ffn_ln_gamma"], "ln_beta1": inputs["L1_ffn_ln_beta"],
        "gcol1": columns(inputs["L1_ffn_ln_gamma"]), "bcol1": columns(inputs["L1_ffn_ln_beta"]), "w1": inputs["L1_ffn_weight"],
    }
    given = {name: laid(np.asarray(a)) for name, a in given.items()}
    nc = bacc.Bacc("TRN2", target_bir_lowering=False, num_devices=1)
    args = {name: nc.dram_tensor(name, a.shape, mybir.dt.from_np(a.dtype), kind="ExternalInput").ap() for name, a in given.items()}
    out = nc.dram_tensor("result", (TOKENS, DM), FP32, kind="ExternalOutput").ap()
    program(nc, out=out, **args)
    result = run_bass_kernel_spmd(nc, [given], core_ids=[0])
    return result.results[0]["result"].reshape(BATCH, SEQ, DM)
```

```python
import numpy as np
import concourse.bass as bass
from concourse import mybir
from contextlib import ExitStack

FP32 = mybir.dt.float32
FP32R = mybir.dt.float32r
ALU = mybir.AluOpType
ACT = mybir.ActivationFunctionType
AX = mybir.AxisListType
REDUCE = bass.bass_isa.ReduceOp

P = 128
BATCH, SEQ, DM = 4, 2048, 512
TOKENS = BATCH * SEQ
HEADS, DH = 16, 64
HID = HEADS * DH
HALVES = 2
HALF = HID // HALVES
HH = HEADS // HALVES
PAIRS = HALF // P
KT = DM // P
ST = 512
CH = P
CHUNKS = ST // CH
ROUNDS = TOKENS // ST
ROUNDS_PER_BATCH = SEQ // ST
TILES = TOKENS // P
LN_EPS = 1e-5
FFN_LN_EPS = 1e-3
RMS_EPS = float(np.finfo(np.float32).eps)
QB, Q_EPS = 128.0, 1e-5
MASKED = -1e30


class Count:

    def __init__(self, sem, per_round, step=1):
        self.sem, self.per_round, self.step = sem, per_round, step

    def credit(self, engine):
        engine.sem_inc(self.sem, self.step * self.per_round)

    def now(self, r, j):
        return (r + 1) * (self.step * self.per_round) + self.step * j

    def before(self, r, j):
        return r * (self.step * self.per_round) + self.step * j


def past(n, first):
    return type(n) is not int or n >= first


def split_fp32r(hi):
    return hi.bitcast(FP32)


def attention_half(nc, half, xT, wT, woT, wdT, bd, norm_w, g_dram, y_dram, ssq, late):
    hid0 = half * HALF
    with ExitStack() as ctx:
        def sb(name, shape, dt=FP32):
            return ctx.enter_context(nc.sbuf_tensor(f"{name}_{half}", shape, dt))

        def sem(name):
            return nc.alloc_semaphore(f"{name}_{half}")

        def counted(name, per_round, step=1):
            return Count(sem(name), per_round, step)

        W = {}
        for name in ("v", "g", "k", "q", "og"):
            W[name] = (sb(f"w_{name}_hi", [P, KT, HALF], FP32R), sb(f"w_{name}_lo", [P, KT, HALF], FP32R))
        wo_hi, wo_lo = sb("wo_hi", [P, PAIRS, DM], FP32R), sb("wo_lo", [P, PAIRS, DM], FP32R)
        if half == 0:
            wd_raw = sb("wd_raw", [P, KT, HEADS])
            wd_hi, wd_lo = sb("wd_hi", [P, KT, P], FP32R), sb("wd_lo", [P, KT, P], FP32R)
            bd_sb = sb("bd", [HEADS, 1])
        norm_sb = sb("norm", [P, PAIRS])
        x_raw = sb("x_raw", [P, KT, ST])
        x_hi, x_lo = sb("x_hi", [P, KT, ST], FP32R), sb("x_lo", [P, KT, ST], FP32R)
        qT, kT = sb("qT", [P, 2, ST]), sb("kT", [P, 2, ST])
        gate = sb("gate", [P, ST])
        osig = sb("osig", [P, 2, ST])
        q_dec = sb("q_dec", [P, ST])
        k_dec = sb("k_dec", [P, CHUNKS, 2, DH])
        G = sb("G", [P, 2, 2, CHUNKS, CH])
        E = sb("E", [P, 2, CHUNKS, CH])
        A = sb("A", [P, 2, CHUNKS, CH])
        v = sb("v", [P, CHUNKS, HALF])
        o_hi, o_lo = sb("o_hi", [P, PAIRS, ST], FP32R), sb("o_lo", [P, PAIRS, ST], FP32R)
        o_gated = sb("o_gated", [P, ST])
        sq = sb("sq", [P, ST])
        sq_sum = sb("sq_sum", [P, ST])
        S_in = sb("S_in", [P, PAIRS, P])
        S = sb("S", [P, 2, CHUNKS, P])
        gT = sb("gT", [HEADS, ST])
        gs = sb("gs", [P, CHUNKS, HH])
        mask = sb("mask", [P, CH])
        ident = sb("ident", [P, P])
        ones = sb("ones", [P, CH])
        z_l = A[0:HEADS, 0, :, :].rearrange("p c t -> p (c t)")
        z_m = A[0:HEADS, 1, :, :].rearrange("p c t -> p (c t)")

        pj = [ctx.enter_context(nc.psum_tensor(f"pj{b}_{half}", [P, 512], FP32)) for b in range(4)]
        sc = [ctx.enter_context(nc.psum_tensor(f"sc{b}_{half}", [P, CHUNKS, CH], FP32)) for b in range(2)]
        kk = ctx.enter_context(nc.psum_tensor(f"kk_{half}", [P, CHUNKS, P], FP32))
        ot = ctx.enter_context(nc.psum_tensor(f"ot_{half}", [P, ST], FP32))

        stage_names = ("v", "g", "k", "q", "og", "o")
        const_made = sem("const_made")
        small_loaded = sem("small_loaded")
        w_loaded = {name: sem(f"w_{name}_loaded") for name in stage_names}
        pad_made, wd_hi_made, wd_lo_made = sem("pad_made"), sem("wd_hi_made"), sem("wd_lo_made")
        w_hi_made, w_lo_made = sem("w_hi_made"), sem("w_lo_made")
        z_done, v_done = counted("z_done", 1), counted("v_done", CHUNKS)
        g_done, k_done = counted("g_done", PAIRS), counted("k_done", PAIRS)
        q_done, og_done = counted("q_done", PAIRS), counted("og_done", PAIRS)
        gst_done, kt_done = counted("gst_done", 1), counted("kt_done", PAIRS)
        sc_done, kv_done = counted("sc_done", 2 * PAIRS), counted("kv_done", PAIRS)
        o_done, y_done = counted("o_done", PAIRS), counted("y_done", CHUNKS)
        ssq_done = counted("ssq_done", 1)
        xh_ready, zabs_ready = counted("xh_ready", 1), counted("zabs_ready", 1)
        zexp_ready, zlog_ready = counted("zexp_ready", 1), counted("zlog_ready", 1)
        v_ready, gate_ready = counted("v_ready", CHUNKS), counted("gate_ready", PAIRS)
        q_ready, osig_ready = counted("q_ready", PAIRS), counted("osig_ready", PAIRS)
        e_ready, d_ready = counted("e_ready", PAIRS), counted("d_ready", PAIRS)
        sq_ready, oh_ready = counted("sq_ready", PAIRS), counted("oh_ready", PAIRS)
        xl_ready, zmax_ready = counted("xl_ready", 1), counted("zmax_ready", 1)
        glog_ready, gT_ready = counted("glog_ready", 1), counted("gT_ready", 1)
        k_ready, gs_ready = counted("k_ready", PAIRS), counted("gs_ready", 1)
        kdec_ready, a_ready = counted("kdec_ready", PAIRS), counted("a_ready", 2 * PAIRS)
        s_step, s_ready = counted("s_step", 2 * PAIRS * CHUNKS), counted("s_ready", PAIRS)
        og_ready, ol_ready = counted("og_ready", PAIRS), counted("ol_ready", PAIRS)
        carried, ssq_read = counted("carried", PAIRS), counted("ssq_read", 1)
        zeroed = sem("zeroed")
        y_free = counted("y_free", CHUNKS)
        dsub_ready, dmask_ready = counted("dsub_ready", PAIRS), counted("dmask_ready", PAIRS)
        qd_ready, sqsum_ready = counted("qd_ready", PAIRS), counted("sqsum_ready", PAIRS)
        x_loaded = counted("x_loaded", 1, 16)
        gT_stored, gT_loaded = counted("gT_stored", 1, 16), counted("gT_loaded", 1, 16)
        G_loaded = [counted(f"G_loaded{s}", PAIRS // 2, 16) for s in range(2)]
        y_stored = [counted(f"y_stored{s}", CHUNKS // 2, 16) for s in range(2)]

        if half == 0:
            y_out = sb("y_out", [P, 2, DM])
        else:
            x_tok = sb("x_tok", [P, CHUNKS, DM])
            y_first = [osig[:, 0, :], osig[:, 1, :], sq[:, :], o_gated[:, :]]
            xn_of = [sq[:, :], o_gated[:, :]]
            stats, mv = sb("stats", [P, CHUNKS, 6]), sb("mv", [P, CHUNKS, 2])
            rms = sb("rms", [P, CHUNKS])
            var1, rstd, var2 = (sb(n, [P, CHUNKS]) for n in ("var1", "rstd", "var2"))
            g_bc, b_bc = sb("g_bc", [P, DM]), sb("b_bc", [P, DM])
            top_now = sb("top_now", [P, CHUNKS])
            minus_half = sb("minus_half", [P, CHUNKS])
            xt_loaded = [counted(f"xt_loaded{c}", 1, 16) for c in range(CHUNKS)]
            yf_loaded = [counted(f"yf_loaded{c}", 1, 16) for c in range(CHUNKS)]
            x1_stored = counted("x1_stored", CHUNKS, 16)
            rms_ready, t2_ready = counted("rms_ready", 2), counted("t2_ready", CHUNKS)
            st_ready, mv_ready = counted("st_ready", CHUNKS), counted("mv_ready", CHUNKS)
            var_ready = counted("var_ready", 5)
            x1_ready = counted("x1_ready", CHUNKS)
            xn_step = counted("xn_step", 3 * CHUNKS + 1)
            sq_rstd = counted("sq_rstd", 1)
            loaded_gb = sem("loaded_gb")

        decays = G[:, :, :, :, :].rearrange("p s h c t -> p (s h c t)").rearrange("p (k n) -> p k n", k=KT)
        stage = {"v": (v[:, :, :],), "g": (decays,), "k": (kT[:, :, :], qT[:, :, :]),
                 "q": tuple(buffer[:, :, :, :].rearrange("p j c t -> p j (c t)") for buffer in (A, E)),
                 "og": (v[:, :, :],), "o": (decays,)}

        def pieces(name):
            n = KT // len(stage[name])
            return [(piece, slice(i * n, (i + 1) * n)) for i, piece in enumerate(stage[name])]


        block = ctx.enter_context(nc.Block())

        @block.sync
        def _(sp):
            for c in (x_loaded, gT_stored, gT_loaded, *G_loaded, *y_stored):
                c.credit(sp)
            sp.dma_start(x_raw[:, :, :], xT[:, 0:ST].rearrange("(k p) t -> p k t", p=P)).then_inc(x_loaded.sem, 16)
            if half == 0:
                sp.dma_start(wd_raw[:, :, :], wdT.rearrange("(k p) h -> p k h", p=P)).then_inc(small_loaded, 16)
                sp.dma_start(bd_sb[:, :], bd.rearrange("(h a) -> h a", a=1)).then_inc(small_loaded, 16)
            sp.dma_start(norm_sb[:, :], norm_w[:, half * PAIRS:(half + 1) * PAIRS]).then_inc(small_loaded, 16)
            for name in stage_names:
                if name == "og":
                    sp.wait_ge(w_lo_made, 1)
                elif name == "o":
                    sp.wait_ge(w_lo_made, 2)
                if name == "o":
                    src = woT[hid0:hid0 + HALF, :].rearrange("(b p) n -> p b n", p=P)
                else:
                    src = wT[name][:, hid0:hid0 + HALF].rearrange("(k p) n -> p k n", p=P)
                for piece, blocks in pieces(name):
                    sp.dma_start(piece, src[:, blocks, :]).then_inc(w_loaded[name], 16)
            if half == 1:
                for c in (*xt_loaded, *yf_loaded, x1_stored):
                    c.credit(sp)
                sp.dma_start(g_bc[:, :], late["ln_gamma"].rearrange("(a n) -> a n", a=1).broadcast_to((P, DM))).then_inc(loaded_gb, 16)
                sp.dma_start(b_bc[:, :], late["ln_beta"].rearrange("(a n) -> a n", a=1).broadcast_to((P, DM))).then_inc(loaded_gb, 16)
            sp.wait_ge(w_lo_made, 5 + PAIRS)
            with sp.Fori(0, ROUNDS) as n:
                start = sp.snap(((n + 1) % ROUNDS) * ST)
                sp.wait_ge(xl_ready.sem, xl_ready.now(n, 1))
                sp.dma_start(x_raw[:, :, :], xT[:, bass.ds(start, ST)].rearrange("(k p) t -> p k t", p=P)).then_inc(x_loaded.sem, 16)
                if half == 0:
                    sp.wait_ge(gT_ready.sem, gT_ready.now(n, 1))
                    sp.dma_start(g_dram[:, bass.ds(n * ST, ST)], gT[:, :]).then_inc(gT_stored.sem, 16)
                    sp.wait_ge(gT_stored.sem, gT_stored.now(n, 1))
                else:
                    sp.wait_ge(gst_done.sem, gst_done.before(n, 1))
                    sp.dma_start(gT[0:HH, :], g_dram[HH:HEADS, bass.ds(n * ST, ST)]).then_inc(gT_loaded.sem, 16)
                for p in range(PAIRS):
                    start = sp.snap(n * ST)
                    sp.wait_ge(kdec_ready.sem, kdec_ready.before(n, p + 3) if p < 2 else kdec_ready.now(n, p - 1))
                    sp.nop(nofuse=True)
                    sp.wait_ge(a_ready.sem, a_ready.before(n, 2 * (p + 3)) if p < 2 else a_ready.now(n, 2 * (p - 1)))
                    src = g_dram[half * HH + 2 * p:half * HH + 2 * p + 2, bass.ds(start, ST)].unsqueeze(0).broadcast_to((P, 2, ST))
                    sp.dma_start(G[:, p % 2, :, :, :].rearrange("p h c t -> p h (c t)"), src).then_inc(G_loaded[p % 2].sem, 16)
                if half == 0:
                    for c in range(CHUNKS):
                        sp.wait_ge(y_free.sem, y_free.now(n, c + 1))
                        sp.dma_start(y_dram[bass.ds(n * ST + c * P, P), :], y_out[:, c % 2, :]).then_inc(y_stored[c % 2].sem, 16)
                else:
                    for c in range(CHUNKS):
                        sp.wait_ge(x1_stored.sem, x1_stored.before(n, CHUNKS))
                        sp.wait_ge(xn_step.sem, xn_step.before(n, 3 * CHUNKS + 1))
                        sp.dma_start(x_tok[:, c, :], late["x"][bass.ds(n * ST + c * P, P), :]).then_inc(xt_loaded[c].sem, 16)
                    for c in range(CHUNKS):
                        if c < 2:
                            sp.wait_ge(og_ready.sem, og_ready.now(n, PAIRS - 1 + c))
                        elif c == 2:
                            sp.wait_ge(sqsum_ready.sem, sqsum_ready.now(n, PAIRS))
                        else:
                            sp.wait_ge(ol_ready.sem, ol_ready.now(n, PAIRS))
                        sp.dma_start(y_first[c], y_dram[bass.ds(n * ST + c * P, P), :]).then_inc(yf_loaded[c].sem, 16)
                    for c in range(CHUNKS):
                        sp.wait_ge(x1_ready.sem, x1_ready.now(n, c + 1))
                        sp.dma_start(late["x1"][bass.ds(n * ST + c * P, P), :], x_tok[:, c, :]).then_inc(x1_stored.sem, 16)
            for c, per in ([(y, CHUNKS // 2) for y in y_stored] if half == 0 else [(x1_stored, CHUNKS)]):
                sp.wait_ge(c.sem, c.now(ROUNDS - 1, per))
            sp.wait_ge(x_loaded.sem, x_loaded.now(ROUNDS, 1))

        @block.gpsimd
        def _(pool):
            for c in (dsub_ready, dmask_ready, qd_ready, sqsum_ready):
                c.credit(pool)
            pool.memset(mask[:, :], 0.0).then_inc(const_made, 1)
            pool.memset(ident[:, :], 0.0).then_inc(const_made, 1)
            pool.memset(ones[:, :], 1.0).then_inc(const_made, 1)
            pool.wait_ge(const_made, 3)
            pool.affine_select(out=mask[:, :], in_=mask[:, :], compare_op=ALU.is_ge, fill=MASKED, base=0,
                               pattern=[[1, CH]], channel_multiplier=-1).then_inc(const_made, 1)
            pool.affine_select(out=ident[:, :], in_=ident[:, :], compare_op=ALU.not_equal, fill=1.0, base=0,
                               pattern=[[-1, P]], channel_multiplier=1).then_inc(const_made, 1)
            if half == 1:
                var_ready.credit(pool)
                pool.memset(minus_half[:, :], -0.5).then_inc(const_made, 1)
            pool.wait_ge(const_made, 5 + (half == 1))

            def decay(n, p):
                Gp = G[:, p % 2, :, :, :]
                pool.wait_ge(e_ready.sem, e_ready.now(n, p + 1))
                if p == 0:
                    pool.wait_ge(gs_ready.sem, gs_ready.now(n, 1))
                pool.tensor_tensor(Gp, Gp, gs[:, :, 2 * p:2 * p + 2].rearrange("p c h -> p h c").unsqueeze(3).broadcast_to((P, 2, CHUNKS, CH)),
                                   ALU.subtract).then_inc(dsub_ready.sem, 1)
                pool.wait_ge(dsub_ready.sem, dsub_ready.now(n, p + 1))
                G8 = Gp.rearrange("p h c t -> p (h c) t")
                pool.tensor_tensor(G8, G8, mask[:, :].unsqueeze(1).broadcast_to((P, 2 * CHUNKS, CH)), ALU.add).then_inc(dmask_ready.sem, 1)

            def query_decay(n, p):
                pool.wait_ge(q_ready.sem, q_ready.now(n, p + 1))
                pool.wait_ge(o_done.sem, o_done.now(n, p) if p else o_done.before(n, PAIRS))
                pool.tensor_tensor(q_dec[:, :], qT[:, p % 2, :], E[:, p % 2, :, :].rearrange("p c t -> p (c t)"),
                                   ALU.mult).then_inc(qd_ready.sem, 1)

            def squares(n, p):
                pool.wait_ge(sq_ready.sem, sq_ready.now(n, p + 1))
                if p == 0:
                    pool.wait_ge(ssq_done.sem, ssq_done.before(n, 1))
                    pool.nop(nofuse=True)
                    pool.tensor_scalar(sq_sum[:, :], sq[:, :], 1.0, 0.0, ALU.mult, ALU.add).then_inc(sqsum_ready.sem, 1)
                else:
                    pool.wait_ge(sqsum_ready.sem, sqsum_ready.now(n, p))
                    pool.tensor_tensor(sq_sum[:, :], sq_sum[:, :], sq[:, :], ALU.add).then_inc(sqsum_ready.sem, 1)

            with pool.Fori(0, ROUNDS) as n:
                decay(n, 0)
                query_decay(n, 0)
                decay(n, 1)
                query_decay(n, 1)
                squares(n, 0)
                decay(n, 2)
                query_decay(n, 2)
                squares(n, 1)
                decay(n, 3)
                query_decay(n, 3)
                squares(n, 2)
                squares(n, 3)
                if half == 1:
                    pool.wait_ge(rms_ready.sem, rms_ready.now(n, 1))
                    pool.tensor_tensor(rms[:, :], rms[:, :], minus_half[:, :], ALU.pow).then_inc(var_ready.sem, 1)
                    pool.wait_ge(mv_ready.sem, mv_ready.now(n, CHUNKS))
                    pool.nop(nofuse=True)
                    pool.tensor_scalar(var1[:, :], mv[:, :, 1], 1.0, LN_EPS, ALU.mult, ALU.add).then_inc(var_ready.sem, 1)
                    pool.wait_ge(var_ready.sem, var_ready.now(n, 2))
                    pool.tensor_tensor(rstd[:, :], var1[:, :], minus_half[:, :], ALU.pow).then_inc(var_ready.sem, 1)
                    pool.wait_ge(rms_ready.sem, rms_ready.now(n, 2))
                    pool.nop(nofuse=True)
                    pool.tensor_scalar(var2[:, :], var2[:, :], 1.0, FFN_LN_EPS, ALU.mult, ALU.add).then_inc(var_ready.sem, 1)
                    pool.wait_ge(var_ready.sem, var_ready.now(n, 4))
                    pool.tensor_tensor(late["rho"][:, bass.ds(n * CHUNKS, CHUNKS)], var2[:, :], minus_half[:, :], ALU.pow).then_inc(var_ready.sem, 1)

        @block.scalar
        def _(act):
            for c in (xh_ready, zabs_ready, zexp_ready, zlog_ready, v_ready, gate_ready, q_ready, osig_ready,
                      e_ready, d_ready, sq_ready, oh_ready):
                c.credit(act)
            if half == 0:
                y_free.credit(act)
            if half == 0:
                act.wait_ge(small_loaded, 48)
                act.wait_ge(pad_made, 2)
                act.activation(wd_hi[:, :, 0:HEADS], wd_raw[:, :, :], ACT.Copy).then_inc(wd_hi_made, 1)
            def split_x(n_of_x):
                act.wait_ge(x_loaded.sem, x_loaded.now(n_of_x, 1))
                act.activation(x_hi[:, :, :], x_raw[:, :, :], ACT.Copy).then_inc(xh_ready.sem, 1)

            split_x(0)
            for name in stage_names[:-1]:
                act.wait_ge(w_loaded[name], 16 * len(stage[name]))
                for piece, blocks in pieces(name):
                    split = act.activation(W[name][0][:, blocks, :], piece, ACT.Copy)
                split.then_inc(w_hi_made, 1)
            act.wait_ge(small_loaded, 48 if half == 0 else 16)
            act.wait_ge(w_loaded["o"], 16)
            for b in range(PAIRS):
                act.activation(wo_hi[:, b, :], decays[:, b, :], ACT.Copy, scale=norm_sb[:, b:b + 1]).then_inc(w_hi_made, 1)
            act.wait_ge(w_lo_made, 5)

            def log_decay(n):
                act.wait_ge(zmax_ready.sem, zmax_ready.now(n, 1))
                act.activation(z_l, ot[0:HEADS, :], ACT.Abs, bias=bd_sb[:, :]).then_inc(zabs_ready.sem, 1)
                act.wait_ge(zabs_ready.sem, zabs_ready.now(n, 1))
                act.activation(z_l, z_l, ACT.Exp, scale=-1.0).then_inc(zexp_ready.sem, 1)
                act.wait_ge(zexp_ready.sem, zexp_ready.now(n, 1))
                act.activation(z_l, z_l, ACT.Ln, bias=1.0).then_inc(zlog_ready.sem, 1)

            def values(n):
                for c in range(CHUNKS):
                    act.wait_ge(v_done.sem, v_done.now(n, c + 1))
                    act.activation(v[:, c, :], pj[c][:, :], ACT.Copy).then_inc(v_ready.sem, 1)

            def gate_tanh(n, p):
                act.wait_ge(g_done.sem, g_done.now(n, p + 1))
                act.wait_ge(k_ready.sem, k_ready.now(n, p) if p else k_ready.before(n, PAIRS))
                act.activation(gate[:, :], pj[0][:, :], ACT.Tanh, scale=0.5).then_inc(gate_ready.sem, 1)

            def queries(n, p):
                act.wait_ge(q_done.sem, q_done.now(n, p + 1))
                act.wait_ge(sc_done.sem, sc_done.now(n, 2 * (p - 1)) if p >= 2 else sc_done.before(n, 2 * (p + 3)))
                act.wait_ge(qd_ready.sem, qd_ready.now(n, p - 1) if p >= 2 else qd_ready.before(n, p + 3))
                act.activation(qT[:, p % 2, :], pj[2][:, :], ACT.Copy, scale=0.5).then_inc(q_ready.sem, 1)

            def out_gate(n, p):
                act.wait_ge(og_done.sem, og_done.now(n, p + 1))
                act.wait_ge(og_ready.sem, og_ready.now(n, p - 1) if p >= 2 else og_ready.before(n, p + 3))
                if half == 1 and p < 2:
                    act.wait_ge(t2_ready.sem, t2_ready.before(n, p + 1))
                act.activation(osig[:, p % 2, :], pj[3][:, :], ACT.Tanh, scale=0.5).then_inc(osig_ready.sem, 1)

            def chunk_decay(n, p):
                act.wait_ge(G_loaded[p % 2].sem, G_loaded[p % 2].now(n, p // 2 + 1))
                act.wait_ge(qd_ready.sem, qd_ready.now(n, p - 1) if p >= 2 else qd_ready.before(n, p + 3))
                act.wait_ge(s_ready.sem, s_ready.now(n, p - 1) if p >= 2 else s_ready.before(n, p + 3))
                act.activation(E[0:DH, p % 2, :, :], G[0:DH, p % 2, 0, :, :], ACT.Exp)
                act.activation(E[DH:P, p % 2, :, :], G[DH:P, p % 2, 1, :, :], ACT.Exp).then_inc(e_ready.sem, 1)

            def token_decay(n, p):
                act.wait_ge(dmask_ready.sem, dmask_ready.now(n, p + 1))
                act.activation(G[:, p % 2, :, :, :], G[:, p % 2, :, :, :], ACT.Exp).then_inc(d_ready.sem, 1)

            def square(n, p):
                act.wait_ge(o_done.sem, o_done.now(n, p + 1))
                if half == 1 and p == 0:
                    act.wait_ge(xn_step.sem, xn_step.before(n, 3 * CHUNKS + 1))
                act.wait_ge(sqsum_ready.sem, sqsum_ready.now(n, p) if p else sqsum_ready.before(n, PAIRS))
                act.activation(sq[:, :], ot[:, :], ACT.Square).then_inc(sq_ready.sem, 1)

            def out_hi(n, p):
                act.wait_ge(og_ready.sem, og_ready.now(n, p + 1))
                act.wait_ge(y_done.sem, y_done.before(n, CHUNKS))
                act.activation(o_hi[:, p, :], o_gated[:, :], ACT.Copy).then_inc(oh_ready.sem, 1)

            with act.Fori(0, ROUNDS) as n:
                if half == 0:
                    log_decay(n)
                values(n)
                gate_tanh(n, 0); queries(n, 0); out_gate(n, 0)
                chunk_decay(n, 0)
                gate_tanh(n, 1); queries(n, 1); out_gate(n, 1)
                chunk_decay(n, 1)
                token_decay(n, 0)
                gate_tanh(n, 2); queries(n, 2)
                token_decay(n, 1)
                square(n, 0); out_hi(n, 0)
                out_gate(n, 2)
                chunk_decay(n, 2)
                gate_tanh(n, 3); queries(n, 3)
                square(n, 1); out_hi(n, 1)
                token_decay(n, 2)
                chunk_decay(n, 3)
                out_gate(n, 3)
                split_x(n + 1)
                token_decay(n, 3)
                square(n, 2); out_hi(n, 2)
                square(n, 3); out_hi(n, 3)
                if half == 0:
                    for c in range(CHUNKS):
                        act.wait_ge(y_done.sem, y_done.now(n, c + 1))
                        s = y_stored[c % 2]
                        act.wait_ge(s.sem, s.now(n, 1) if c >= 2 else s.before(n, 2))
                        act.activation(y_out[:, c % 2, :], pj[c][:, :], ACT.Copy).then_inc(y_free.sem, 1)

        @block.vector
        def _(dve):
            for c in (xl_ready, zmax_ready, glog_ready, gT_ready, k_ready, gs_ready, kdec_ready, a_ready, s_step,
                      s_ready, og_ready, ol_ready, carried, ssq_read):
                c.credit(dve)
            if half == 1:
                for c in (y_free, rms_ready, t2_ready, st_ready, mv_ready, x1_ready, xn_step, sq_rstd):
                    c.credit(dve)
            if half == 0:
                dve.memset(wd_hi[:, :, :].bitcast(FP32), 0.0).then_inc(pad_made, 1)
                dve.memset(wd_lo[:, :, :].bitcast(FP32), 0.0).then_inc(pad_made, 1)
            dve.memset(S[:, :, :, :], 0.0)
            dve.memset(S_in[:, :, :], 0.0)
            if half == 0:
                dve.wait_ge(wd_hi_made, 1)
                dve.tensor_tensor(wd_lo[:, :, 0:HEADS], wd_raw[:, :, :], split_fp32r(wd_hi[:, :, 0:HEADS]), ALU.subtract).then_inc(wd_lo_made, 1)

            def split_x(n_of_x):
                dve.wait_ge(xh_ready.sem, xh_ready.now(n_of_x, 1))
                dve.tensor_tensor(x_lo[:, :, :], x_raw[:, :, :], split_fp32r(x_hi[:, :, :]), ALU.subtract).then_inc(xl_ready.sem, 1)

            split_x(0)
            for i, name in enumerate(stage_names[:-1]):
                dve.wait_ge(w_hi_made, i + 1)
                for piece, blocks in pieces(name):
                    split = dve.tensor_tensor(W[name][1][:, blocks, :], piece, split_fp32r(W[name][0][:, blocks, :]), ALU.subtract)
                split.then_inc(w_lo_made, 1)
            if half == 1:
                dve.memset(late["top"][:, :], 0.0)
            dve.wait_ge(small_loaded, 48 if half == 0 else 16)
            dve.wait_ge(w_loaded["o"], 16)
            for b in range(PAIRS):
                dve.wait_ge(w_hi_made, 6 + b)
                dve.scalar_tensor_tensor(wo_lo[:, b, :], decays[:, b, :], norm_sb[:, b:b + 1], split_fp32r(wo_hi[:, b, :]),
                                         ALU.mult, ALU.subtract).then_inc(w_lo_made, 1)
            dve.wait_ge(w_lo_made, 5 + PAIRS)

            def log_decay(n):
                dve.wait_ge(z_done.sem, z_done.now(n, 1))
                dve.tensor_scalar(z_m, ot[0:HEADS, :], bd_sb[:, :], 0.0, ALU.add, ALU.max).then_inc(zmax_ready.sem, 1)
                dve.wait_ge(zlog_ready.sem, zlog_ready.now(n, 1))
                dve.wait_ge(zmax_ready.sem, zmax_ready.now(n, 1))
                dve.scalar_tensor_tensor(z_m, z_m, -1.0, z_l, ALU.mult, ALU.subtract).then_inc(glog_ready.sem, 1)
                dve.wait_ge(glog_ready.sem, glog_ready.now(n, 1))
                dve.wait_ge(gT_stored.sem, gT_stored.before(n, 1))
                for c in range(CHUNKS):
                    scan = dve.tensor_tensor_scan(gT[:, c * CH:(c + 1) * CH], ones[0:HEADS, :], z_m[:, c * CH:(c + 1) * CH], 0.0,
                                                  ALU.mult, ALU.add)
                scan.then_inc(gT_ready.sem, 1)

            def keys(n, p):
                dve.wait_ge(k_done.sem, k_done.now(n, p + 1))
                dve.wait_ge(gate_ready.sem, gate_ready.now(n, p + 1))
                dve.wait_ge(sc_done.sem, sc_done.now(n, 2 * (p - 1)) if p >= 2 else sc_done.before(n, 2 * (p + 3)))
                dve.scalar_tensor_tensor(kT[:, p % 2, :], gate[:, :], 1.0, pj[1][:, :], ALU.add, ALU.mult).then_inc(k_ready.sem, 1)

            def token_logs(n):
                dve.wait_ge(gst_done.sem, gst_done.now(n, 1))
                dve.wait_ge(dsub_ready.sem, dsub_ready.before(n, PAIRS))
                dve.tensor_copy(gs[:, :, :].rearrange("p c h -> p (c h)"), ot[:, 0:CHUNKS * HH]).then_inc(gs_ready.sem, 1)

            def key_decay(n, p):
                dve.wait_ge(kt_done.sem, kt_done.now(n, p + 1))
                dve.wait_ge(d_ready.sem, d_ready.now(n, p + 1))
                dve.wait_ge(kv_done.sem, kv_done.now(n, p) if p else kv_done.before(n, PAIRS))
                to_end = G[:, p % 2, :, :, CH - 1].rearrange("p h c -> p c h").unsqueeze(3).broadcast_to((P, CHUNKS, 2, DH))
                dve.tensor_tensor(k_dec[:, :, :, :], kk[:, :, :].rearrange("p c (h d) -> p c h d", h=2), to_end,
                                  ALU.mult).then_inc(kdec_ready.sem, 1)

            def scores(n, p):
                for j in range(2):
                    dve.wait_ge(sc_done.sem, sc_done.now(n, 2 * p + j + 1))
                    if j == 0:
                        dve.wait_ge(o_done.sem, o_done.now(n, p) if p else o_done.before(n, PAIRS))
                    dve.tensor_tensor(A[:, j, :, :], sc[j][:, :, :], G[:, p % 2, j, :, :], ALU.mult).then_inc(a_ready.sem, 1)

            def states(n, p, batch):
                dve.wait_ge(kv_done.sem, kv_done.now(n, p + 1))
                dve.wait_ge(zeroed, batch + 1)
                dve.wait_ge(carried.sem, carried.before(n, p + 1))
                dve.wait_ge(carried.sem, carried.now(n, p - 1) if p >= 2 else carried.before(n, p + 3))
                for c in range(CHUNKS):
                    if c:
                        dve.wait_ge(s_step.sem, s_step.now(n, 2 * (p * CHUNKS + c)))
                    for h in range(2):
                        rows = slice(h * DH, (h + 1) * DH)
                        before = S_in[rows, p, h * DH:(h + 1) * DH] if c == 0 else S[rows, p % 2, c - 1, h * DH:(h + 1) * DH]
                        step = dve.scalar_tensor_tensor(S[rows, p % 2, c, h * DH:(h + 1) * DH], before, E[rows, p % 2, c, CH - 1:CH],
                                                        kk[rows, c, h * DH:(h + 1) * DH], ALU.mult, ALU.add)
                        step.then_inc(s_step.sem, 1)
                dve.wait_ge(s_step.sem, s_step.now(n, 2 * (p + 1) * CHUNKS))
                dve.sem_inc(s_ready.sem, 1)

            def out_gated(n, p):
                dve.wait_ge(sq_ready.sem, sq_ready.now(n, p + 1))
                dve.wait_ge(osig_ready.sem, osig_ready.now(n, p + 1))
                dve.wait_ge(ol_ready.sem, ol_ready.now(n, p) if p else ol_ready.before(n, PAIRS))
                dve.scalar_tensor_tensor(o_gated[:, :], osig[:, p % 2, :], 1.0, ot[:, :], ALU.add, ALU.mult).then_inc(og_ready.sem, 1)
                dve.tensor_copy(S_in[:, p, :], S[:, p % 2, CHUNKS - 1, :]).then_inc(carried.sem, 1)

            def out_lo(n, p):
                dve.wait_ge(oh_ready.sem, oh_ready.now(n, p + 1))
                dve.tensor_tensor(o_lo[:, p, :], o_gated[:, :], split_fp32r(o_hi[:, p, :]), ALU.subtract).then_inc(ol_ready.sem, 1)

            def finish(n):
                dve.tensor_tensor(rms[:, :], ssq[:, bass.ds(n * CHUNKS, CHUNKS)], kk[:, 0, 0:CHUNKS], ALU.add).then_inc(ssq_read.sem, 1)
                dve.wait_ge(ssq_read.sem, ssq_read.now(n, 1))
                dve.tensor_scalar(rms[:, :], rms[:, :], 4.0 / HID, 4.0 * RMS_EPS, ALU.mult, ALU.add).then_inc(rms_ready.sem, 1)
                for c in range(CHUNKS + 3):
                    if c < CHUNKS:
                        dve.wait_ge(y_done.sem, y_done.now(n, c + 1))
                        dve.wait_ge(yf_loaded[c].sem, yf_loaded[c].now(n, 1))
                        dve.tensor_tensor(y_first[c], pj[c][:, :], y_first[c], ALU.add).then_inc(y_free.sem, 1)
                    if 1 <= c <= CHUNKS:
                        b = c - 1
                        dve.wait_ge(y_free.sem, y_free.now(n, b + 1))
                        dve.wait_ge(var_ready.sem, var_ready.now(n, 1))
                        dve.wait_ge(xt_loaded[b].sem, xt_loaded[b].now(n, 1))
                        dve.scalar_tensor_tensor(x_tok[:, b, :], y_first[b], rms[:, b:b + 1], x_tok[:, b, :], ALU.mult, ALU.add).then_inc(t2_ready.sem, 1)
                    if 2 <= c <= CHUNKS + 1:
                        b = c - 2
                        dve.wait_ge(t2_ready.sem, t2_ready.now(n, b + 1))
                        dve.nop(nofuse=True)
                        dve.bn_stats(stats[:, b, :], x_tok[:, b, :]).then_inc(st_ready.sem, 1)
                    if c >= 3:
                        b = c - 3
                        dve.wait_ge(st_ready.sem, st_ready.now(n, b + 1))
                        dve.nop(nofuse=True)
                        dve.bn_aggr(mv[:, b, :], stats[:, b, :]).then_inc(mv_ready.sem, 1)
                dve.wait_ge(var_ready.sem, var_ready.now(n, 3))
                for c in range(CHUNKS):
                    dve.tensor_scalar(x_tok[:, c, :], x_tok[:, c, :], mv[:, c, 0:1], rstd[:, c:c + 1], ALU.subtract, ALU.mult).then_inc(x1_ready.sem, 1)
                dve.tensor_tensor(var2[:, :], mv[:, :, 1], rstd[:, :], ALU.mult).then_inc(sq_rstd.sem, 1)
                dve.wait_ge(sq_rstd.sem, sq_rstd.now(n, 1))
                dve.tensor_tensor(var2[:, :], var2[:, :], rstd[:, :], ALU.mult).then_inc(rms_ready.sem, 1)
                dve.wait_ge(loaded_gb, 32)
                dve.wait_ge(var_ready.sem, var_ready.now(n, 5))
                for c in range(CHUNKS):
                    xn = xn_of[c % 2]
                    if c >= 2:
                        dve.wait_ge(xn_step.sem, xn_step.now(n, 3 * (c - 1)))
                    dve.wait_ge(x1_ready.sem, x1_ready.now(n, c + 1))
                    dve.scalar_tensor_tensor(xn, x_tok[:, c, :], late["rho"][:, bass.ds(n * CHUNKS + c, 1)], g_bc[:, :], ALU.mult, ALU.mult).then_inc(xn_step.sem, 1)
                    dve.wait_ge(xn_step.sem, xn_step.now(n, 3 * c + 1))
                    dve.tensor_tensor(xn, xn, b_bc[:, :], ALU.add).then_inc(xn_step.sem, 1)
                    dve.wait_ge(xn_step.sem, xn_step.now(n, 3 * c + 2))
                    dve.tensor_reduce(top_now[:, c:c + 1], xn, AX.X, ALU.max, apply_absolute_value=True).then_inc(xn_step.sem, 1)
                dve.wait_ge(xn_step.sem, xn_step.now(n, 3 * CHUNKS))
                dve.tensor_tensor(late["top"][:, :], late["top"][:, :], top_now[:, :], ALU.max).then_inc(xn_step.sem, 1)

            with dve.Fori(0, BATCH) as batch:
                dve.wait_ge(carried.sem, carried.before(batch * ROUNDS_PER_BATCH, PAIRS))
                dve.memset(S_in[:, :, :], 0.0).then_inc(zeroed, 1)
                with dve.Fori(0, ROUNDS_PER_BATCH) as r:
                    n = batch * ROUNDS_PER_BATCH + r
                    if half == 0:
                        log_decay(n)
                    keys(n, 0)
                    token_logs(n)
                    keys(n, 1)
                    key_decay(n, 0); scores(n, 0)
                    keys(n, 2)
                    states(n, 0, batch)
                    out_gated(n, 0); out_lo(n, 0)
                    key_decay(n, 1); scores(n, 1)
                    keys(n, 3)
                    states(n, 1, batch)
                    out_gated(n, 1); out_lo(n, 1)
                    key_decay(n, 2); scores(n, 2)
                    states(n, 2, batch)
                    out_gated(n, 2); out_lo(n, 2)
                    key_decay(n, 3); scores(n, 3)
                    states(n, 3, batch)
                    out_gated(n, 3); out_lo(n, 3)
                    split_x(n + 1)
                    dve.wait_ge(ssq_done.sem, ssq_done.now(n, 1))
                    if half == 0:
                        dve.tensor_copy(ssq[:, bass.ds(n * CHUNKS, CHUNKS)], kk[:, 0, 0:CHUNKS]).then_inc(ssq_read.sem, 1)
                    else:
                        finish(n)


        @block.tensor
        def _(pe):
            for c in (z_done, v_done, g_done, k_done, q_done, og_done, gst_done, kt_done, sc_done, kv_done, o_done,
                      y_done, ssq_done):
                c.credit(pe)
            pe.wait_ge(const_made, 5)

            def projection(out, w, cols):
                hi, lo = w
                for t, (a, b) in enumerate(((hi, x_hi), (lo, x_hi), (hi, x_lo))):
                    for k in range(KT):
                        last = pe.matmul(out, a[:, k, cols], b[:, k, :], start=(t + k == 0), stop=(t == 2 and k == KT - 1))
                return last

            def decay_logits(n):
                pe.wait_ge(wd_lo_made, 1)
                pe.wait_ge(sq_ready.sem, sq_ready.before(n, PAIRS))
                pe.wait_ge(og_ready.sem, og_ready.before(n, PAIRS))
                for t, (a, b) in enumerate(((wd_hi, x_hi), (wd_lo, x_hi), (wd_hi, x_lo))):
                    for k in range(KT):
                        last = pe.matmul(ot[:, :], a[:, k, :], b[:, k, :],
                                         start=(t + k == 0), stop=(t == 2 and k == KT - 1))
                last.then_inc(z_done.sem, 1)

            def values(n):
                pe.wait_ge(w_lo_made, 1)
                for c in range(CHUNKS):
                    pe.wait_ge(y_free.sem, y_free.before(n, c + 1))
                    for t, (a, b) in enumerate(((x_hi, 0), (x_hi, 1), (x_lo, 0))):
                        for k in range(KT):
                            last = pe.matmul(pj[c][:, :], a[:, k, c * P:(c + 1) * P], W["v"][b][:, k, :],
                                             start=(t + k == 0), stop=(t == 2 and k == KT - 1))
                    last.then_inc(v_done.sem, 1)

            bank_of = {"g": 0, "k": 1, "q": 2, "og": 3}
            done_of = {"g": g_done, "k": k_done, "q": q_done, "og": og_done}
            read_of = {"g": gate_ready, "k": k_ready, "q": q_ready, "og": osig_ready}

            def project(n, name, p):
                b = bank_of[name]
                pe.wait_ge(w_lo_made, ("v", "g", "k", "q", "og").index(name) + 1)
                if p == 0:
                    pe.wait_ge(v_ready.sem, v_ready.now(n, b + 1))
                else:
                    pe.wait_ge(read_of[name].sem, read_of[name].now(n, p))
                projection(pj[b][:, :], W[name], slice(p * P, (p + 1) * P)).then_inc(done_of[name].sem, 1)

            def token_logs(n):
                if half == 0:
                    pe.wait_ge(gT_ready.sem, gT_ready.now(n, 1))
                    pe.wait_ge(zabs_ready.sem, zabs_ready.now(n, 1))
                else:
                    pe.wait_ge(gT_loaded.sem, gT_loaded.now(n, 1))
                    pe.wait_ge(sq_ready.sem, sq_ready.before(n, PAIRS))
                    pe.wait_ge(og_ready.sem, og_ready.before(n, PAIRS))
                pe.nop(nofuse=True)
                for c in range(CHUNKS):
                    last = pe.transpose(ot[:, c * HH:(c + 1) * HH], gT[0:HH, c * CH:(c + 1) * CH], ident[0:HH, 0:HH])
                last.then_inc(gst_done.sem, 1)

            def scores(n, p):
                pe.wait_ge(k_ready.sem, k_ready.now(n, p + 1))
                pe.wait_ge(s_ready.sem, s_ready.now(n, p) if p else s_ready.before(n, PAIRS))
                if p == 0:
                    pe.wait_ge(ssq_read.sem, ssq_read.before(n, 1))
                for c in range(CHUNKS):
                    last = pe.transpose(kk[:, c, :], kT[:, p % 2, c * CH:(c + 1) * CH], ident[:, :])
                last.then_inc(kt_done.sem, 1)
                pe.wait_ge(q_ready.sem, q_ready.now(n, p + 1))
                pe.wait_ge(a_ready.sem, a_ready.now(n, 2 * p) if p else a_ready.before(n, 2 * PAIRS))
                for c in range(CHUNKS):
                    cols = slice(c * CH, (c + 1) * CH)
                    for h in range(2):
                        rows = slice(h * DH, (h + 1) * DH)
                        last = pe.matmul(sc[h][:, c, :], kT[rows, p % 2, cols], qT[rows, p % 2, cols], start=True, stop=True)
                        if c == CHUNKS - 1:
                            last.then_inc(sc_done.sem, 1)

            def updates(n, p):
                pe.wait_ge(kdec_ready.sem, kdec_ready.now(n, p + 1))
                pe.wait_ge(v_ready.sem, v_ready.now(n, CHUNKS))
                for c in range(CHUNKS):
                    last = pe.matmul(kk[:, c, :], k_dec[:, c, :, :].rearrange("p h d -> p (h d)"), v[:, c, p * P:(p + 1) * P],
                                     start=True, stop=True)
                last.then_inc(kv_done.sem, 1)

            def outputs(n, p):
                if p == 0:
                    pe.wait_ge(gs_ready.sem, gs_ready.now(n, 1))
                else:
                    pe.wait_ge(sq_ready.sem, sq_ready.now(n, p))
                    pe.wait_ge(og_ready.sem, og_ready.now(n, p))
                pe.wait_ge(a_ready.sem, a_ready.now(n, 2 * p + 2))
                for c in range(CHUNKS):
                    for h in range(2):
                        cols = slice(p * P + h * DH, p * P + (h + 1) * DH)
                        pe.matmul(ot[h * DH:(h + 1) * DH, c * CH:(c + 1) * CH], v[:, c, cols], A[:, h, c, :],
                                  start=(c == 0), stop=False, skip_group_check=True)
                pe.wait_ge(s_ready.sem, s_ready.now(n, p + 1))
                pe.wait_ge(qd_ready.sem, qd_ready.now(n, p + 1))
                for c in range(CHUNKS):
                    state = S_in[:, p, :] if c == 0 else S[:, p % 2, c - 1, :]
                    last = pe.matmul(ot[:, c * CH:(c + 1) * CH], state, q_dec[:, c * CH:(c + 1) * CH], start=False,
                                     stop=(c == CHUNKS - 1), skip_group_check=True)
                last.then_inc(o_done.sem, 1)

            def project_out(n, p, chunks=range(CHUNKS)):
                pe.wait_ge(w_lo_made, 5 + PAIRS)
                pe.wait_ge(oh_ready.sem, oh_ready.now(n, p + 1))
                pe.wait_ge(ol_ready.sem, ol_ready.now(n, p + 1))
                if p == 0:
                    for name in ("g", "k", "q", "og"):
                        pe.wait_ge(read_of[name].sem, read_of[name].now(n, PAIRS))
                for c in chunks:
                    cols = slice(c * P, (c + 1) * P)
                    for t, (a, b) in enumerate(((o_hi, wo_hi), (o_hi, wo_lo), (o_lo, wo_hi))):
                        last = pe.matmul(pj[c][:, :], a[:, p, cols], b[:, p, :], start=(p == 0 and t == 0),
                                         stop=(p == PAIRS - 1 and t == 2))
                    if p == PAIRS - 1:
                        last.then_inc(y_done.sem, 1)

            def sum_squares(n):
                pe.wait_ge(sqsum_ready.sem, sqsum_ready.now(n, PAIRS))
                pe.wait_ge(s_ready.sem, s_ready.now(n, PAIRS))
                for c in range(CHUNKS):
                    last = pe.matmul(kk[:, 0, c:c + 1], sq_sum[:, c * P:(c + 1) * P], ones[:, 0:1], start=(c == 0), stop=True,
                                     skip_group_check=True)
                last.then_inc(ssq_done.sem, 1)

            with pe.Fori(0, ROUNDS) as n:
                pe.wait_ge(xl_ready.sem, xl_ready.now(n, 1))
                if half == 0:
                    decay_logits(n)
                values(n)
                for name in ("g", "k", "q", "og"):
                    project(n, name, 0)
                token_logs(n)
                for name in ("g", "k", "q", "og"):
                    project(n, name, 1)
                scores(n, 0)
                for name in ("g", "k", "q"):
                    project(n, name, 2)
                updates(n, 0)
                project(n, "og", 2)
                outputs(n, 0)
                scores(n, 1)
                for name in ("g", "k"):
                    project(n, name, 3)
                updates(n, 1)
                project(n, "q", 3)
                outputs(n, 1)
                scores(n, 2)
                project(n, "og", 3)
                updates(n, 2)
                project_out(n, 0)
                outputs(n, 2)
                scores(n, 3)
                project_out(n, 1, range(0, 3))
                updates(n, 3)
                project_out(n, 1, range(3, CHUNKS))
                project_out(n, 2, range(0, 1))
                outputs(n, 3)
                project_out(n, 2, range(1, CHUNKS))
                sum_squares(n)
                project_out(n, 3)


GAMMA_SETUP = 3
SETUP = 7 + 2 * KT


def quantised_product(nc, part, X, rho, top, x1, w, g_col, b_col, extremes, out):
    LAST = KT - 1
    LOWS = KT - 1 if extremes is None else KT - 3
    NORMS = CHUNKS - 2 if extremes is None else CHUNKS
    with ExitStack() as ctx:
        def sb(name, shape, dt=FP32):
            return ctx.enter_context(nc.sbuf_tensor(f"{name}_{part}", shape, dt))

        def sem(name):
            return nc.alloc_semaphore(f"{name}_{part}")

        def counted(name, per_round, step=1):
            return Count(sem(name), per_round, step)

        wq = sb("wq", [P, KT, DM], FP32R)
        xs = sb("xs", [P, 2, CHUNKS, DM])
        xq = sb("xq", [P, 2, KT, ST])
        w_raw = xq[:, 1, :, :]
        hi, lo = sb("hi", [P, 2, KT, ST], FP32R), sb("lo", [P, 2, KT, ST], FP32R)
        ident, minus_half = sb("ident", [P, P]), sb("minus_half", [P, CHUNKS])
        gcol, bcol = sb("gcol", [P, KT]), sb("bcol", [P, KT])
        beta, gamma = sb("beta", [P, 1]), sb("gamma", [P, 1])
        part_sum, part_top = sb("part_sum", [P, 1]), sb("part_top", [P, 1])
        above, below, g_inv, scale = (sb(x, [P, 1]) for x in ("above", "below", "g_inv", "scale"))
        low = sb("low", [P, DM])
        stats, mv = sb("stats", [P, CHUNKS, 6]), sb("mv", [P, 2, CHUNKS, 2])
        var1, rstd, shift = sb("var1", [P, CHUNKS]), sb("rstd", [P, CHUNKS]), sb("shift", [P, CHUNKS])
        ends_now = sb("ends_now", [P, 2])

        tb = [ctx.enter_context(nc.psum_tensor(f"tb{k}_{part}", [P, ST], FP32)) for k in range(KT)]
        yb = [ctx.enter_context(nc.psum_tensor(f"yb{c}_{part}", [P, DM], FP32)) for c in range(CHUNKS)]

        const_made, loaded, w_loaded = sem("const_made"), sem("loaded"), sem("w_loaded")
        sums_made, reduced, setup = sem("sums_made"), sem("reduced"), sem("setup")
        x_loaded = [sem(f"x_loaded{s}") for s in range(2)]
        xs_ready, t_done = counted("xs_ready", CHUNKS), counted("t_done", KT)
        xn_ready, clipped = counted("xn_ready", KT), counted("clipped", LAST)
        clipped_last = counted("clipped_last", 1)
        hi_ready, lo_ready = counted("hi_ready", KT), counted("lo_ready", LOWS)
        lo_late = counted("lo_late", KT - LOWS)
        y_done, sum_ready = counted("y_done", CHUNKS), counted("sum_ready", CHUNKS)
        st_ready, mv_ready = counted("st_ready", CHUNKS), counted("mv_ready", CHUNKS)
        var_ready, x_ready = counted("var_ready", 4), counted("x_ready", NORMS)
        x_late = counted("x_late", CHUNKS - NORMS)
        ends_ready = counted("ends_ready", 3)
        stored = counted("stored", 1, 16)

        block = ctx.enter_context(nc.Block())

        def tile(n, c):
            return X[:, bass.ds(n * CHUNKS + c, 1), :].rearrange("p a f -> p (a f)")

        def low_of(engine, n, k):
            if k < LOWS:
                engine.wait_ge(lo_ready.sem, lo_ready.now(n, k + 1))
            else:
                engine.wait_ge(lo_late.sem, lo_late.now(n, k - LOWS + 1))

        def tiles(n):
            return X[:, bass.ds(n * CHUNKS, CHUNKS), :]

        @block.sync
        def _(sp):
            stored.credit(sp)
            sp.dma_start(gcol[:, :], g_col).then_inc(loaded, 16)
            sp.dma_start(bcol[:, :], b_col).then_inc(loaded, 16)
            sp.dma_start(w_raw, w.rearrange("(k p) n -> p k n", p=P)).then_inc(w_loaded, 16)
            if x1 is not None:
                for n in range(ROUNDS):
                    if n >= 2:
                        sp.wait_ge(x_loaded[n % 2], 16 * (n // 2))
                    sp.dma_start(X[:, n * CHUNKS:(n + 1) * CHUNKS, :],
                                 x1[n * ST:(n + 1) * ST, :].rearrange("(c p) f -> p c f", p=P)).then_inc(x_loaded[n % 2], 16)
                for s in range(2):
                    sp.wait_ge(x_loaded[s], 16 * (ROUNDS // 2))
                    sp.sem_inc(x_loaded[s], 32)
            if out is not None:
                with sp.Fori(0, ROUNDS) as n:
                    sp.wait_ge(x_ready.sem, x_ready.now(n, NORMS))
                    sp.wait_ge(x_late.sem, x_late.now(n, CHUNKS - NORMS))
                    sp.dma_start(out[bass.ds(n * ST, ST), :].rearrange("(c p) f -> p c f", p=P), tiles(n)).then_inc(stored.sem, 16)
                sp.wait_ge(stored.sem, stored.now(ROUNDS - 1, 1))

        @block.gpsimd
        def _(pool):
            for c in (clipped, var_ready, lo_late):
                c.credit(pool)
            pool.memset(ident[:, :], 0.0).then_inc(const_made, 1)
            pool.memset(minus_half[:, :], -0.5).then_inc(const_made, 1)
            pool.wait_ge(const_made, 2)
            pool.affine_select(out=ident[:, :], in_=ident[:, :], compare_op=ALU.not_equal, fill=1.0, base=0,
                               pattern=[[-1, P]], channel_multiplier=1).then_inc(const_made, 1)
            pool.wait_ge(sums_made, 1)
            pool.partition_all_reduce(gamma[:, :], part_top[:, :], P, REDUCE.max).then_inc(reduced, 1)
            pool.wait_ge(sums_made, 2)
            pool.partition_all_reduce(beta[:, :], part_sum[:, :], P, REDUCE.add).then_inc(reduced, 1)

            def clip(n, s):
                for k in range(LAST):
                    pool.wait_ge(xn_ready.sem, xn_ready.now(n, k + 1))
                    pool.nop(nofuse=True)
                    pool.tensor_scalar(xq[:, s, k, :], xq[:, s, k, :], QB - Q_EPS, -QB + Q_EPS, ALU.min, ALU.max).then_inc(clipped.sem, 1)

            def norm_factors(n, s):
                pool.wait_ge(mv_ready.sem, mv_ready.now(n, CHUNKS))
                pool.wait_ge(x_ready.sem, x_ready.before(n, NORMS))
                if NORMS < CHUNKS:
                    pool.wait_ge(x_late.sem, x_late.before(n, CHUNKS - NORMS))
                pool.nop(nofuse=True)
                pool.tensor_scalar(var1[:, :], mv[:, s, :, 1], 1.0, LN_EPS, ALU.mult, ALU.add).then_inc(var_ready.sem, 1)
                pool.tensor_scalar(shift[:, :], mv[:, s, :, 0], -1.0, 0.0, ALU.mult, ALU.add).then_inc(var_ready.sem, 1)
                pool.wait_ge(var_ready.sem, var_ready.now(n, 2))
                pool.tensor_tensor(rstd[:, :], var1[:, :], minus_half[:, :], ALU.pow).then_inc(var_ready.sem, 1)
                pool.wait_ge(var_ready.sem, var_ready.now(n, 3))
                pool.tensor_tensor(shift[:, :], shift[:, :], rstd[:, :], ALU.mult).then_inc(var_ready.sem, 1)

            def low_parts(n, s):
                for k in range(LOWS, KT):
                    pool.wait_ge(hi_ready.sem, hi_ready.now(n, k + 1))
                    pool.tensor_tensor(lo[:, s, k, :], xq[:, s, k, :], split_fp32r(hi[:, s, k, :]), ALU.subtract).then_inc(lo_late.sem, 1)

            def round_of(n, s):
                if past(n, 1):
                    norm_factors(n - 1, 1 - s)
                low_parts(n + 1, 1 - s)
                clip(n + 2, s)

            clip(0, 0)
            low_parts(0, 0)
            clip(1, 1)
            for n in range(2):
                round_of(n, n)
            with pool.Fori(1, ROUNDS // 2) as i:
                for s in range(2):
                    round_of(i * 2 + s, s)
            norm_factors(ROUNDS - 1, 1)

        @block.scalar
        def _(act):
            for c in (xs_ready, xn_ready, hi_ready, x_ready):
                c.credit(act)

            def scale_tokens(n, s):
                start = n * CHUNKS if type(n) is int else act.snap((n % ROUNDS) * CHUNKS)
                for c in range(CHUNKS):
                    act.activation(xs[:, s, c, :], X[:, bass.ds(start + c, 1), :].rearrange("p a f -> p (a f)"),
                                   ACT.Copy, scale=rho[:, bass.ds(start + c, 1)]).then_inc(xs_ready.sem, 1)

            def normalised(n, s):
                for k in range(KT):
                    act.wait_ge(t_done.sem, t_done.now(n, k + 1))
                    if past(n, 2):
                        low_of(act, n - 2, k)
                    act.activation(xq[:, s, k, :], tb[k][:, :], ACT.Identity, scale=gcol[:, k:k + 1], bias=bcol[:, k:k + 1]).then_inc(xn_ready.sem, 1)

            def high_parts(n, s):
                for k in range(KT):
                    if k < LAST:
                        act.wait_ge(clipped.sem, clipped.now(n, k + 1))
                    else:
                        act.wait_ge(clipped_last.sem, clipped_last.now(n, 1))
                    if k == 0 and past(n, 2):
                        act.wait_ge(y_done.sem, y_done.before(n - 1, CHUNKS))
                    act.activation(hi[:, s, k, :], xq[:, s, k, :], ACT.Copy).then_inc(hi_ready.sem, 1)

            def norm(n):
                act.wait_ge(var_ready.sem, var_ready.now(n, 4))
                for c in range(NORMS):
                    act.activation(tile(n, c), tile(n, c), ACT.Identity, scale=rstd[:, c:c + 1], bias=shift[:, c:c + 1]).then_inc(x_ready.sem, 1)

            def round_of(n, s):
                high_parts(n + 1, 1 - s)
                normalised(n + 2, s)
                if past(n, 1):
                    norm(n - 1)
                if x1 is not None:
                    act.wait_ge(x_loaded[1 - s], (n + s) * 8 + 32)
                act.wait_ge(t_done.sem, t_done.now(n + 1, KT))
                act.wait_ge(x_ready.sem, x_ready.before(n, NORMS))
                if NORMS < CHUNKS and past(n, 1):
                    act.wait_ge(x_late.sem, x_late.before(n - 1, CHUNKS - NORMS))
                scale_tokens(n + 3, 1 - s)

            for n in range(2):
                if x1 is not None:
                    act.wait_ge(x_loaded[n], 16)
                scale_tokens(n, n)
            act.wait_ge(setup, GAMMA_SETUP)
            normalised(0, 0)
            if x1 is not None:
                act.wait_ge(x_loaded[0], 32)
            scale_tokens(2, 0)
            high_parts(0, 0)
            act.wait_ge(setup, SETUP)
            normalised(1, 1)
            for n in range(2):
                round_of(n, n)
            with act.Fori(1, ROUNDS // 2) as i:
                for s in range(2):
                    round_of(i * 2 + s, s)
            norm(ROUNDS - 1)

        @block.vector
        def _(dve):
            for c in (clipped_last, lo_ready, sum_ready, st_ready, mv_ready, *([x_late] if NORMS < CHUNKS else [])):
                c.credit(dve)

            def clip(n, s):
                dve.wait_ge(xn_ready.sem, xn_ready.now(n, KT))
                dve.tensor_scalar(xq[:, s, LAST, :], xq[:, s, LAST, :], QB - Q_EPS, -QB + Q_EPS, ALU.min, ALU.max).then_inc(clipped_last.sem, 1)

            dve.tensor_reduce(part_top[:, :], top[:, :], AX.X, ALU.max).then_inc(sums_made, 1)
            done = 0

            def chained(step):
                nonlocal done
                done += 1
                step.then_inc(setup, 1)
                dve.wait_ge(setup, done)

            dve.wait_ge(reduced, 1)
            chained(dve.reciprocal(g_inv[:, :], gamma[:, :]))
            dve.wait_ge(loaded, 32)
            chained(dve.tensor_scalar(gcol[:, :], gcol[:, :], g_inv[:, :], QB, ALU.mult, ALU.mult))
            chained(dve.tensor_scalar(bcol[:, :], bcol[:, :], g_inv[:, :], QB, ALU.mult, ALU.mult))
            dve.wait_ge(w_loaded, 16)
            dve.tensor_reduce(part_sum[:, :], w_raw.rearrange("p k n -> p (k n)"), AX.X, ALU.add,
                              apply_absolute_value=True).then_inc(sums_made, 1)
            clip(0, 0)
            dve.wait_ge(reduced, 2)
            chained(dve.tensor_scalar(beta[:, :], beta[:, :], 1.0 / (DM * DM), None, ALU.mult))
            chained(dve.tensor_scalar(above[:, :], beta[:, :], Q_EPS, 0.5, ALU.add, ALU.mult))
            chained(dve.tensor_scalar(below[:, :], beta[:, :], Q_EPS, -0.5, ALU.add, ALU.mult))
            for k in range(KT):
                chained(dve.tensor_scalar(low[:, :], w_raw[:, k, :], below[:, :], None, ALU.is_lt))
                chained(dve.scalar_tensor_tensor(wq[:, k, :], w_raw[:, k, :], above[:, :], low[:, :], ALU.is_gt, ALU.subtract))
            chained(dve.scalar_tensor_tensor(scale[:, :], gamma[:, :], 1.0 / QB, beta[:, :], ALU.mult, ALU.mult))
            assert done == SETUP
            if extremes is not None:
                ends_ready.credit(dve)
                chained(dve.memset(extremes[:, :], -3.0e38))

            def low_parts(n, s):
                for k in range(LOWS):
                    dve.wait_ge(hi_ready.sem, hi_ready.now(n, k + 1))
                    dve.tensor_tensor(lo[:, s, k, :], xq[:, s, k, :], split_fp32r(hi[:, s, k, :]), ALU.subtract).then_inc(lo_ready.sem, 1)

            def add(n, s):
                for c in range(CHUNKS + 2):
                    if c == 3:
                        clip(n + 2, s)
                    if c < CHUNKS:
                        dve.wait_ge(y_done.sem, y_done.now(n, c + 1))
                        dve.scalar_tensor_tensor(tile(n, c), yb[c][:, :], scale[:, :], tile(n, c), ALU.mult, ALU.add).then_inc(sum_ready.sem, 1)
                    if 1 <= c <= CHUNKS:
                        dve.wait_ge(sum_ready.sem, sum_ready.now(n, c))
                        dve.nop(nofuse=True)
                        dve.bn_stats(stats[:, c - 1, :], tile(n, c - 1)).then_inc(st_ready.sem, 1)
                    if c >= 2:
                        if c == 2 and past(n, 2):
                            dve.wait_ge(var_ready.sem, var_ready.before(n - 1, 2))
                        dve.wait_ge(st_ready.sem, st_ready.now(n, c - 1))
                        dve.nop(nofuse=True)
                        dve.bn_aggr(mv[:, s, c - 2, :], stats[:, c - 2, :]).then_inc(mv_ready.sem, 1)

            def ends(n):
                dve.wait_ge(x_ready.sem, x_ready.now(n, CHUNKS))
                dve.wait_ge(ends_ready.sem, ends_ready.before(n, 3))
                dve.nop(nofuse=True)
                dve.tensor_reduce(ends_now[:, 0:1], tiles(n), AX.XY, ALU.max).then_inc(ends_ready.sem, 1)
                dve.tensor_reduce(ends_now[:, 1:2], tiles(n), AX.XY, ALU.min, negate=True).then_inc(ends_ready.sem, 1)
                dve.wait_ge(ends_ready.sem, ends_ready.now(n, 2))
                dve.tensor_tensor(extremes[:, :], extremes[:, :], ends_now[:, :], ALU.max).then_inc(ends_ready.sem, 1)

            def norm(n, s):
                dve.wait_ge(var_ready.sem, var_ready.now(n, 4))
                for c in range(NORMS, CHUNKS):
                    dve.tensor_scalar(tile(n, c), tile(n, c), mv[:, s, c, 0:1], rstd[:, c:c + 1], ALU.subtract, ALU.mult).then_inc(x_late.sem, 1)

            def round_of(n, s):
                low_parts(n + 1, 1 - s)
                add(n, s)
                if NORMS < CHUNKS and past(n, 1):
                    norm(n - 1, 1 - s)
                if extremes is not None and past(n, 1):
                    ends(n - 1)

            low_parts(0, 0)
            clip(1, 1)
            for n in range(2):
                round_of(n, n)
            with dve.Fori(1, ROUNDS // 2) as i:
                for s in range(2):
                    round_of(i * 2 + s, s)
            if NORMS < CHUNKS:
                norm(ROUNDS - 1, 1)
            if extremes is not None:
                ends(ROUNDS - 1)

        @block.tensor
        def _(pe):
            t_done.credit(pe)
            y_done.credit(pe)
            pe.wait_ge(const_made, 3)

            def transposes(n, s):
                pe.wait_ge(xs_ready.sem, xs_ready.now(n, CHUNKS))
                for k in range(KT):
                    pe.wait_ge(xn_ready.sem, xn_ready.before(n, k + 1))
                    for c in range(CHUNKS):
                        last = pe.transpose(tb[k][:, c * P:(c + 1) * P], xs[:, s, c, k * P:(k + 1) * P], ident[:, :])
                    last.then_inc(t_done.sem, 1)

            transposes(0, 0)
            transposes(1, 1)
            pe.wait_ge(setup, SETUP)
            with pe.Fori(0, ROUNDS // 2) as i:
                for s in range(2):
                    n = i * 2 + s
                    transposes(n + 2, s)
                    for c in range(CHUNKS):
                        pe.wait_ge(sum_ready.sem, sum_ready.before(n, c + 1))
                        for k in range(KT):
                            if c == 0:
                                low_of(pe, n, k)
                            for part_of in (hi, lo):
                                last = pe.matmul(yb[c][:, :], part_of[:, s, k, c * P:(c + 1) * P], wq[:, k, :],
                                                 start=(k == 0 and part_of is hi), stop=(k == KT - 1 and part_of is lo))
                        last.then_inc(y_done.sem, 1)


LATENT, CHECKS = 24, 12
SCALES = (2, 4, 8, 16, 32)
LOG_SCALES = [float(x) for x in np.log(np.array(SCALES, np.float32))]
SUM_LX = float(np.sum(np.array(LOG_SCALES, np.float32)))
DEN = float(np.float32(5.0 * np.sum(np.array(LOG_SCALES) ** 2) - np.sum(LOG_SCALES) ** 2))


def wave_filter(nc, X, extremes, basis, freq, w_el, C, M):
    with ExitStack() as ctx:
        def sb(name, shape, dt=FP32):
            return ctx.enter_context(nc.sbuf_tensor(f"{name}_filter", shape, dt))

        def sem(name):
            return nc.alloc_semaphore(f"{name}_filter")

        n_seq = SCALES[-1] ** 2
        seq, above = sb("seq", [1, n_seq]), sb("above", [1, n_seq])
        ends, span, inv = sb("ends", [P, 2]), sb("span", [P, 1]), sb("inv", [P, 1])
        total, mean, count = (sb(x, [1, len(SCALES)]) for x in ("total", "mean", "count"))
        logs, num, lx = sb("logs", [1, len(SCALES)]), sb("num", [1, 4]), sb("lx", [1, len(SCALES)])
        D = sb("D", [P, 1])
        dim1 = sb("dim1", [1, 1])
        omega, a_par, b_par, omega_d = (sb(x, [P, 1]) for x in ("omega", "a_par", "b_par", "omega_d"))
        ka, arg, phase, f = (sb(x, [P, KT]) for x in ("ka", "arg", "phase", "f"))
        B, Bf, Cf = sb("B", [P, KT, DM]), sb("Bf", [P, KT, DM]), sb("Cf", [P, KT, DM])
        wel = sb("wel", [P, KT, LATENT])
        Mf = sb("Mf", [P, KT, LATENT])
        cb = [ctx.enter_context(nc.psum_tensor(f"cb{m}_filter", [P, DM], FP32)) for m in range(KT)]
        mb = ctx.enter_context(nc.psum_tensor("mb_filter", [P, KT, LATENT], FP32))
        seq_loaded = sem("seq_loaded")
        loaded, reduced, step, logged, spread, sined = (sem(x) for x in ("loaded", "reduced", "step", "logged", "spread", "sined"))
        c_done, c_read, m_done, hi_made = sem("c_done"), sem("c_read"), sem("m_done"), sem("hi_made")
        n_step = {}
        block = ctx.enter_context(nc.Block())

        @block.sync
        def _(sp):
            for token in range(n_seq // DM):
                sp.dma_start(seq[0:1, token * DM:(token + 1) * DM], X[token:token + 1, 0, :]).then_inc(seq_loaded, 16)
            sp.dma_start(ka[:, :], freq).then_inc(loaded, 16)
            sp.dma_start(B[:, :, :], basis.rearrange("(k p) n -> p k n", p=P)).then_inc(loaded, 16)
            sp.dma_start(wel[:, :, :], w_el.rearrange("(k p) n -> p k n", p=P)).then_inc(loaded, 16)

        @block.vector
        def _(dve):
            done = 0

            def chained(ins, name=None):
                nonlocal done
                done += 1
                ins.then_inc(step, 1)
                dve.wait_ge(step, done)
                if name:
                    n_step[name] = done

            for j, value in enumerate(LOG_SCALES):
                chained(dve.memset(lx[:, j:j + 1], value))
            for part in M:
                chained(dve.memset(part[:, :, :].bitcast(FP32), 0.0))
            dve.wait_ge(seq_loaded, 16 * (n_seq // DM))
            dve.wait_ge(reduced, 1)
            chained(dve.tensor_tensor(span[:, :], ends[:, 0:1], ends[:, 1:2], ALU.add))
            chained(dve.tensor_scalar(span[:, :], span[:, :], 1e-10, None, ALU.add))
            chained(dve.reciprocal(inv[:, :], span[:, :]))
            chained(dve.tensor_scalar(seq[:, :], seq[:, :], ends[0:1, 1:2], inv[0:1, :], ALU.add, ALU.mult))
            for j, size in enumerate(SCALES):
                m = size * size
                chained(dve.tensor_reduce(total[:, j:j + 1], seq[:, 0:m], AX.X, ALU.add))
                chained(dve.tensor_scalar(mean[:, j:j + 1], total[:, j:j + 1], 1.0 / m, None, ALU.mult))
                chained(dve.tensor_scalar(above[:, 0:m], seq[:, 0:m], mean[:, j:j + 1], None, ALU.is_gt))
                chained(dve.tensor_reduce(count[:, j:j + 1], above[:, 0:m], AX.X, ALU.add))
            chained(dve.tensor_scalar(count[:, :], count[:, :], 1.0, None, ALU.max), "counts")
            dve.wait_ge(logged, 1)
            chained(dve.tensor_tensor(lx[:, :], lx[:, :], logs[:, :], ALU.mult))
            chained(dve.tensor_reduce(num[:, 0:1], lx[:, :], AX.X, ALU.add))
            chained(dve.tensor_reduce(num[:, 1:2], logs[:, :], AX.X, ALU.add))
            chained(dve.tensor_scalar(num[:, 2:3], num[:, 0:1], -float(len(SCALES)) / DEN, None, ALU.mult))
            chained(dve.scalar_tensor_tensor(num[:, 3:4], num[:, 1:2], SUM_LX / DEN, num[:, 2:3], ALU.mult, ALU.add))
            chained(dve.tensor_scalar(dim1[:, :], num[:, 3:4], 1.0, 2.0, ALU.max, ALU.min), "dimension")
            dve.wait_ge(spread, 1)
            chained(dve.tensor_scalar(omega[:, :], D[:, :], 0.2, 1.0, ALU.mult, ALU.add))
            dve.wait_ge(loaded, 48)
            chained(dve.tensor_scalar(a_par[:, :], D[:, :], 0.5, 1.0, ALU.mult, ALU.add))
            chained(dve.tensor_scalar(b_par[:, :], D[:, :], 0.1, None, ALU.mult))
            chained(dve.tensor_tensor(omega_d[:, :], omega[:, :], D[:, :], ALU.mult))
            chained(dve.tensor_scalar(arg[:, :], ka[:, :], a_par[:, :], omega_d[:, :], ALU.mult, ALU.add))
            chained(dve.tensor_scalar(arg[:, :], arg[:, :], -1.0, float(np.pi), ALU.mult, ALU.add))
            chained(dve.tensor_tensor(phase[:, :], ka[:, :], ka[:, :], ALU.mult))
            chained(dve.scalar_tensor_tensor(phase[:, :], phase[:, :], b_par[:, :], ka[:, :], ALU.mult, ALU.subtract))
            chained(dve.tensor_scalar(phase[:, :], phase[:, :], omega_d[:, :], None, ALU.add))
            chained(dve.tensor_scalar(phase[:, :], phase[:, :], -1.0, float(np.pi / 2), ALU.mult, ALU.add), "angles")
            dve.wait_ge(sined, 2)
            chained(dve.tensor_tensor(f[:, :], arg[:, :], phase[:, :], ALU.mult))
            chained(dve.tensor_tensor(Bf[:, :, :], B[:, :, :], f[:, :].unsqueeze(2).broadcast_to((P, KT, DM)), ALU.mult), "scaled")
            for m in range(KT):
                dve.wait_ge(c_done, m + 1)
                dve.tensor_copy(Cf[:, m, :], cb[m][:, :]).then_inc(c_read, 1)
                if m:
                    dve.wait_ge(hi_made, m)
                    dve.tensor_tensor(C[1][:, m - 1, :], Cf[:, m - 1, :], split_fp32r(C[0][:, m - 1, :]), ALU.subtract)
            dve.wait_ge(m_done, 1)
            dve.tensor_copy(Mf[:, :, :], mb[:, :, :]).then_inc(c_read, 1)
            dve.wait_ge(hi_made, KT)
            dve.tensor_tensor(C[1][:, KT - 1, :], Cf[:, KT - 1, :], split_fp32r(C[0][:, KT - 1, :]), ALU.subtract)
            dve.wait_ge(hi_made, KT + 1)
            dve.tensor_tensor(M[1][:, :, 0:LATENT], Mf[:, :, :], split_fp32r(M[0][:, :, 0:LATENT]), ALU.subtract)

        @block.gpsimd
        def _(pool):
            pool.partition_all_reduce(ends[:, :], extremes[:, :], P, REDUCE.max).then_inc(reduced, 1)
            pool.wait_ge(step, n_step["dimension"])
            pool.partition_broadcast(D[:, :], dim1[:, :]).then_inc(spread, 1)

        @block.scalar
        def _(act):
            act.wait_ge(step, n_step["counts"])
            act.activation(logs[:, :], count[:, :], ACT.Ln).then_inc(logged, 1)
            act.wait_ge(step, n_step["angles"])
            act.activation(arg[:, :], arg[:, :], ACT.Sin).then_inc(sined, 1)
            act.activation(phase[:, :], phase[:, :], ACT.Sin).then_inc(sined, 1)
            for m in range(KT):
                act.wait_ge(c_read, m + 1)
                act.activation(C[0][:, m, :], Cf[:, m, :], ACT.Copy).then_inc(hi_made, 1)
            act.wait_ge(c_read, KT + 1)
            act.activation(M[0][:, :, 0:LATENT], Mf[:, :, :], ACT.Copy).then_inc(hi_made, 1)

        @block.tensor
        def _(pe):
            pe.wait_ge(step, n_step["scaled"])
            for m in range(KT):
                for k in range(KT):
                    last = pe.matmul(cb[m][:, :], Bf[:, k, m * P:(m + 1) * P], B[:, k, :], start=(k == 0), stop=(k == KT - 1))
                last.then_inc(c_done, 1)
            pe.wait_ge(c_read, KT)
            for m in range(KT):
                for k in range(KT):
                    last = pe.matmul(mb[:, m, :], Cf[:, k, m * P:(m + 1) * P], wel[:, k, :], start=(k == 0), stop=(k == KT - 1),
                                     skip_group_check=True)
            last.then_inc(m_done, 1)


def mix(nc, X, rho, top, C, M, checks, b_el, w_le, b_le, gamma_w, beta_w):
    with ExitStack() as ctx:
        def sb(name, shape, dt=FP32):
            return ctx.enter_context(nc.sbuf_tensor(f"{name}_mix", shape, dt))

        def sem(name):
            return nc.alloc_semaphore(f"{name}_mix")

        def counted(name, per_round, step=1):
            return Count(sem(name), per_round, step)

        L = LATENT
        BF16 = mybir.dt.bfloat16
        hi, lo = sb("hi", [P, 2, KT, ST], FP32R), sb("lo", [P, 2, KT, ST], FP32R)
        ident, minus_half = sb("ident", [P, P]), sb("minus_half", [P, CHUNKS])
        xs = sb("xs", [P, CHUNKS, DM])
        le_hi, le_lo = sb("le_hi", [L + 1, DM], FP32R), sb("le_lo", [L + 1, DM], FP32R)
        code = sb("code", [L + 1, ST], FP32R)
        bits, syn, fix = (sb(x, [L, ST], BF16) for x in ("bits", "syn", "fix"))
        parity_f, first_f = sb("parity_f", [L, L]), sb("first_f", [L, L])
        parity, first = sb("parity", [L, L], BF16), sb("first", [L, L], BF16)
        bel = sb("bel", [L, 1])
        g_bc, b_bc = sb("g_bc", [P, DM]), sb("b_bc", [P, DM])
        xn = sb("xn", [P, 2, DM])
        le = xn[0:L + 1, 0, :]
        stats, mv = sb("stats", [P, CHUNKS, 6]), sb("mv", [P, 2, CHUNKS, 2])
        var1, rstd, var2, shift = (sb(x, [P, CHUNKS]) for x in ("var1", "rstd", "var2", "shift"))
        top_now = sb("top_now", [P, CHUNKS])

        tb = [ctx.enter_context(nc.psum_tensor(f"tb{k}_mix", [P, ST], FP32)) for k in range(2)]
        yb = [ctx.enter_context(nc.psum_tensor(f"yb{c}_mix", [P, DM], FP32)) for c in range(CHUNKS)]
        lat = ctx.enter_context(nc.psum_tensor("lat_mix", [P, ST], FP32))
        chk = ctx.enter_context(nc.psum_tensor("chk_mix", [L, ST], FP32))

        const_made, loaded, prepared = sem("const_made"), sem("loaded"), sem("prepared")
        t_done, xs_loaded = counted("t_done", KT), counted("xs_loaded", 1, 16)
        hi_ready, lo_ready = counted("hi_ready", KT), counted("lo_ready", KT)
        lat_done, syn_done, weight_done = counted("lat_done", 1), counted("syn_done", 1), counted("weight_done", 1)
        bits_ready, syn_ready = counted("bits_ready", 1), counted("syn_ready", 1)
        fix_ready, code_ready = counted("fix_ready", 1), counted("code_ready", 1)
        y_done, sum_ready = counted("y_done", CHUNKS), counted("sum_ready", CHUNKS)
        st_ready, mv_ready = counted("st_ready", CHUNKS), counted("mv_ready", CHUNKS)
        var_ready, x_ready = counted("var_ready", 8), counted("x_ready", CHUNKS)
        xn_ready, xb_ready = counted("xn_ready", CHUNKS), counted("xb_ready", CHUNKS)
        top_ready = counted("top_ready", CHUNKS + 1)
        block = ctx.enter_context(nc.Block())

        def tile(t):
            return X[:, bass.ds(t, 1), :].rearrange("p a f -> p (a f)")

        @block.sync
        def _(sp):
            xs_loaded.credit(sp)
            sp.dma_start(xs[:, :, :], X[:, 0:CHUNKS, :]).then_inc(xs_loaded.sem, 16)
            sp.dma_start(xn[0:L, 0, :], w_le).then_inc(loaded, 16)
            sp.dma_start(xn[L:L + 1, 0, :], b_le.rearrange("(a n) -> a n", a=1)).then_inc(loaded, 16)
            sp.dma_start(parity_f[:, :], checks[0]).then_inc(loaded, 16)
            sp.dma_start(first_f[:, :], checks[1]).then_inc(loaded, 16)
            sp.dma_start(bel[:, :], b_el.rearrange("(h a) -> h a", a=1)).then_inc(loaded, 16)
            sp.dma_start(g_bc[:, :], gamma_w.rearrange("(a n) -> a n", a=1).broadcast_to((P, DM))).then_inc(loaded, 16)
            sp.dma_start(b_bc[:, :], beta_w.rearrange("(a n) -> a n", a=1).broadcast_to((P, DM))).then_inc(loaded, 16)
            with sp.Fori(0, ROUNDS) as n:
                tile_next = sp.snap(((n + 1) % ROUNDS) * CHUNKS)
                sp.wait_ge(t_done.sem, t_done.now(n, KT))
                sp.dma_start(xs[:, :, :], X[:, bass.ds(tile_next, CHUNKS), :]).then_inc(xs_loaded.sem, 16)
            sp.wait_ge(t_done.sem, t_done.now(ROUNDS, KT))
            sp.dma_start(xs[:, :, :], X[:, CHUNKS:2 * CHUNKS, :]).then_inc(xs_loaded.sem, 16)
            sp.wait_ge(xs_loaded.sem, xs_loaded.now(ROUNDS + 1, 1))

        @block.gpsimd
        def _(pool):
            var_ready.credit(pool)
            xb_ready.credit(pool)
            pool.memset(ident[:, :], 0.0).then_inc(const_made, 1)
            pool.memset(minus_half[:, :], -0.5).then_inc(const_made, 1)
            pool.wait_ge(const_made, 2)
            pool.affine_select(out=ident[:, :], in_=ident[:, :], compare_op=ALU.not_equal, fill=1.0, base=0,
                               pattern=[[-1, P]], channel_multiplier=1).then_inc(const_made, 1)
            pool.wait_ge(const_made, 3)

            def norm_factors(n, s):
                pool.wait_ge(mv_ready.sem, mv_ready.now(n, CHUNKS))
                pool.wait_ge(x_ready.sem, x_ready.before(n, CHUNKS))
                pool.nop(nofuse=True)
                pool.tensor_scalar(var1[:, :], mv[:, s, :, 1], 1.0, LN_EPS, ALU.mult, ALU.add).then_inc(var_ready.sem, 1)
                pool.tensor_scalar(shift[:, :], mv[:, s, :, 0], -1.0, 0.0, ALU.mult, ALU.add).then_inc(var_ready.sem, 1)
                pool.wait_ge(var_ready.sem, var_ready.now(n, 2))
                pool.tensor_tensor(rstd[:, :], var1[:, :], minus_half[:, :], ALU.pow).then_inc(var_ready.sem, 1)
                pool.wait_ge(var_ready.sem, var_ready.now(n, 3))
                pool.tensor_tensor(shift[:, :], shift[:, :], rstd[:, :], ALU.mult).then_inc(var_ready.sem, 1)
                pool.tensor_tensor(var2[:, :], mv[:, s, :, 1], rstd[:, :], ALU.mult).then_inc(var_ready.sem, 1)
                pool.wait_ge(var_ready.sem, var_ready.now(n, 5))
                pool.tensor_tensor(var2[:, :], var2[:, :], rstd[:, :], ALU.mult).then_inc(var_ready.sem, 1)
                pool.wait_ge(var_ready.sem, var_ready.now(n, 6))
                pool.nop(nofuse=True)
                pool.tensor_scalar(var2[:, :], var2[:, :], 1.0, FFN_LN_EPS, ALU.mult, ALU.add).then_inc(var_ready.sem, 1)
                pool.wait_ge(var_ready.sem, var_ready.now(n, 7))
                pool.tensor_tensor(rho[:, bass.ds(n * CHUNKS, CHUNKS)], var2[:, :], minus_half[:, :], ALU.pow).then_inc(var_ready.sem, 1)

            def tail(n, s):
                norm_factors(n, s)
                for c in range(CHUNKS):
                    pool.wait_ge(xn_ready.sem, xn_ready.now(n, c + 1))
                    pool.tensor_tensor(xn[:, c % 2, :], xn[:, c % 2, :], b_bc[:, :], ALU.add).then_inc(xb_ready.sem, 1)

            with pool.Fori(0, ROUNDS // 2) as i:
                for s in range(2):
                    tail(i * 2 + s, s)

        @block.scalar
        def _(act):
            hi_ready.credit(act)
            x_ready.credit(act)
            act.wait_ge(loaded, 112)
            act.activation(le_hi[:, :], le, ACT.Copy).then_inc(prepared, 1)

            def high_parts(n, slot, blocks):
                for k in blocks:
                    act.wait_ge(t_done.sem, t_done.now(n, k + 1))
                    act.activation(hi[:, slot, k, :], tb[k % 2][:, :], ACT.Copy).then_inc(hi_ready.sem, 1)

            def norm(n):
                act.wait_ge(var_ready.sem, var_ready.now(n, 4))
                for c in range(CHUNKS):
                    act.activation(tile(n * CHUNKS + c), tile(n * CHUNKS + c), ACT.Identity, scale=rstd[:, c:c + 1],
                                   bias=shift[:, c:c + 1]).then_inc(x_ready.sem, 1)

            def round_of(n, s):
                high_parts(n + 1, 1 - s, (2, 3))
                if past(n, 1):
                    norm(n - 1)
                act.wait_ge(y_done.sem, y_done.now(n, CHUNKS))
                high_parts(n + 2, s, (0, 1))

            high_parts(0, 0, range(KT))
            high_parts(1, 1, (0, 1))
            for n in range(2):
                round_of(n, n)
            with act.Fori(1, ROUNDS // 2) as i:
                for s in range(2):
                    round_of(i * 2 + s, s)
            norm(ROUNDS - 1)

        @block.vector
        def _(dve):
            for c in (lo_ready, bits_ready, syn_ready, fix_ready, code_ready, sum_ready, st_ready, mv_ready,
                      xn_ready, top_ready):
                c.credit(dve)
            dve.memset(top[:, :], 0.0)
            dve.memset(code[:, :].bitcast(FP32), 1.0)
            dve.wait_ge(loaded, 112)
            dve.tensor_copy(parity[:, :], parity_f[:, :])
            dve.tensor_copy(first[:, :], first_f[:, :]).then_inc(prepared, 1)
            dve.wait_ge(prepared, 2)
            dve.tensor_tensor(le_lo[:, :], le, split_fp32r(le_hi[:, :]), ALU.subtract).then_inc(prepared, 1)

            def low_parts(n, slot, blocks):
                for k in blocks:
                    dve.wait_ge(hi_ready.sem, hi_ready.now(n, k + 1))
                    dve.tensor_tensor(lo[:, slot, k, :], tb[k % 2][:, :], split_fp32r(hi[:, slot, k, :]), ALU.subtract).then_inc(lo_ready.sem, 1)

            def bits_of(n):
                dve.wait_ge(lat_done.sem, lat_done.now(n, 1))
                dve.tensor_scalar(bits[:, :], lat[0:L, :], bel[:, :], 0.0, ALU.add, ALU.is_gt).then_inc(bits_ready.sem, 1)

            def syndrome(n):
                dve.wait_ge(syn_done.sem, syn_done.now(n, 1))
                dve.tensor_scalar(syn[:, :], chk[:, :], 0.5, None, ALU.is_gt).then_inc(syn_ready.sem, 1)

            def correct(n):
                dve.wait_ge(weight_done.sem, weight_done.now(n, 1))
                dve.wait_ge(syn_ready.sem, syn_ready.now(n, 1))
                dve.scalar_tensor_tensor(fix[:, :], chk[:, :], 3.5, syn[:, :], ALU.is_lt, ALU.mult).then_inc(fix_ready.sem, 1)
                if past(n, 1):
                    dve.wait_ge(y_done.sem, y_done.before(n, CHUNKS))
                dve.wait_ge(fix_ready.sem, fix_ready.now(n, 1))
                dve.tensor_tensor(code[0:L, :], bits[:, :], fix[:, :], ALU.not_equal).then_inc(code_ready.sem, 1)

            def add(n, c):
                dve.wait_ge(y_done.sem, y_done.now(n, c + 1))
                dve.tensor_tensor(tile(n * CHUNKS + c), yb[c][:, :], tile(n * CHUNKS + c), ALU.add).then_inc(sum_ready.sem, 1)

            def moments(n, s, c):
                dve.wait_ge(sum_ready.sem, sum_ready.now(n, c + 1))
                dve.nop(nofuse=True)
                dve.bn_stats(stats[:, c, :], tile(n * CHUNKS + c)).then_inc(st_ready.sem, 1)
                if c == 0 and past(n, 2):
                    dve.wait_ge(var_ready.sem, var_ready.before(n - 1, 5))
                dve.wait_ge(st_ready.sem, st_ready.now(n, c + 1))
                dve.nop(nofuse=True)
                dve.bn_aggr(mv[:, s, c, :], stats[:, c, :]).then_inc(mv_ready.sem, 1)

            def normalised(n, c):
                if c == 0:
                    dve.wait_ge(var_ready.sem, var_ready.now(n, 8))
                if c < 2:
                    dve.wait_ge(top_ready.sem, top_ready.before(n, c + 3))
                else:
                    dve.wait_ge(top_ready.sem, top_ready.now(n, c - 1))
                dve.wait_ge(x_ready.sem, x_ready.now(n, c + 1))
                dve.scalar_tensor_tensor(xn[:, c % 2, :], tile(n * CHUNKS + c), rho[:, bass.ds(n * CHUNKS + c, 1)], g_bc[:, :],
                                         ALU.mult, ALU.mult).then_inc(xn_ready.sem, 1)

            def top_of(n, c):
                dve.wait_ge(xb_ready.sem, xb_ready.now(n, c + 1))
                if c == 0:
                    dve.wait_ge(top_ready.sem, top_ready.before(n, CHUNKS + 1))
                dve.tensor_reduce(top_now[:, c:c + 1], xn[:, c % 2, :], AX.X, ALU.max, apply_absolute_value=True).then_inc(top_ready.sem, 1)

            def top_so_far(n):
                dve.wait_ge(top_ready.sem, top_ready.now(n, CHUNKS))
                dve.tensor_tensor(top[:, :], top[:, :], top_now[:, :], ALU.max).then_inc(top_ready.sem, 1)

            def round_of(n, s):
                tail = past(n, 1)
                if tail:
                    moments(n - 1, 1 - s, 3)
                add(n, 0)
                low_parts(n + 1, 1 - s, (2, 3))
                moments(n, s, 0)
                add(n, 1)
                if tail:
                    normalised(n - 1, 0)
                    normalised(n - 1, 1)
                moments(n, s, 1)
                bits_of(n + 1)
                if tail:
                    top_of(n - 1, 0)
                    normalised(n - 1, 2)
                add(n, 2)
                syndrome(n + 1)
                moments(n, s, 2)
                if tail:
                    top_of(n - 1, 1)
                    normalised(n - 1, 3)
                    top_of(n - 1, 2)
                add(n, 3)
                correct(n + 1)
                low_parts(n + 2, s, (0, 1))
                if tail:
                    top_of(n - 1, 3)
                    top_so_far(n - 1)

            low_parts(0, 0, range(KT))
            bits_of(0)
            syndrome(0)
            correct(0)
            low_parts(1, 1, (0, 1))
            for n in range(2):
                round_of(n, n)
            with dve.Fori(1, ROUNDS // 2) as i:
                for s in range(2):
                    round_of(i * 2 + s, s)
            n = ROUNDS - 1
            moments(n, 1, 3)
            normalised(n, 0)
            normalised(n, 1)
            for c in range(CHUNKS):
                top_of(n, c)
                if c + 2 < CHUNKS:
                    normalised(n, c + 2)
            top_so_far(n)

        @block.tensor
        def _(pe):
            for c in (t_done, lat_done, syn_done, weight_done, y_done):
                c.credit(pe)
            pe.wait_ge(const_made, 3)

            def transposes(n, blocks):
                if 0 in blocks:
                    pe.wait_ge(xs_loaded.sem, xs_loaded.now(n, 1))
                for k in blocks:
                    pe.wait_ge(lo_ready.sem, lo_ready.now(n, k - 1) if k >= 2 else lo_ready.before(n, k + 3))
                    for c in range(CHUNKS):
                        last = pe.transpose(tb[k % 2][:, c * P:(c + 1) * P], xs[:, c, k * P:(k + 1) * P], ident[:, :])
                    last.then_inc(t_done.sem, 1)

            def latent(n, s):
                pe.wait_ge(lo_ready.sem, lo_ready.now(n, KT))
                pe.wait_ge(bits_ready.sem, bits_ready.before(n, 1))
                for t, (a, b) in enumerate(((M[0], hi), (M[1], hi), (M[0], lo))):
                    for k in range(KT):
                        last = pe.matmul(lat[:, :], a[:, k, :], b[:, s, k, :], start=(t + k == 0), stop=(t == 2 and k == KT - 1))
                last.then_inc(lat_done.sem, 1)

            def checks_of(n):
                pe.wait_ge(bits_ready.sem, bits_ready.now(n, 1))
                pe.wait_ge(fix_ready.sem, fix_ready.before(n, 1))
                pe.nop(nofuse=True)
                pe.matmul(chk[:, :], parity[:, :], bits[:, :], start=True, stop=True).then_inc(syn_done.sem, 1)

            def weights_of(n):
                pe.wait_ge(syn_ready.sem, syn_ready.now(n, 1))
                pe.nop(nofuse=True)
                pe.matmul(chk[:, :], first[:, :], syn[:, :], start=True, stop=True).then_inc(weight_done.sem, 1)

            def mixed(n, s, c):
                pe.wait_ge(sum_ready.sem, sum_ready.before(n, c + 1))
                for t, (a, b) in enumerate(((hi, C[0]), (hi, C[1]), (lo, C[0]))):
                    for k in range(KT):
                        pe.matmul(yb[c][:, :], a[:, s, k, c * P:(c + 1) * P], b[:, k, :], start=(t + k == 0), stop=False)
                if c == 0:
                    pe.wait_ge(code_ready.sem, code_ready.now(n, 1))
                    pe.nop(nofuse=True)
                for part in (le_hi, le_lo):
                    last = pe.matmul(yb[c][:, :], code[:, c * P:(c + 1) * P], part[:, :], start=False, stop=(part is le_lo))
                last.then_inc(y_done.sem, 1)

            transposes(0, range(KT))
            pe.wait_ge(prepared, 3)
            latent(0, 0)
            checks_of(0)
            transposes(1, (0, 1))
            weights_of(0)
            with pe.Fori(0, ROUNDS // 2) as i:
                for s in range(2):
                    n = i * 2 + s
                    mixed(n, s, 0)
                    transposes(n + 1, (2, 3))
                    mixed(n, s, 1)
                    latent(n + 1, 1 - s)
                    mixed(n, s, 2)
                    checks_of(n + 1)
                    transposes(n + 2, (0, 1))
                    mixed(n, s, 3)
                    weights_of(n + 1)


def program(nc, x, x_t, wv_t, wg_t, wk_t, wq_t, wog_t, wo_t, wd_t, bd, norm_w, ln_gamma0, ln_beta0, gcol0, bcol0, w0,
            basis, freq, w_el, b_el, parity, first, w_le, b_le, ln_gamma1, ln_beta1, gcol1, bcol1, w1, out):
    g_dram = nc.dram_tensor("log_decay_dram", [HEADS, TOKENS], FP32, kind="Internal").ap()
    y_dram = nc.dram_tensor("y_first_dram", [TOKENS, DM], FP32, kind="Internal").ap()
    x1_dram = nc.dram_tensor("x1_dram", [TOKENS, DM], FP32, kind="Internal").ap()
    wT = {"v": wv_t, "g": wg_t, "k": wk_t, "q": wq_t, "og": wog_t}
    with nc.sbuf_tensor("rho", [P, TILES], FP32) as rho, nc.sbuf_tensor("top", [P, CHUNKS], FP32) as top:
        with nc.sbuf_tensor("ssq", [P, TILES], FP32) as ssq:
            late = {"x": x, "x1": x1_dram, "ln_gamma": ln_gamma0, "ln_beta": ln_beta0, "rho": rho, "top": top}
            for half in range(HALVES):
                with nc.cleanup_on_exit():
                    attention_half(nc, half, x_t, wT, wo_t, wd_t, bd, norm_w, g_dram, y_dram, ssq, late)
        with nc.sbuf_tensor("X", [P, TILES, DM], FP32) as X, nc.sbuf_tensor("extremes", [P, 2], FP32) as extremes:
            with nc.cleanup_on_exit():
                quantised_product(nc, "first", X, rho, top, x1_dram, w0, gcol0, bcol0, extremes, None)
            with ExitStack() as ctx:
                C = [ctx.enter_context(nc.sbuf_tensor(f"C_{part}", [P, KT, DM], FP32R)) for part in ("hi", "lo")]
                M = [ctx.enter_context(nc.sbuf_tensor(f"M_{part}", [P, KT, P], FP32R)) for part in ("hi", "lo")]
                with nc.cleanup_on_exit():
                    wave_filter(nc, X, extremes, basis, freq, w_el, C, M)
                with nc.cleanup_on_exit():
                    mix(nc, X, rho, top, C, M, (parity, first), b_el, w_le, b_le, ln_gamma1, ln_beta1)
            with nc.cleanup_on_exit():
                quantised_product(nc, "second", X, rho, top, None, w1, gcol1, bcol1, None, out)


def kernel(**inputs):
    import concourse.bacc as bacc
    from concourse.bass_utils import run_bass_kernel_spmd

    def laid(a):
        return np.ascontiguousarray(a)

    def columns(v):
        return laid(np.asarray(v).reshape(-1, P).T)

    x = np.asarray(inputs["L0_attn_x"]).reshape(TOKENS, DM)
    point, wave = np.arange(DM), np.arange(DM // 2 + 1)
    angle = 2 * np.pi * ((wave[:, None] * point[None, :]) % DM) / DM
    cosines, sines = np.cos(angle) * np.sqrt(2 / DM), np.sin(angle[1:-1]) * np.sqrt(2 / DM)
    cosines[[0, -1]] /= np.sqrt(2)
    basis = np.concatenate([cosines, sines]).astype(np.float32)
    freq = np.concatenate([wave, wave[1:-1]]).astype(np.float32) / np.float32(DM) + np.float32(1e-8)
    rows = ("111011100011", "110111000110", "101110001101", "011100011011", "000011111111", "111100000000",
            "000011110000", "110011001100", "101010101010", "010101010101", "100110011001", "011001100110")
    parity = np.zeros((LATENT, LATENT), np.float32)
    parity[:CHECKS, :CHECKS] = [[int(b) for b in row] for row in rows]
    parity[CHECKS:, :CHECKS] = np.eye(CHECKS)
    first = np.zeros((LATENT, LATENT), np.float32)
    first[:CHECKS, :] = 1.0

    given = {
        "x": x, "x_t": laid(x.T),
        **{f"w{n}_t": laid(np.asarray(inputs[f"L0_attn_W{n}"]).T) for n in ("v", "g", "k", "q", "og", "o", "d")},
        "bd": inputs["L0_attn_bd"], "norm_w": columns(inputs["L0_attn_norm_w"]),
        "ln_gamma0": inputs["L0_ffn_ln_gamma"], "ln_beta0": inputs["L0_ffn_ln_beta"],
        "gcol0": columns(inputs["L0_ffn_ln_gamma"]), "bcol0": columns(inputs["L0_ffn_ln_beta"]), "w0": inputs["L0_ffn_weight"],
        "basis": basis, "freq": columns(freq), "w_el": inputs["L1_attn_W_el"], "b_el": inputs["L1_attn_b_el"],
        "parity": parity, "first": first, "w_le": inputs["L1_attn_W_le"], "b_le": inputs["L1_attn_b_le"],
        "ln_gamma1": inputs["L1_ffn_ln_gamma"], "ln_beta1": inputs["L1_ffn_ln_beta"],
        "gcol1": columns(inputs["L1_ffn_ln_gamma"]), "bcol1": columns(inputs["L1_ffn_ln_beta"]), "w1": inputs["L1_ffn_weight"],
    }
    given = {name: laid(np.asarray(a)) for name, a in given.items()}
    nc = bacc.Bacc("TRN2", target_bir_lowering=False, num_devices=1)
    args = {name: nc.dram_tensor(name, a.shape, mybir.dt.from_np(a.dtype), kind="ExternalInput").ap() for name, a in given.items()}
    out = nc.dram_tensor("result", (TOKENS, DM), FP32, kind="ExternalOutput").ap()
    program(nc, out=out, **args)
    result = run_bass_kernel_spmd(nc, [given], core_ids=[0])
    return result.results[0]["result"].reshape(BATCH, SEQ, DM)
```
